# Optimizing a Trainium2 kernel written in Bass

```python
import numpy as np
import jax
import jax.numpy as jnp

def _softmax(x, axis=-1):
    return jax.nn.softmax(x, axis=axis)

def _gelu(x):
    return jax.nn.gelu(x, approximate=True)

def _silu(x):
    return jax.nn.silu(x)

def _sigmoid(x):
    return jax.nn.sigmoid(x)

def _layernorm(x, axis=-1, eps=1e-05):
    m = jnp.mean(x, axis=axis, keepdims=True)
    v = jnp.var(x, axis=axis, keepdims=True)
    return (x - m) / jnp.sqrt(v + eps)

def _scatter_add(tgt, idx, src, axis=0):
    return tgt.at[idx].add(src)

def _segment_sum(src, seg, n):
    return jax.ops.segment_sum(src, seg, n)
kernel_name = 'mk_flamingo_gated_d2_seqx_r8_969ed3'

def setup_inputs(seed: int=0):
    np.random.seed(seed)
    _w = jnp.asarray

    def _rec_inputs():
        import jax
        import jax.numpy as jnp
        _rk = jax.random.key(seed)
        x = -0.0003929 + 0.9999 * jax.random.normal(jax.random.fold_in(_rk, 1), (4, 256, 256), jnp.float32)
        _lenS = 256 - jax.random.randint(jax.random.fold_in(_rk, 7), (4,), 0, max(1, 256 // 4) + 1, jnp.int32)
        _lenS2 = 512 - jax.random.randint(jax.random.fold_in(_rk, 8), (4,), 0, max(1, 512 // 4) + 1, jnp.int32)
        _ctx_2048P = jax.random.normal(jax.random.fold_in(_rk, 11), (4, 16, 256), jnp.float32)
        _ctx_2048c = jax.random.dirichlet(jax.random.fold_in(_rk, 511), 0.3 * jnp.ones((16,), jnp.float32), (4, 512))
        _ctx_2048t = jnp.einsum('bsk,bkd->bsd', _ctx_2048c, _ctx_2048P)
        _ctx_2048t = _ctx_2048t * jax.lax.rsqrt(jnp.mean(jnp.square(_ctx_2048t)) + 1e-12) * 0.953939
        ctx_2048 = -0.000514642 + 1.00011 * (_ctx_2048t + 0.3 * jax.random.normal(jax.random.fold_in(_rk, 611), (4, 512, 256), jnp.float32))
        _validS = jnp.arange(256)[None, :] < _lenS[:, None]
        _validS2 = jnp.arange(512)[None, :] < _lenS2[:, None]
        _causal = jnp.tril(jnp.ones((256, 256), dtype=bool))
        mask_BxSxS2_ff0 = jnp.where(jnp.ones((4, 256, 512), dtype=bool), 0.0, -1000000000.0).astype(jnp.float32)
        _g = jax.random.normal(jax.random.fold_in(_rk, 9001), (2, 2), jnp.float32)
        _g = jnp.sign(_g) * jnp.maximum(jnp.abs(_g), 1.0) + (_g == 0) * 1.0
        g_xattn = _g[0]
        g_ffn = _g[1]
        return (x, ctx_2048, mask_BxSxS2_ff0, g_xattn, g_ffn)
    x, ctx_2048, mask_BxSxS2_ff0, g_xattn, g_ffn = _rec_inputs()

    def _L0_xattn_setup():
        import jax, jax.numpy as jnp
        import numpy as np
        NUM_HEADS = 16
        EPS = 1e-08

        def _dyn_quant(x):
            s = jnp.maximum(jnp.max(jnp.abs(x), axis=-1, keepdims=True) / 127.0, EPS)
            q = jnp.clip(jnp.round(x / s), -127.0, 127.0)
            return (q, s)

        def _quant_weight(w):
            s = jnp.maximum(jnp.max(jnp.abs(w), axis=1, keepdims=True) / 127.0, EPS)
            q = jnp.clip(jnp.round(w / s), -127.0, 127.0)
            return (q, s)

        def _w8a8_linear(x, w, b):
            qx, sx = _dyn_quant(x)
            qw, sw = _quant_weight(w)
            y = jnp.einsum('bnc,oc->bno', qx, qw) * (sx * sw[:, 0])
            return y + b
        key = jax.random.key(seed)
        ks = jax.random.split(key, 9)
        B, N, L, C = (2, 512, 64, 256)
        sc = 0.02
        return {'x': jax.random.normal(ks[0], (B, N, C), jnp.float32), 'cond': jax.random.normal(ks[1], (B, L, C), jnp.float32), 'mask': jnp.zeros((B, N, L), jnp.float32), 'wq': jax.random.normal(ks[2], (C, C), jnp.float32) * sc, 'bq': jnp.zeros((C,), jnp.float32), 'wk': jax.random.normal(ks[3], (C, C), jnp.float32) * sc, 'bk': jnp.zeros((C,), jnp.float32), 'wv': jax.random.normal(ks[4], (C, C), jnp.float32) * sc, 'bv': jnp.zeros((C,), jnp.float32), 'wo': jax.random.normal(ks[5], (C, C), jnp.float32) * sc, 'bo': jnp.zeros((C,), jnp.float32)}
    _L0_xattn_all = _L0_xattn_setup()
    _L0_xattn_in = {k: v for k, v in _L0_xattn_all.items() if k in ('wq', 'bq', 'wk', 'bk', 'wv', 'bv', 'wo', 'bo')}
    del _L0_xattn_all

    def _L0_ffn_setup():
        import jax, jax.numpy as jnp
        import numpy as np
        TOP_K = 4
        key = jax.random.key(seed)
        ks = jax.random.split(key, 8)
        B, S, H = (1, 128, 256)
        E, I = (60, 176)
        I_SH = 704
        s = 0.02
        return {'hidden_states': jax.random.normal(ks[0], (B, S, H), jnp.float32), 'gate_w': jax.random.normal(ks[1], (E, H), jnp.float32) * s, 'shared_gate_w': jax.random.normal(ks[2], (1, H), jnp.float32) * s, 'w13': jax.random.normal(ks[3], (E, 2 * I, H), jnp.float32) * s, 'w2': jax.random.normal(ks[4], (E, H, I), jnp.float32) * s, 'se_gate_up_w': jax.random.normal(ks[5], (2 * I_SH, H), jnp.float32) * s, 'se_down_w': jax.random.normal(ks[6], (H, I_SH), jnp.float32) * s}
    _L0_ffn_all = _L0_ffn_setup()
    _L0_ffn_in = {k: v for k, v in _L0_ffn_all.items() if k in ('gate_w', 'shared_gate_w', 'w13', 'w2', 'se_gate_up_w', 'se_down_w')}
    del _L0_ffn_all

    def _L1_xattn_setup():
        import jax, jax.numpy as jnp
        import numpy as np
        from jax import lax
        LN_EPS = 1e-05
        key = jax.random.key(seed)
        ks = jax.random.split(key, 8)
        B, S, T, D = (4, 128, 256, 256)
        scale = 0.02
        return {'Z': jax.random.normal(ks[0], (B, S, D), dtype=jnp.float32), 'kv': jax.random.normal(ks[1], (B, T, D), dtype=jnp.float32), 'decay': jnp.float32(0.9), 'W_in': jax.random.normal(ks[2], (D, D), dtype=jnp.float32) * scale, 'b_in': jnp.zeros((D,), dtype=jnp.float32), 'W_out': jax.random.normal(ks[3], (D, D), dtype=jnp.float32) * scale, 'b_out': jnp.zeros((D,), dtype=jnp.float32), 'gamma': jnp.ones((D,), dtype=jnp.float32), 'beta': jnp.zeros((D,), dtype=jnp.float32)}
    _L1_xattn_all = _L1_xattn_setup()
    _L1_xattn_in = {k: v for k, v in _L1_xattn_all.items() if k in ('decay', 'W_in', 'b_in', 'W_out', 'b_out', 'gamma', 'beta')}
    del _L1_xattn_all

    def _L1_ffn_setup():
        import jax, jax.numpy as jnp
        import numpy as np
        E = 8
        K = 2
        DIM = 256
        INTER = 176
        N_SHARED = 2
        STD = 0.02
        key = jax.random.key(seed)
        ks = jax.random.split(key, 9)
        B, S = (2, 256)
        return {'x': jax.random.normal(ks[0], (B, S, DIM), dtype=jnp.float32), 'gate_w': jax.random.normal(ks[1], (E, DIM), dtype=jnp.float32) * STD, 'router_bias': jnp.zeros((E,), dtype=jnp.float32), 'W1': jax.random.normal(ks[2], (E, DIM, INTER), dtype=jnp.float32) * STD, 'W3': jax.random.normal(ks[3], (E, DIM, INTER), dtype=jnp.float32) * STD, 'W2': jax.random.normal(ks[4], (E, INTER, DIM), dtype=jnp.float32) * STD, 'sw1': jax.random.normal(ks[5], (N_SHARED * INTER, DIM), dtype=jnp.float32) * STD, 'sw3': jax.random.normal(ks[6], (N_SHARED * INTER, DIM), dtype=jnp.float32) * STD, 'sw2': jax.random.normal(ks[7], (DIM, N_SHARED * INTER), dtype=jnp.float32) * STD}
    _L1_ffn_all = _L1_ffn_setup()
    _L1_ffn_in = {k: v for k, v in _L1_ffn_all.items() if k in ('gate_w', 'router_bias', 'W1', 'W3', 'W2', 'sw1', 'sw3', 'sw2')}
    del _L1_ffn_all
    return {'x': x, 'ctx_2048': ctx_2048, 'mask_BxSxS2_ff0': mask_BxSxS2_ff0, 'g_xattn': g_xattn, 'g_ffn': g_ffn, 'L0_xattn_wq': _L0_xattn_in['wq'], 'L0_xattn_bq': _L0_xattn_in['bq'], 'L0_xattn_wk': _L0_xattn_in['wk'], 'L0_xattn_bk': _L0_xattn_in['bk'], 'L0_xattn_wv': _L0_xattn_in['wv'], 'L0_xattn_bv': _L0_xattn_in['bv'], 'L0_xattn_wo': _L0_xattn_in['wo'], 'L0_xattn_bo': _L0_xattn_in['bo'], 'L0_ffn_gate_w': _L0_ffn_in['gate_w'], 'L0_ffn_shared_gate_w': _L0_ffn_in['shared_gate_w'], 'L0_ffn_w13': _L0_ffn_in['w13'], 'L0_ffn_w2': _L0_ffn_in['w2'], 'L0_ffn_se_gate_up_w': _L0_ffn_in['se_gate_up_w'], 'L0_ffn_se_down_w': _L0_ffn_in['se_down_w'], 'L1_xattn_decay': _L1_xattn_in['decay'], 'L1_xattn_W_in': _L1_xattn_in['W_in'], 'L1_xattn_b_in': _L1_xattn_in['b_in'], 'L1_xattn_W_out': _L1_xattn_in['W_out'], 'L1_xattn_b_out': _L1_xattn_in['b_out'], 'L1_xattn_gamma': _L1_xattn_in['gamma'], 'L1_xattn_beta': _L1_xattn_in['beta'], 'L1_ffn_gate_w': _L1_ffn_in['gate_w'], 'L1_ffn_router_bias': _L1_ffn_in['router_bias'], 'L1_ffn_W1': _L1_ffn_in['W1'], 'L1_ffn_W3': _L1_ffn_in['W3'], 'L1_ffn_W2': _L1_ffn_in['W2'], 'L1_ffn_sw1': _L1_ffn_in['sw1'], 'L1_ffn_sw3': _L1_ffn_in['sw3'], 'L1_ffn_sw2': _L1_ffn_in['sw2']}

def reference(x, ctx_2048, mask_BxSxS2_ff0, g_xattn, g_ffn, L0_xattn_wq, L0_xattn_bq, L0_xattn_wk, L0_xattn_bk, L0_xattn_wv, L0_xattn_bv, L0_xattn_wo, L0_xattn_bo, L0_ffn_gate_w, L0_ffn_shared_gate_w, L0_ffn_w13, L0_ffn_w2, L0_ffn_se_gate_up_w, L0_ffn_se_down_w, L1_xattn_decay, L1_xattn_W_in, L1_xattn_b_in, L1_xattn_W_out, L1_xattn_b_out, L1_xattn_gamma, L1_xattn_beta, L1_ffn_gate_w, L1_ffn_router_bias, L1_ffn_W1, L1_ffn_W3, L1_ffn_W2, L1_ffn_sw1, L1_ffn_sw3, L1_ffn_sw2):
    import jax
    import jax.numpy as jnp

    def _L0_xattn_ref(x, cond, mask, wq, bq, wk, bk, wv, bv, wo, bo):
        import jax, jax.numpy as jnp
        import numpy as np
        NUM_HEADS = 16
        EPS = 1e-08

        def _dyn_quant(x):
            s = jnp.maximum(jnp.max(jnp.abs(x), axis=-1, keepdims=True) / 127.0, EPS)
            q = jnp.clip(jnp.round(x / s), -127.0, 127.0)
            return (q, s)

        def _quant_weight(w):
            s = jnp.maximum(jnp.max(jnp.abs(w), axis=1, keepdims=True) / 127.0, EPS)
            q = jnp.clip(jnp.round(w / s), -127.0, 127.0)
            return (q, s)

        def _w8a8_linear(x, w, b):
            qx, sx = _dyn_quant(x)
            qw, sw = _quant_weight(w)
            y = jnp.einsum('bnc,oc->bno', qx, qw) * (sx * sw[:, 0])
            return y + b
        B, N, C = x.shape
        L = cond.shape[1]
        H = NUM_HEADS
        D = C // H
        inv_sqrt_d = np.float32(1.0 / np.sqrt(D))
        q = _w8a8_linear(x, wq, bq).reshape(B, N, H, D).transpose(0, 2, 1, 3)
        k = (cond @ wk.T + bk).reshape(B, L, H, D).transpose(0, 2, 1, 3)
        v = (cond @ wv.T + bv).reshape(B, L, H, D).transpose(0, 2, 1, 3)
        scores = jnp.einsum('bhnd,bhld->bhnl', q, k) * inv_sqrt_d + mask[:, None]
        attn = jax.nn.softmax(scores, axis=-1)
        o = jnp.einsum('bhnl,bhld->bhnd', attn, v)
        o = o.transpose(0, 2, 1, 3).reshape(B, N, C)
        return _w8a8_linear(o, wo, bo)

    def _L0_ffn_ref(hidden_states, gate_w, shared_gate_w, w13, w2, se_gate_up_w, se_down_w):
        import jax, jax.numpy as jnp
        import numpy as np
        TOP_K = 4
        orig_shape = hidden_states.shape
        E, H = gate_w.shape
        I = w2.shape[2]
        x = hidden_states.reshape(-1, H)
        M = x.shape[0]
        gu = x @ se_gate_up_w.T
        I_sh = se_down_w.shape[1]
        shared = jax.nn.silu(gu[:, :I_sh]) * gu[:, I_sh:] @ se_down_w.T
        shared = shared * jax.nn.sigmoid(x @ shared_gate_w.T)
        logits = x @ gate_w.T
        probs = jax.nn.softmax(logits.astype(jnp.float32), axis=-1)
        weights, sel = jax.lax.top_k(probs, TOP_K)
        cw = jnp.zeros((M, E), jnp.float32).at[jnp.arange(M)[:, None], sel].add(weights)

        def step(acc, ews):
            w13_e, w2_e, cw_e = ews
            gu_e = x @ w13_e.T
            h = jax.nn.silu(gu_e[:, :I]) * gu_e[:, I:]
            return (acc + cw_e[:, None] * (h @ w2_e.T), None)
        sparse, _ = jax.lax.scan(step, jnp.zeros((M, H), jnp.float32), (w13, w2, cw.T))
        return (shared + sparse).reshape(orig_shape)

    def _L1_xattn_ref(Z, kv, decay, W_in, b_in, W_out, b_out, gamma, beta):
        import jax, jax.numpy as jnp
        import numpy as np
        from jax import lax
        LN_EPS = 1e-05
        B, T, D = kv.shape
        K = jax.nn.sigmoid(decay)
        x = jnp.einsum('btd,ed->bte', kv, W_in) + b_in

        def scan_fn(s, xt):
            s = K * s + xt
            return (s, s)
        s0 = jnp.zeros((B, D), dtype=kv.dtype)
        _, states = lax.scan(scan_fn, s0, jnp.swapaxes(x, 0, 1))
        states = jnp.swapaxes(states, 0, 1)
        proj = jnp.einsum('btd,ed->bte', states, W_out) + b_out
        summary = jnp.mean(proj, axis=1, keepdims=True)
        y = Z + summary
        mu = jnp.mean(y, axis=-1, keepdims=True)
        var = jnp.mean((y - mu) ** 2, axis=-1, keepdims=True)
        return (y - mu) / jnp.sqrt(var + LN_EPS) * gamma + beta

    def _L1_ffn_ref(x, gate_w, router_bias, W1, W3, W2, sw1, sw3, sw2):
        import jax, jax.numpy as jnp
        import numpy as np
        E = 8
        K = 2
        DIM = 256
        INTER = 176
        N_SHARED = 2
        STD = 0.02
        B, S, D = x.shape
        X = x.reshape(-1, D)
        T = X.shape[0]
        logits = jnp.einsum('td,ed->te', X, gate_w)
        scores = jax.nn.sigmoid(logits)
        sel = scores + router_bias[None, :]
        _, idx = jax.lax.top_k(sel, K)
        w = jnp.take_along_axis(scores, idx, axis=1)
        w = w / jnp.clip(jnp.sum(w, axis=-1, keepdims=True), 1e-12)
        gate_full = jnp.zeros((T, E), dtype=w.dtype).at[jnp.arange(T)[:, None], idx].set(w)
        h1 = jnp.einsum('td,edh->eth', X, W1)
        h3 = jnp.einsum('td,edh->eth', X, W3)
        y = jnp.einsum('eth,ehd->etd', jax.nn.silu(h1) * h3, W2)
        out = jnp.einsum('etd,te->td', y, gate_full)
        shared = jnp.einsum('th,dh->td', jax.nn.silu(jnp.einsum('td,hd->th', X, sw1)) * jnp.einsum('td,hd->th', X, sw3), sw2)
        out = out + shared
        return out.reshape(B, S, D)
    x = x + jnp.tanh(g_xattn[0]) * _L0_xattn_ref(_layernorm(x, axis=-1), ctx_2048, mask_BxSxS2_ff0, L0_xattn_wq, L0_xattn_bq, L0_xattn_wk, L0_xattn_bk, L0_xattn_wv, L0_xattn_bv, L0_xattn_wo, L0_xattn_bo)
    x = x + jnp.tanh(g_ffn[0]) * _L0_ffn_ref(_layernorm(x, axis=-1), L0_ffn_gate_w, L0_ffn_shared_gate_w, L0_ffn_w13, L0_ffn_w2, L0_ffn_se_gate_up_w, L0_ffn_se_down_w)
    x = x + jnp.tanh(g_xattn[1]) * _L1_xattn_ref(_layernorm(x, axis=-1), ctx_2048, L1_xattn_decay, L1_xattn_W_in, L1_xattn_b_in, L1_xattn_W_out, L1_xattn_b_out, L1_xattn_gamma, L1_xattn_beta)
    x = x + jnp.tanh(g_ffn[1]) * _L1_ffn_ref(_layernorm(x, axis=-1), L1_ffn_gate_w, L1_ffn_router_bias, L1_ffn_W1, L1_ffn_W3, L1_ffn_W2, L1_ffn_sw1, L1_ffn_sw3, L1_ffn_sw2)
    return x

_drawn_inputs = setup_inputs


def setup_inputs(seed=0):
    import zlib

    import numpy as np

    out = dict(_drawn_inputs(seed))
    spreads = {'g_ffn': (-1.0, 0.6),
     'L0_xattn_bq': (0.0, 0.8),
     'L0_xattn_bk': (0.0, 2.0),
     'L0_xattn_bv': (0.0, 0.438),
     'L0_xattn_bo': (0.0, 0.1),
     'L1_xattn_b_in': (0.0, 0.594),
     'L1_xattn_b_out': (0.0, 0.54),
     'L1_xattn_gamma': (1.0, 0.588),
     'L1_xattn_beta': (0.0, 0.583),
     'L1_ffn_router_bias': (0.0, 2.0)}
    factors = {'L0_xattn_wq': 8.0,
     'L0_xattn_wk': 8.0,
     'L0_ffn_gate_w': 8.0,
     'L0_ffn_shared_gate_w': 8.0,
     'L0_ffn_w13': 8.0,
     'L0_ffn_w2': 8.0,
     'L0_ffn_se_gate_up_w': 7.344,
     'L0_ffn_se_down_w': 7.493,
     'L1_ffn_gate_w': 8.0,
     'L1_ffn_W1': 8.0,
     'L1_ffn_W3': 8.0,
     'L1_ffn_W2': 8.0,
     'L1_ffn_sw1': 8.0,
     'L1_ffn_sw3': 8.0,
     'L1_ffn_sw2': 8.0}
    for name, (base, spread) in spreads.items():
        noise = np.random.default_rng([zlib.crc32(name.encode()), seed]).standard_normal(out[name].shape)
        drawn = base * np.exp(spread * noise) if base else spread * noise
        out[name] = jnp.asarray(drawn.astype(out[name].dtype))
    for name, factor in factors.items():
        out[name] = (out[name] * factor).astype(out[name].dtype)
    return out
```

```python
from contextlib import ExitStack

import concourse.bass as bass
from concourse import mybir

P = 128
F32 = mybir.dt.float32
BF16 = mybir.dt.bfloat16
I32 = mybir.dt.int32
U32 = mybir.dt.uint32
ALU = mybir.AluOpType
ACT = mybir.ActivationFunctionType
AX = mybir.AxisListType

B, S, D = 4, 256, 256
L = 512
H, DH = 16, 16
TOK = B * S
NT = TOK // P
CC = D // P
LT = L // P
QT = S // P
LN_EPS = 1e-5
Q_EPS = 1e-8
MAGIC = 12582912.0
BIG = 3.0e38
I_EXP = 176
IC = I_EXP // 2


NB = 6
PAIRS = NB // 2


class Layer:

    def __init__(self, n, experts, top, shared, own_tiles):
        self.n, self.E, self.K, self.shared = n, experts, top, shared
        self.own = own_tiles
        self.main = experts if own_tiles else -(-((TOK * top - experts) // P + experts) // NB) * NB
        self.extra = (TOK * top - experts) // P if own_tiles else 0
        self.tiles = -(-(self.main + self.extra) // B) * B
        self.chunks = [(c, min(P, shared - c)) for c in range(0, shared, P)]
        self.most = TOK // P


L0 = Layer(0, 60, 4, 704, 1)
L1 = Layer(1, 8, 2, 352, 0)
LAYERS = (L0, L1)
ROWS = ("bq", "bv", "bo", "b_out", "gamma", "beta")
NSC = 2 + 2 + 1 + L1.E


class Steps:

    def __init__(self, engine, sem, base=0):
        self.engine, self.sem, self.base, self.n = engine, sem, base, 0

    def add(self, instruction, by=1):
        instruction.then_inc(self.sem, by)
        self.n += by

    def wait(self):
        self.engine.wait_ge(self.sem, self.base + self.n)

    def done(self, instruction):
        self.add(instruction)
        self.wait()


def build(nc, T, out, dbg=None):
    with ExitStack() as ctx:
        def sb(name, shape, dt=F32):
            return ctx.enter_context(nc.sbuf_tensor(name, shape, dt))

        def sem(name):
            return ctx.enter_context(nc.semaphore(name))

        bank = [ctx.enter_context(nc.psum_tensor(f"bank{i}", [P, 512], F32)) for i in range(8)]

        xg_dram = [nc.dram_tensor(f"sorted_x{y.n}", [y.tiles * P, D], F32).ap() for y in LAYERS]
        y_dram = [nc.dram_tensor(f"expert_y{y.n}", [y.tiles * P, D], F32).ap() for y in LAYERS]

        stage = sb("stage", [P, 27424])
        at = [0]

        def part(shape):
            n = 1
            for m in shape:
                n *= m
            names = "abcd"[:len(shape)]
            v = stage[:, at[0]:at[0] + n].rearrange(f"p ({' '.join(names)}) -> p {' '.join(names)}", **dict(zip(names, shape)))
            at[0] += n
            assert at[0] <= stage.shape[1]
            return v

        x_sb = sb("x_sb", [P, NT, D])
        xn = sb("xn", [P, NT, D])
        tmp = sb("tmp", [P, NT, D])
        codes = sb("codes", [P, NT, D], BF16)
        codesT = sb("codesT", [P, CC, TOK], BF16)
        o_all = part([NT, D])
        st = sb("st", [P, NT, 6])
        mv = sb("mv", [P, NT, 2])
        rstd = sb("rstd", [P, NT])
        vare = sb("vare", [P, NT])
        mhalf = sb("mhalf", [P, NT])
        sx = sb("sx", [P, NT])
        sx4 = sb("sx4", [P, NT])
        rsx = sb("rsx", [P, NT])
        rows = sb("rows", [P, len(ROWS), D])
        scal = sb("scal", [P, NSC])
        tg = sb("tg", [P, 4])
        colb = sb("colb", [P, 2, CC])
        ident = sb("ident", [P, P])
        identb = sb("identb", [P, P], BF16)
        ones = sb("ones", [P, P])
        onesb = sb("onesb", [P, P], BF16)
        before = sb("before", [P, P], BF16)
        zeros = sb("zeros", [P, D])
        w_q = part([2, CC, D])
        w_codes = sb("w_codes", [P, 2, CC, D], BF16)
        w_codesT = sb("w_codesT", [P, 2, CC, D], BF16)
        sw = sb("sw", [P, 4])
        rsw = sb("rsw", [P, 4])
        diag = part([4, P])
        sw_rows = sb("sw_rows", [P, 2, D])
        w_kv = part([4, CC, D])
        ctxT = part([CC, L])
        mask = part([QT, L])
        q_split = part([QT, 2, D])
        q_tmp = sb("q_tmp", [P, QT, D])
        qT = part([2, CC, S])
        kT = part([CC, L])
        v_sb = part([LT, H, 32])
        z_sb = part([2, 4, L])
        pT = part([2, 4, LT, P])
        zmin = sb("zmin", [P, 2, 4])
        psum_row = sb("psum_row", [P, QT, 4, 4])
        rsum = sb("rsum", [P, QT, 4, 4])
        oT = sb("oT", [P, 4, P])
        krow = sb("krow", [P, 1])
        coef = part([L])
        csum = sb("csum", [P, 1])
        ccol = sb("ccol", [P, LT])
        ctx_nat = part([B, LT, D])
        zT = sb("zT", [P, CC, B])
        mT = sb("mT", [P, CC, B])
        bin_s = sb("bin_s", [P, CC])
        mTb = part([CC, B, P])
        summary = sb("summary", [P, B, D])
        at[0] = 0
        xnT = sb("xnT", [P, CC, TOK])
        gate_w = [sb(f"gate_w{y.n}", [P, CC, y.E + 1 - y.n]) for y in LAYERS]
        NSH = len(L0.chunks)
        sh_in = sb("sh_in", [P, CC, 2 * L0.shared])
        sh_out = sb("sh_out", [P, NSH, D])
        sh_act = part([2, 512])
        sh_h = part([NSH, 512])
        sh_y = part([NT, D])
        EM, KM = L0.E, L0.K
        logits = part([NT, 64])
        probs = sb("probs", [P, NT, EM])
        picks = part([NT, EM])
        rmax = sb("rmax", [P, NT])
        rsm = sb("rsm", [P, NT])
        sh_gate = sb("sh_gate", [P, NT])
        top8 = sb("top8", [P, NT, 8])
        idx8 = sb("idx8", [P, NT, 8], U32)
        idxf = sb("idxf", [P, NT, 8])
        hot = part([NT, KM, EM])
        hot2 = part([NT, KM, EM])
        member = sb("member", [P, NT, EM], BF16)
        earlier = sb("earlier", [P, NT + 1, EM], BF16)
        iota_e = sb("iota_e", [P, EM])
        iota_v = sb("iota_v", [P, 32])
        cnt = sb("cnt", [P, EM])
        ntile = sb("ntile", [P, EM])
        incl = sb("incl", [P, EM])
        base = sb("base", [P, EM])
        over = sb("over", [P, EM])
        pos = part([NT, EM])
        posb = part([NT, EM])
        slotf = sb("slotf", [P, NT, KM])
        slot = sb("slot", [P, NT, KM], U32)
        wts = sb("wts", [P, NT, KM])
        owner_c = hot2.rearrange("p t k e -> p (t k) e")[0:1]
        owner_f = sb("owner_f", [1, 32])
        owner = sb("owner", [1, 32], I32)
        nextra = sb("nextra", [1, 2], I32)
        xg = part([NB, D])
        xgT = part([NB, CC, P])
        w13 = part([NB, CC, 2 * I_EXP])
        w2 = part([NB, 2, D])[0:IC]
        e_act = sb("e_act", [P, 2, I_EXP])
        e_h = sb("e_h", [P, 2, I_EXP])
        e_hT = sb("e_hT", [IC, 2, 2, P])
        e_y = part([4, D])
        NG = 4
        yk = part([NG, D])
        acc = part([NT, D])

        FULL = (4, 6)
        ld_x, ld_small, ld_wqo, ld_wkv, ld_ctx, ld_nat = map(sem, ("ld_x", "ld_small", "ld_wqo", "ld_wkv", "ld_ctx", "ld_nat"))
        ld_mask = [sem("ld_mask0"), sem("ld_mask1")]
        zero_tile, zeroed = sem("zero_tile"), [sem("zeroed0"), sem("zeroed1")]
        pool_step, dve_step, act_step = sem("pool_step"), sem("dve_step"), sem("act_step")
        consts = sem("consts")
        var_ready, rstd_ready = sem("var_ready"), sem("rstd_ready")
        coded, code_t, code_ev = sem("coded"), sem("code_t"), sem("code_ev")
        diag_ready, sw_full, setup_done = sem("diag_ready"), sem("sw_full"), sem("setup_done")
        seq_pe, seq_dve = sem("seq_pe"), sem("seq_dve")
        gates_ready = sem("gates_ready")
        dve_loop = sem("dve_loop")
        work_full = [sem("work_full0"), sem("work_full1")]
        work_free = [sem("work_free0"), sem("work_free1")]
        score_full, scored, expd = sem("score_full"), sem("scored"), sem("expd")
        t_full, t_free = sem("t_full"), [sem("t_free0"), sem("t_free1")]
        av_done, score_seen = sem("av_done"), sem("score_seen")
        oproj_full, oproj_free = sem("oproj_full"), sem("oproj_free")
        fs = []
        for y in LAYERS:
            fs.append({k: sem(f"{k}{y.n}") for k in (
                "ld_sh", "ld_gate", "x_ready", "xT_full", "xT_ev", "log_full", "log_ev", "r_act", "mem_ready", "pos_full",
                "slots_ready", "plan_ready", "scattered", "up_full", "up_act", "up_free", "sh_full", "sh_free",
                "xT2_full", "xT2_ev", "e_up_full", "e_silu", "e_mul", "hT_full", "hT_ev", "y_full", "y_ev",
                "ox_ld", "o_tfull", "o_tev", "o_up", "o_silu", "o_mul", "o_hfull", "o_hev", "o_y", "o_yev", "o_st", "o_done", "extra_done",
                "gathered", "combined") if y.extra or k[0:2] not in ("o_", "ox")})
            for i in range(PAIRS):
                for k in ("ld_x", "ld_w13_", "ld_w2_"):
                    fs[-1][f"{k}{i}"] = sem(f"{k}{i}_{y.n}")
            for i in range(2):
                fs[-1][f"y_st{i}"] = sem(f"y_st{i}_{y.n}")
            for i in range(NG):
                fs[-1][f"gat{i}"] = sem(f"gat{i}_{y.n}")
        stored = sem("stored")
        dbg_sem = sem("dbg_sem")

        block = ctx.enter_context(nc.Block())
        R = {n: rows[:, i, :] for i, n in enumerate(ROWS)}

        def bc(ap, axis, n):
            v = ap.unsqueeze(axis)
            shape = list(v.shape)
            shape[axis] = n
            return v.to_broadcast(shape)

        def head(g, j):
            cc, par = divmod(g, 2)
            return cc, par, cc * 8 + 2 * j + par

        @block.sync
        def _(sp):
            sp.dma_start(x_sb[:], T["x"].rearrange("(t p) d -> p t d", p=P)).then_inc(ld_x, 16)
            sp.dma_start(w_q[:], T["w_qo"].rearrange("w (c p) d -> p w c d", p=P)).then_inc(ld_wqo, 16)
            sp.dma_start(rows[:], T["rows"].rearrange("(o r) d -> o r d", o=1).to_broadcast([P, len(ROWS), D])).then_inc(ld_small, 16)
            sp.dma_start(scal[:], T["scalars"].rearrange("(o r) -> o r", o=1).to_broadcast([P, NSC])).then_inc(ld_small, 16)
            sp.dma_start(colb[:], T["colb"]).then_inc(ld_small, 16)
            sp.dma_start(w_kv[:], T["w_kv"].rearrange("w (c p) d -> p w c d", p=P)).then_inc(ld_wkv, 16)
            sp.dma_start(ctx_nat[:], T["ctx"].rearrange("b (t p) d -> p b t d", p=P)).then_inc(ld_nat, 16)
            for y in LAYERS:
                f = fs[y.n]
                sp.dma_start(gate_w[y.n][:], T[f"gate{y.n}"]).then_inc(f["ld_gate"], 16)

            def shared_weights(y):
                f = fs[y.n]
                sp.dma_start(sh_in[:, :, 0:2 * y.shared], T[f"sh_in{y.n}"]).then_inc(f["ld_sh"], 16)
                for c, (c0, n) in enumerate(y.chunks):
                    sp.dma_start(sh_out[0:n, c, :], T[f"sh_out{y.n}"][c0:c0 + n, :]).then_inc(f["ld_sh"], 16)

            shared_weights(L0)
            sp.wait_ge(zero_tile, 1)

            def load_ctx(b):
                sp.dma_start(ctxT[:], T["ctxT"][bass.ds(b, 1)].rearrange("o p c l -> p (o c) l")).then_inc(ld_ctx, 16)

            def load_mask(b, nt):
                sp.dma_start(mask[:, nt, :], T["mask"][bass.ds(b * QT + nt, 1)].rearrange("o p l -> p (o l)")).then_inc(ld_mask[nt], 16)

            def zero_quarter(b):
                for y in LAYERS:
                    n = y.tiles // B
                    for d in (xg_dram[y.n], y_dram[y.n]):
                        sp.dma_start(d.rearrange("(p a) d -> p a d", p=P)[:, bass.ds(b * n, n), :],
                                     bc(zeros[:], 1, n)).then_inc(zeroed[y.n], 16)

            load_ctx(0)
            load_mask(0, 0)
            load_mask(0, 1)
            zero_quarter(0)
            with sp.Fori(0, B - 1) as b:
                sp.wait_ge(work_full[1], b * 6 + 4)
                load_ctx(b + 1)
                for nt in range(QT):
                    sp.wait_ge(scored, b * (QT * 16) + (nt + 1) * 16)
                    load_mask(b + 1, nt)
                    if nt == 0:
                        zero_quarter(b + 1)
            if dbg is not None and "attn" in dbg:
                sp.wait_ge(fs[0]["x_ready"], 1)
                sp.dma_start(dbg["attn"].rearrange("(t p) d -> p t d", p=P), x_sb[:]).then_inc(dbg_sem, 16)
                sp.wait_ge(dbg_sem, 16)

            def experts(y):
                f = fs[y.n]
                wi, wo = T[f"w13_{y.n}"], T[f"w2_{y.n}"]

                def owners(p):
                    return [sp.value_load(owner[0:1, bass.ds(p * 2 + h, 1)], min_val=0, max_val=y.E - 1) for h in range(2)]

                def load_w(dst, src, p, s, key, own):
                    if y.own:
                        sp.dma_start(dst[:, 2 * s:2 * s + 2].rearrange("p e c n -> p e (c n)"),
                                     src[bass.ds(p * 2, 2)].rearrange("e p c n -> p e (c n)")).then_inc(f[f"{key}{s}"], 32)
                    else:
                        for h in range(2):
                            sp.dma_start(dst[:, 2 * s + h], src[bass.ds(own[h], 1)].rearrange("o p c n -> p (o c) n"))\
                              .then_inc(f[f"{key}{s}"], 16)

                def load_x(p, s):
                    sp.dma_start(xg[:, 2 * s:2 * s + 2, :],
                                 xg_dram[y.n][bass.ds(p * 2 * P, 2 * P), :].rearrange("(h p) d -> p h d", p=P)).then_inc(f[f"ld_x{s}"], 16)

                pairs = y.main // 2
                if y.own:
                    sp.wait_ge(f["x_ready"], 1)
                else:
                    sp.wait_ge(f["plan_ready"], 1)
                for p in range(PAIRS):
                    own = None if y.own else owners(p)
                    load_w(w13, wi, p, p, "ld_w13_", own)
                    load_w(w2, wo, p, p, "ld_w2_", own)
                sp.wait_ge(f["scattered"], 16 * NT * y.K)
                for p in range(PAIRS):
                    load_x(p, p)
                sp.wait_ge(f["xT2_full"], 2)
                load_x(PAIRS, 0)

                def pair(p, s, whole, more_x):
                    own = None
                    if whole:
                        if not y.own:
                            own = owners(p + PAIRS)
                        sp.wait_ge(f["e_up_full"], p * 2 + 2)
                        load_w(w13, wi, p + PAIRS, s, "ld_w13_", own)
                    if more_x:
                        sp.wait_ge(f["xT2_full"], p * 2 + 4)
                        load_x(p + PAIRS + 1, (s + 1) % PAIRS)
                    if whole:
                        sp.wait_ge(f["y_full"], p * 2 + 2)
                        load_w(w2, wo, p + PAIRS, s, "ld_w2_", own)

                def store(p, q):
                    sp.wait_ge(f["y_ev"], p * 2 + 2)
                    sp.dma_start(y_dram[y.n][bass.ds(p * 2 * P, 2 * P), :].rearrange("(h p) d -> p h d", p=P),
                                 e_y[:, 2 * q:2 * q + 2, :]).then_inc(f[f"y_st{q}"], 16)

                turns = (pairs - PAIRS) // (2 * PAIRS)
                with sp.Fori(0, turns) as it:
                    for u in range(2 * PAIRS):
                        pair(it * (2 * PAIRS) + u, u % PAIRS, True, True)
                        store(it * (2 * PAIRS) + u, u % 2)
                for p in range(turns * 2 * PAIRS, pairs):
                    pair(p, p % PAIRS, p + PAIRS < pairs, p + PAIRS + 1 < pairs)
                    store(p, p % 2)
                if y.extra:
                    n = sp.value_load(nextra[0:1, 0:1], min_val=0, max_val=y.extra)
                    for q in range(2):
                        sp.wait_ge(f[f"y_st{q}"], 16 * (y.main // 4))
                    with sp.Fori(0, y.extra) as v:
                        with sp.If(n > v):
                            e = sp.value_load(owner[0:1, bass.ds(v, 1)], min_val=0, max_val=y.E - 1)
                            sp.dma_start(w13[:, 0], wi[bass.ds(e, 1)].rearrange("o p c n -> p (o c) n")).then_inc(f["ox_ld"], 16)
                            sp.dma_start(w2[:, 0], wo[bass.ds(e, 1)].rearrange("o p c n -> p (o c) n")).then_inc(f["ox_ld"], 16)
                            sp.dma_start(xg[:, 0, :], xg_dram[y.n][bass.ds((v + y.main) * P, P), :]).then_inc(f["ox_ld"], 16)
                            sp.wait_ge(f["o_yev"], v + 1)
                            sp.dma_start(y_dram[y.n][bass.ds((v + y.main) * P, P), :], e_y[:, 0, :]).then_inc(f["o_st"], 16)
                            sp.wait_ge(f["o_st"], v * 16 + 16)
                            sp.sem_inc(f["o_done"], 1)
                sp.sem_inc(f["extra_done"], 1)

            experts(L0)
            sp.wait_ge(fs[0]["sh_full"], NT)
            shared_weights(L1)
            if dbg is not None and "ffn0" in dbg:
                sp.wait_ge(fs[0]["combined"], 1)
                sp.dma_start(dbg["ffn0"].rearrange("(t p) d -> p t d", p=P), x_sb[:]).then_inc(dbg_sem, 16)
                sp.wait_ge(dbg_sem, 32)
            if dbg is not None and "seq" in dbg:
                sp.wait_ge(fs[1]["x_ready"], 1)
                sp.dma_start(dbg["seq"].rearrange("(t p) d -> p t d", p=P), x_sb[:]).then_inc(dbg_sem, 16)
                sp.wait_ge(dbg_sem, 48)
            experts(L1)
            sp.wait_ge(fs[1]["combined"], 1)
            sp.dma_start(out.rearrange("(t p) d -> p t d", p=P), x_sb[:]).then_inc(stored, 16)
            sp.wait_ge(stored, 16)

        @block.gpsimd
        def _(gp):
            step = Steps(gp, pool_step)
            step.done(gp.memset(zeros[:], 0.0))
            gp.sem_inc(zero_tile, 1)
            step.done(gp.memset(ident[:], 0.0))
            step.done(gp.affine_select(out=ident[:], in_=ident[:], compare_op=ALU.not_equal, fill=1.0, base=0,
                                       pattern=[[-1, P]], channel_multiplier=1))
            step.add(gp.tensor_copy(identb[:], ident[:]))
            step.done(gp.memset(ones[:], 1.0))
            step.add(gp.tensor_copy(onesb[:], ones[:]))
            step.add(gp.affine_select(out=before[:], in_=ones[:], compare_op=ALU.is_gt, fill=0.0, base=0,
                                      pattern=[[1, P]], channel_multiplier=-1))
            step.add(gp.iota(iota_e[:], pattern=[[1, EM]], base=0, channel_multiplier=0, allow_small_or_imprecise_dtypes=True))
            step.add(gp.iota(iota_v[:], pattern=[[1, 32]], base=0, channel_multiplier=0, allow_small_or_imprecise_dtypes=True))
            step.add(gp.memset(v_sb[:], 0.0))
            step.add(gp.memset(q_split[:], 0.0))
            step.done(gp.memset(mhalf[:], -0.5))
            gp.sem_inc(consts, 1)

            def power(n):
                gp.wait_ge(var_ready, n)
                gp.tensor_tensor(rstd[:], vare[:], mhalf[:], ALU.pow).then_inc(rstd_ready, 1)

            def dispatch(y):
                f = fs[y.n]
                gp.wait_ge(f["slots_ready"], 1)
                gp.wait_ge(zeroed[y.n], 2 * B * 16)
                for i in range(NT):
                    for k in range(y.K):
                        gp.indirect_dma_start(out=xg_dram[y.n][:, :], out_offset=bass.IndirectOffsetOnAxis(slot[:, i, k:k + 1], 0),
                                              in_=xn[:, i, :], in_offset=None).then_inc(f["scattered"], 16)

            def collect(y):
                f = fs[y.n]
                for q in range(2):
                    gp.wait_ge(f[f"y_st{q}"], 16 * (y.main // 4))
                gp.wait_ge(f["extra_done"], 1)
                for i in range(NT):
                    for k in range(y.K):
                        n = i * y.K + k
                        if n >= NG:
                            gp.wait_ge(f["gathered"], n - NG + 1)
                        gp.indirect_dma_start(out=yk[:, n % NG, :], out_offset=None, in_=y_dram[y.n][:, :],
                                              in_offset=bass.IndirectOffsetOnAxis(slot[:, i, k:k + 1], 0)).then_inc(f[f"gat{n % NG}"], 16)

            power(1)
            power(2)
            dispatch(L0)
            collect(L0)
            power(3)
            power(4)
            power(5)
            dispatch(L1)
            collect(L1)

        @block.vector
        def _(dve):
            step = Steps(dve, dve_step)
            V = nc.vector
            norms = [0]

            def norm(src, dst):
                for i in range(NT):
                    step.add(V.bn_stats(st[:, i, :], src[:, i, :]))
                step.wait()
                for i in range(NT):
                    step.add(V.bn_aggr(mv[:, i, :], st[:, i, :]))
                step.wait()
                V.tensor_scalar(vare[:], mv[:, :, 1], LN_EPS, None, ALU.add).then_inc(var_ready, 1)
                norms[0] += 1
                dve.wait_ge(rstd_ready, norms[0])
                for i in range(NT):
                    step.add(V.tensor_scalar(dst[:, i, :], src[:, i, :], mv[:, i, 0:1], rstd[:, i:i + 1], ALU.subtract, ALU.mult))
                step.wait()

            def quantise(src, dst, scales, inverse, n, scratch):
                step.done(V.tensor_reduce(scales, src, AX.X, ALU.max, apply_absolute_value=True))
                step.done(V.tensor_scalar(scales, scales, 1.0 / 127.0, Q_EPS, ALU.mult, ALU.max))
                step.done(V.reciprocal(inverse, scales))
                for i in range(n):
                    step.add(V.tensor_scalar(scratch[:, i, :], src[:, i, :], inverse[:, i:i + 1], MAGIC, ALU.mult, ALU.add))
                step.wait()
                step.done(V.tensor_scalar(scratch, scratch, MAGIC, 127.0, ALU.subtract, ALU.min))
                V.tensor_scalar(dst, scratch, -127.0, None, ALU.max).then_inc(coded, 1)

            dve.wait_ge(ld_x, 16)
            norm(x_sb, xn)
            quantise(xn[:], codes[:], sx[:], rsx[:], NT, tmp[:])
            step.done(V.tensor_scalar(sx4[:], sx[:], 0.25, None, ALU.mult))
            dve.wait_ge(ld_wqo, 16)
            dve.wait_ge(coded, 1)
            wq3 = w_q[:].rearrange("p w c d -> p (w c) d")
            quantise(wq3, w_codes[:].rearrange("p w c d -> p (w c) d"), sw[:], rsw[:], 4, tmp[:, 0:4, :])
            dve.wait_ge(consts, 1)
            for i in range(4):
                last = V.tensor_scalar(diag[:, i, :], ident[:], sw[:, i:i + 1], None, ALU.mult)
                step.add(last)
            step.wait()
            dve.sem_inc(diag_ready, 1)
            dve.wait_ge(ld_small, 48)
            step.done(V.tensor_scalar(R["bq"], R["bq"], 0.25, None, ALU.mult))
            for c in range(CC):
                dve.wait_ge(code_t, c + 1)
                V.tensor_copy(codesT[:, c, :], bank[c][:].bitcast(BF16)).then_inc(code_ev, 1)
            dve.wait_ge(code_t, 3)
            V.tensor_copy(w_codesT[:].rearrange("p w c d -> p (w c d)"), bank[2][:].bitcast(BF16)).then_inc(code_ev, 1)
            dve.wait_ge(sw_full, 1)
            V.tensor_copy(sw_rows[:].rearrange("p w d -> p (w d)"), bank[3][:]).then_inc(setup_done, 1)
            dve.wait_ge(gates_ready, 1)
            step.done(V.tensor_scalar(krow[:], krow[:], 1.0, None, ALU.add))
            step.done(V.reciprocal(krow[:], krow[:]))
            step.done(V.tensor_tensor_scan(coef[:, L - 1::-1], krow[:].to_broadcast([P, L]), ones[:, 0:1].to_broadcast([P, L]),
                                           0.0, ALU.mult, ALU.add))
            V.tensor_reduce(csum[:], coef[:], AX.X, ALU.add).then_inc(seq_dve, 1)
            dve.wait_ge(seq_pe, 1)
            V.tensor_copy(ccol[:], bank[4][:, 0:LT]).then_inc(seq_dve, 1)
            dve.wait_ge(seq_pe, 2)
            V.tensor_copy(zT[:].rearrange("p c b -> p (c b)"), bank[5][:, 0:CC * B]).then_inc(seq_dve, 1)
            step.done(V.tensor_scalar(bin_s[:], colb[:, 1, :], csum[:], None, ALU.mult))
            dve.wait_ge(seq_pe, 3)
            step.done(V.tensor_tensor(mT[:], bank[4][:, 0:CC * B].rearrange("p (c b) -> p c b", c=CC), bc(bin_s[:], 2, B), ALU.add))
            step.done(V.tensor_scalar(mTb[:].rearrange("p c b n -> p (c b) n"), bc(mT[:].rearrange("p c b -> p (c b)"), 2, P),
                                      1.0 / L, None, ALU.mult))
            dve.sem_inc(seq_dve, 1)
            dve.wait_ge(seq_pe, 4)
            for h in range(2):
                step.add(V.tensor_tensor(summary[:, 2 * h:2 * h + 2, :], bank[6 + h][:].rearrange("p (b d) -> p b d", b=2),
                                         bc(R["b_out"], 1, 2), ALU.add))
            step.wait()
            dve.sem_inc(setup_done, 1)

            SUBS = QT * 4
            NLOOP = 12
            with dve.Fori(0, B) as b:
                ls = Steps(dve, dve_loop, b * NLOOP)
                for nt in range(QT):
                    i = b * QT + nt
                    dve.wait_ge(work_full[nt], b * FULL[nt] + 1)
                    q3 = V.scalar_tensor_tensor(out=q_tmp[:, nt, :], in0=bank[6 + nt][:, 0:D], scalar=sx4[:, bass.ds(i, 1)],
                                                in1=sw_rows[:, 0, :], op0=ALU.mult, op1=ALU.mult)
                    ls.done(q3)
                    dve.sem_inc(work_free[nt], 1)
                    for par in range(2):
                        v = lambda ap: ap.rearrange("p (h two d) -> p h two d", two=2, d=DH)[:, :, par, :]
                        last = V.tensor_tensor(v(q_split[:, nt, par, :]), v(q_tmp[:, nt, :]), v(R["bq"]), ALU.add)
                        ls.add(last)

                def score(s):
                    nt, g = divmod(s, 4)
                    if g == 0:
                        dve.wait_ge(ld_mask[nt], b * 16 + 16)
                    for j in range(4):
                        dve.wait_ge(score_full, b * SUBS * 4 + s * 4 + j + 1)
                        dve.sem_inc(score_seen, 1)
                        V.tensor_tensor_reduce(out=z_sb[:, s % 2, j, :], in0=bank[j][:], in1=mask[:, nt, :], scale=-1.0,
                                               scalar=BIG, op0=ALU.add, op1=ALU.min,
                                               accum_out=zmin[:, s % 2, j:j + 1]).then_inc(scored, 1)
                        if j % 2 and s:
                            take(s - 1, j)
                    if s == 0:
                        values()

                def take(s, j):
                    dve.wait_ge(t_full, b * SUBS * 4 + s * 4 + j + 1)
                    V.tensor_copy(pT[:, s % 2, j].rearrange("p t n -> p (t n)"), bank[5][:]).then_inc(t_free[1], 1)

                def values():
                    for w in range(2):
                        dve.wait_ge(work_full[w], b * FULL[w] + 4)
                        V.tensor_tensor(v_sb[:, 2 * w:2 * w + 2, :, 0:DH],
                                        bank[6 + w][:].rearrange("p (t h d) -> p t h d", h=H, d=DH),
                                        bc(R["bv"].rearrange("p (h d) -> p h d", d=DH), 1, 2), ALU.add).then_inc(work_free[w], 1)

                def finish(nt):
                    dve.wait_ge(expd, b * SUBS * 4 + (nt + 1) * 16)
                    ls.done(V.reciprocal(rsum[:, nt], psum_row[:, nt]))
                    dve.wait_ge(work_full[1], b * 6 + 5 + nt)
                    for cc in range(CC):
                        src = bank[7][:].rearrange("p (g j d) -> p g j d", j=4, d=32)[:, 2 * cc:2 * cc + 2, :, 0:DH]
                        dst = o_all[:, bass.ds(b * QT + nt, 1), :].rearrange("p o (c j r d) -> p (o c) r j d", c=CC, j=4, r=2)[:, cc]
                        ls.add(V.tensor_tensor(dst, src, bc(rsum[:, nt, 2 * cc:2 * cc + 2, :], 3, DH), ALU.mult))
                    ls.wait()
                    dve.sem_inc(work_free[1], 1)

                for s in range(SUBS):
                    score(s)
                    if s == 6:
                        finish(0)
                take(SUBS - 1, 1)
                take(SUBS - 1, 3)
                finish(1)
                assert ls.n == NLOOP, ls.n

            quantise(o_all[:], codes[:], sx[:], rsx[:], NT, tmp[:])
            for c in range(CC):
                dve.wait_ge(code_t, 4 + c)
                V.tensor_copy(codesT[:, c, :], bank[c][:].bitcast(BF16)).then_inc(code_ev, 1)
            for i in range(NT):
                dve.wait_ge(oproj_full, i + 1)
                step.done(V.scalar_tensor_tensor(out=tmp[:, i, :], in0=bank[2 + i % 4][:, 0:D], scalar=sx[:, i:i + 1],
                                                 in1=sw_rows[:, 1, :], op0=ALU.mult, op1=ALU.mult))
                dve.sem_inc(oproj_free, 1)
            step.done(V.tensor_tensor(tmp[:], tmp[:], bc(R["bo"], 1, NT), ALU.add))
            step.done(V.scalar_tensor_tensor(out=x_sb[:], in0=tmp[:], scalar=tg[:, 0:1], in1=x_sb[:], op0=ALU.mult, op1=ALU.add))

            def route(y):
                f, E, K = fs[y.n], y.E, y.K
                lg = logits[:, :, 0:E]
                pr, pk = probs[:, :, 0:E], picks[:, :, 0:E]
                dve.wait_ge(f["log_full"], 1)
                ng = gate_w[y.n].shape[2]
                step.done(V.tensor_copy(logits[:, :, 0:ng], bank[6][:].rearrange("p (t e) -> p t e", t=NT)[:, :, 0:ng]))
                if y.n == 0:
                    step.done(V.tensor_reduce(rmax[:], lg, AX.X, ALU.max))
                    V.tensor_tensor(pr, lg, bc(rmax[:], 2, E), ALU.subtract).then_inc(f["log_ev"], 1)
                    dve.wait_ge(f["r_act"], 2)
                    step.done(V.tensor_reduce(rsm[:], pr, AX.X, ALU.add))
                    step.done(V.reciprocal(rsm[:], rsm[:]))
                    step.done(V.tensor_tensor(pr, pr, bc(rsm[:], 2, E), ALU.mult))
                    step.done(V.tensor_scalar(sh_gate[:], sh_gate[:], 1.0, None, ALU.add))
                    step.done(V.reciprocal(sh_gate[:], sh_gate[:]))
                    keys = probs
                else:
                    dve.sem_inc(f["log_ev"], 1)
                    dve.wait_ge(f["r_act"], 1)
                    step.done(V.tensor_scalar(pr, pr, 1.0, None, ALU.add))
                    step.done(V.reciprocal(pr, pr))
                    step.done(V.tensor_tensor(pk, pr, bc(scal[:, 5:5 + E], 1, NT), ALU.add))
                    keys = picks
                for i in range(NT):
                    step.add(V.max(top8[:, i, :], keys[:, i, 0:E]))
                step.wait()
                for i in range(NT):
                    step.add(V.max_index(idx8[:, i, :], top8[:, i, :], keys[:, i, 0:E]))
                step.wait()
                step.done(V.tensor_copy(idxf[:], idx8[:]))
                h1, h2 = hot[:, :, 0:K, 0:E], hot2[:, :, 0:K, 0:E]
                for k in range(K):
                    step.add(V.tensor_tensor(hot[:, :, k, 0:E], bc(iota_e[:, 0:E], 1, NT), bc(idxf[:, :, k], 2, E), ALU.is_equal))
                step.wait()
                mem = member[:, :, 0:E]
                step.done(V.tensor_tensor(mem, hot[:, :, 0, 0:E], hot[:, :, 1, 0:E], ALU.add))
                for k in range(2, K):
                    step.done(V.tensor_tensor(mem, mem, hot[:, :, k, 0:E], ALU.add))
                step.done(V.memset(earlier[:, 0, 0:E], 0.0))
                for i in range(NT):
                    step.done(V.tensor_tensor(earlier[:, i + 1, 0:E], earlier[:, i, 0:E], member[:, i, 0:E], ALU.add))
                dve.sem_inc(f["mem_ready"], 1)
                if y.n == 0:
                    step.done(V.tensor_copy(wts[:], top8[:, :, 0:K]))
                else:
                    for k in range(K):
                        step.add(V.tensor_tensor(hot2[:, :, k, 0:E], hot[:, :, k, 0:E], pr, ALU.mult))
                    step.wait()
                    for k in range(K):
                        step.add(V.tensor_reduce(wts[:, :, k], hot2[:, :, k, 0:E], AX.X, ALU.add))
                    step.wait()
                    step.done(V.tensor_tensor(rsm[:], wts[:, :, 0], wts[:, :, 1], ALU.add))
                    step.done(V.tensor_scalar(rsm[:], rsm[:], 1e-12, None, ALU.max))
                    step.done(V.reciprocal(rsm[:], rsm[:]))
                    step.done(V.tensor_tensor(wts[:, :, 0:K], wts[:, :, 0:K], bc(rsm[:], 2, K), ALU.mult))
                dve.wait_ge(f["pos_full"], 1)
                c, n, inc, bs, ov = cnt[:, 0:E], ntile[:, 0:E], incl[:, 0:E], base[:, 0:E], over[:, 0:E]
                step.add(V.tensor_copy(c, bank[6][:, 0:E]))
                ps, pb = pos[:, :, 0:E], posb[:, :, 0:E]
                step.done(V.tensor_copy(ps, bank[7][:].rearrange("p (t e) -> p t e", t=NT)[:, :, 0:E]))
                first = P if y.own else 0
                step.done(V.tensor_scalar(n, c, float(first), None, ALU.is_gt))
                for m in range(first + P, TOK, P):
                    step.done(V.scalar_tensor_tensor(out=n, in0=c, scalar=float(m), in1=n, op0=ALU.is_gt, op1=ALU.add))
                step.done(V.tensor_tensor_scan(inc, ones[:, 0:E], n, 0.0, ALU.mult, ALU.add))
                step.done(V.tensor_tensor(bs, inc, n, ALU.subtract))
                step.done(V.tensor_scalar(bs, bs, float(P), None, ALU.mult))
                if y.own:
                    step.done(V.scalar_tensor_tensor(out=ov, in0=iota_e[:, 0:E], scalar=-float(P), in1=bs, op0=ALU.mult, op1=ALU.add))
                    step.done(V.tensor_scalar(ov, ov, float(P * (y.main - 1)), None, ALU.add))
                    step.done(V.tensor_scalar(pb, ps, float(P), None, ALU.is_ge))
                    step.done(V.tensor_tensor(pb, pb, bc(ov, 1, NT), ALU.mult))
                    step.done(V.tensor_tensor(pb, pb, ps, ALU.add))
                    step.done(V.tensor_scalar(ov, iota_e[:, 0:E], float(P), None, ALU.mult))
                    step.done(V.tensor_tensor(pb, pb, bc(ov, 1, NT), ALU.add))
                else:
                    step.done(V.tensor_tensor(pb, ps, bc(bs, 1, NT), ALU.add))
                for k in range(K):
                    step.add(V.tensor_tensor(hot[:, :, k, 0:E], hot[:, :, k, 0:E], pb, ALU.mult))
                step.wait()
                for k in range(K):
                    step.add(V.tensor_reduce(slotf[:, :, k], hot[:, :, k, 0:E], AX.X, ALU.add))
                step.wait()
                V.tensor_copy(slot[:, :, 0:K], slotf[:, :, 0:K]).then_inc(f["slots_ready"], 1)
                NV = y.extra if y.own else y.main
                step.done(V.tensor_tensor(owner_c[0:1, 0:NV, 0:E], bc(incl[0:1, 0:E], 1, NV), bc(iota_v[0:1, 0:NV], 2, E), ALU.is_le))
                step.done(V.tensor_reduce(owner_f[0:1, 0:NV], owner_c[0:1, 0:NV, 0:E], AX.X, ALU.add))
                step.done(V.tensor_scalar(owner_f[0:1, 0:NV], owner_f[0:1, 0:NV], float(E - 1), None, ALU.min))
                step.done(V.tensor_copy(owner[0:1, 0:NV], owner_f[0:1, 0:NV]))
                step.done(V.tensor_copy(nextra[0:1, 0:1], incl[0:1, E - 1:E]))
                dve.sem_inc(f["plan_ready"], 1)

            def shared(y):
                f = fs[y.n]
                nch = len(y.chunks)
                for half in range(2):
                    if half:
                        dve.wait_ge(f["sh_full"], NT // 2)
                    for c, (c0, n) in enumerate(y.chunks):
                        m = half * nch + c
                        dve.wait_ge(f["up_act"], m + 1)
                        V.tensor_tensor(sh_h[0:n, c, :], sh_act[0:n, m % 2, :], bank[2 * (m % 2) + 1][0:n, :],
                                        ALU.mult).then_inc(f["up_free"], 1)
                    for i in range(NT // 2):
                        t = half * (NT // 2) + i
                        dve.wait_ge(f["sh_full"], t + 1)
                        if y.n == 0:
                            V.tensor_scalar(sh_y[:, t, :], bank[4 + t % 2][:, 0:D], sh_gate[:, t:t + 1], None,
                                            ALU.mult).then_inc(f["sh_free"], 1)
                        else:
                            V.tensor_copy(sh_y[:, t, :], bank[4 + t % 2][:, 0:D]).then_inc(f["sh_free"], 1)

            def experts(y):
                f = fs[y.n]

                def take_x(i, u, first):
                    dve.wait_ge(f["xT2_full"], i + 1)
                    if not first:
                        dve.wait_ge(f["e_up_full"], i - NB + 1)
                    V.tensor_copy(xgT[:, u].rearrange("p c n -> p (c n)"), bank[u % 2][:, 0:2 * P]).then_inc(f["xT2_ev"], 1)

                def gated(i, q, first):
                    dve.wait_ge(f["e_silu"], i + 1)
                    if not first:
                        dve.wait_ge(f["hT_full"], i - 1)
                    V.tensor_tensor(e_h[:, q, :], e_act[:, q, :], bank[2 + q][:, I_EXP:2 * I_EXP], ALU.mult).then_inc(f["e_mul"], 1)

                def take_h(i, q, first):
                    dve.wait_ge(f["hT_full"], i + 1)
                    if not first:
                        dve.wait_ge(f["y_full"], i - 1)
                    V.tensor_copy(e_hT[:, q].rearrange("p c n -> p (c n)"), bank[4 + q][0:IC, 0:2 * P]).then_inc(f["hT_ev"], 1)

                def one(t, u, more, turn, first):
                    if more:
                        gated(t + 1, (u + 1) % 2, first)
                    if turn:
                        take_x(t + 3, (u + 3) % NB, first and t + 3 < NB)
                    if more:
                        take_h(t + 1, (u + 1) % 2, first)

                for i in range(3):
                    take_x(i, i, True)
                gated(0, 0, True)
                take_h(0, 0, True)
                last = y.main - 1
                for t in range(NB):
                    one(t, t, True, True, t < 1) if t < 1 or t + 3 >= NB else (gated(t + 1, (t + 1) % 2, False),
                                                                               take_x(t + 3, t + 3, True), take_h(t + 1, (t + 1) % 2, False))
                with dve.Fori(1, y.main // NB - 1) as it:
                    for u in range(NB):
                        one(it * NB + u, u, True, True, False)
                for t in range(y.main - NB, y.main):
                    one(t, t % NB, t + 1 <= last, t + 3 <= last, False)
                if y.extra:
                    n = dve.value_load(nextra[0:1, 0:1], min_val=0, max_val=y.extra)
                    with dve.Fori(0, y.extra) as v:
                        with dve.If(n > v):
                            dve.wait_ge(f["o_silu"], v + 1)
                            V.tensor_tensor(e_h[:, 0, :], e_act[:, 0, :], bank[2][:, I_EXP:2 * I_EXP], ALU.mult).then_inc(f["o_mul"], 1)
                            dve.wait_ge(f["o_hfull"], v + 1)
                            V.tensor_copy(e_hT[:, 0].rearrange("p c n -> p (c n)"), bank[4][0:IC, 0:2 * P]).then_inc(f["o_hev"], 1)

            def combine(y, gate):
                f = fs[y.n]
                for i in range(NT):
                    for k in range(y.K):
                        n = i * y.K + k
                        dve.wait_ge(f[f"gat{n % NG}"], 16 * (n // NG + 1))
                        src = sh_y[:, i, :] if k == 0 else acc[:, i, :]
                        ins = V.scalar_tensor_tensor(out=acc[:, i, :], in0=yk[:, n % NG, :], scalar=wts[:, i, k:k + 1], in1=src,
                                                     op0=ALU.mult, op1=ALU.add)
                        ins.then_inc(f["gathered"], 1)
                        dve.wait_ge(f["gathered"], n + 1)
                    step.add(V.scalar_tensor_tensor(out=x_sb[:, i, :], in0=acc[:, i, :], scalar=gate, in1=x_sb[:, i, :],
                                                    op0=ALU.mult, op1=ALU.add))
                step.wait()
                dve.sem_inc(f["combined"], 1)
                if dbg is not None and not y.n:
                    dve.wait_ge(dbg_sem, 32)

            for y in LAYERS:
                if y.n:
                    norm(x_sb, xn)
                    step.done(V.tensor_tensor(tmp[:].rearrange("p (b q) d -> p b q d", q=QT), xn[:].rearrange("p (b q) d -> p b q d", q=QT),
                                              bc(summary[:], 2, QT), ALU.add))
                    norm(tmp, xn)
                    step.done(V.tensor_tensor(xn[:], xn[:], bc(R["gamma"], 1, NT), ALU.mult))
                    step.done(V.tensor_tensor(xn[:], xn[:], bc(R["beta"], 1, NT), ALU.add))
                    step.done(V.scalar_tensor_tensor(out=x_sb[:], in0=xn[:], scalar=tg[:, 1:2], in1=x_sb[:], op0=ALU.mult, op1=ALU.add))
                norm(x_sb, xn)
                dve.sem_inc(fs[y.n]["x_ready"], 1)
                f = fs[y.n]
                for m in range(4):
                    dve.wait_ge(f["xT_full"], m + 1)
                    V.tensor_copy(xnT[:, m // 2, (m % 2) * 512:(m % 2) * 512 + 512], bank[m][:]).then_inc(f["xT_ev"], 1)
                route(y)
                shared(y)
                experts(y)
                if dbg is not None:
                    dve.wait_ge(dbg_sem, 16 if y.n == 0 else 48)
                combine(y, tg[:, 2 + y.n:3 + y.n])

        @block.scalar
        def _(act):
            A = nc.scalar
            step = Steps(act, act_step)
            act.wait_ge(ld_small, 48)
            step.add(A.activation(tg[:], scal[:, 0:4], ACT.Tanh))
            step.done(A.activation(krow[:], scal[:, 4:5], ACT.Exp, scale=-1.0))
            act.sem_inc(gates_ready, 1)
            SUBS = QT * 4
            with act.Fori(0, B) as b:
                for oc in range(CC):
                    act.wait_ge(work_full[oc], b * FULL[oc] + 2)
                    A.activation(kT[:, oc, :], bank[6 + oc][:], ACT.Identity, bias=colb[:, 0, oc:oc + 1]).then_inc(work_free[oc], 1)
                for nt in range(QT):
                    act.wait_ge(work_full[nt], b * FULL[nt] + 3)
                    A.copy(qT[:, :, :, nt * P:(nt + 1) * P], bank[6 + nt][:].rearrange("p (r c n) -> p r c n", r=2, c=CC)).then_inc(work_free[nt], 1)

                def take(s, j):
                    act.wait_ge(t_full, b * SUBS * 4 + s * 4 + j + 1)
                    A.copy(pT[:, s % 2, j].rearrange("p t n -> p (t n)"), bank[4][:]).then_inc(t_free[0], 1)

                def back(nt):
                    act.wait_ge(av_done, b * SUBS + 4 * (nt + 1))
                    A.copy(oT[:].rearrange("p g n -> p (g n)"), bank[6][:]).then_inc(work_free[0], 1)

                for s in range(SUBS):
                    nt, g = divmod(s, 4)
                    for j in range(4):
                        act.wait_ge(scored, b * SUBS * 4 + s * 4 + j + 1)
                        A.activation(z_sb[:, s % 2, j, :], z_sb[:, s % 2, j, :], ACT.Exp, bias=zmin[:, s % 2, j:j + 1], scale=-1.0,
                                     accum_out=psum_row[:, nt, g, j:j + 1]).then_inc(expd, 1)
                        if j % 2 and s:
                            take(s - 1, j - 1)
                    if s == 5:
                        back(0)
                take(SUBS - 1, 0)
                take(SUBS - 1, 2)
                back(1)

            def route(y):
                f, E = fs[y.n], y.E
                act.wait_ge(f["log_ev"], 1)
                if y.n == 0:
                    A.activation(probs[:], probs[:], ACT.Exp).then_inc(f["r_act"], 1)
                    A.activation(sh_gate[:], logits[:, :, E], ACT.Exp, scale=-1.0).then_inc(f["r_act"], 1)
                else:
                    A.activation(probs[:, :, 0:E], logits[:, :, 0:E], ACT.Exp, scale=-1.0).then_inc(f["r_act"], 1)

            def shared(y):
                f = fs[y.n]
                nch = len(y.chunks)
                for m in range(2 * nch):
                    n = y.chunks[m % nch][1]
                    act.wait_ge(f["up_full"], m + 1)
                    if m >= 2:
                        act.wait_ge(f["up_free"], m - 1)
                    A.activation(sh_act[0:n, m % 2, :], bank[2 * (m % 2)][0:n, :], ACT.Silu).then_inc(f["up_act"], 1)

            def experts(y):
                f = fs[y.n]

                def silu(i, q, first):
                    act.wait_ge(f["e_up_full"], i + 1)
                    if not first:
                        act.wait_ge(f["e_mul"], i - 1)
                    A.activation(e_act[:, q, :], bank[2 + q][:, 0:I_EXP], ACT.Silu).then_inc(f["e_silu"], 1)

                def take_y(t, u, rounds, first):
                    act.wait_ge(f["y_full"], t + 1)
                    if not first:
                        act.wait_ge(f[f"y_st{u // 2 % 2}"], rounds)
                    A.copy(e_y[:, u % 4, :], bank[6 + u % 2][:, 0:D]).then_inc(f["y_ev"], 1)

                silu(0, 0, True)
                last = y.main - 1

                def one(t, u, rounds, more, first_s, first_y):
                    if more:
                        silu(t + 1, (u + 1) % 2, first_s)
                    take_y(t, u, rounds, first_y)

                W = 2 * NB
                turns = y.main // W
                for t in range(NB):
                    one(t, t, 16 * (t // 4), True, t + 1 < 2, t < 4)
                with act.Fori(0, (y.main - 2 * NB) // W) as it:
                    for v in range(W):
                        t = it * W + NB + v
                        one(t, NB + v, it * (16 * W // 4) + 16 * ((NB + v) // 4), True, False, False)
                for t in range(NB + (y.main - 2 * NB) // W * W, y.main):
                    one(t, t, 16 * (t // 4), t + 1 <= last, False, False)
                if y.extra:
                    n = act.value_load(nextra[0:1, 0:1], min_val=0, max_val=y.extra)
                    with act.Fori(0, y.extra) as v:
                        with act.If(n > v):
                            act.wait_ge(f["o_tfull"], v + 1)
                            A.copy(xgT[:, 0].rearrange("p c n -> p (c n)"), bank[0][:, 0:2 * P]).then_inc(f["o_tev"], 1)
                            act.wait_ge(f["o_up"], v + 1)
                            A.activation(e_act[:, 0, :], bank[2][:, 0:I_EXP], ACT.Silu).then_inc(f["o_silu"], 1)
                            act.wait_ge(f["o_y"], v + 1)
                            A.copy(e_y[:, 0, :], bank[6][:, 0:D]).then_inc(f["o_yev"], 1)

            for y in LAYERS:
                act.wait_ge(fs[y.n]["ld_gate"], 16)
                route(y)
                shared(y)
                act.wait_ge(fs[y.n]["plan_ready"], 1)
                experts(y)

        @block.tensor
        def _(pe):
            M = nc.tensor
            pe.wait_ge(consts, 1)

            def transpose_codes(order):
                for c in range(CC):
                    for i in range(NT):
                        last = M.transpose(bank[c][:].bitcast(BF16)[:, i * P:(i + 1) * P], codes[:, i, c * P:(c + 1) * P], identb[:])
                    last.then_inc(code_t, 1)

            pe.wait_ge(coded, 1)
            transpose_codes(0)
            pe.wait_ge(coded, 2)
            tb = bank[2][:].bitcast(BF16).rearrange("p (w c d) -> p w c d", w=2, c=CC)
            for w in range(2):
                for oc in range(CC):
                    for c in range(CC):
                        last = M.transpose(tb[:, w, c, oc * P:(oc + 1) * P], w_codes[:, w, oc, c * P:(c + 1) * P], identb[:])
            last.then_inc(code_t, 1)
            pe.wait_ge(diag_ready, 1)
            M.matmul(bank[3][:], ones[:], diag[:].rearrange("p a b -> p (a b)"), start=True, stop=True).then_inc(sw_full, 1)
            pe.wait_ge(seq_dve, 1)
            for t in range(LT):
                last = M.matmul(bank[4][:, t:t + 1], coef[0:1, t * P:(t + 1) * P], ones[0:1, 0:1], start=True, stop=True)
            last.then_inc(seq_pe, 1)
            pe.wait_ge(seq_dve, 2)
            pe.wait_ge(ld_nat, 16)
            for c in range(CC):
                for b in range(B):
                    for t in range(LT):
                        last = M.matmul(bank[5][:, c * B + b:c * B + b + 1], ctx_nat[:, b, t, c * P:(c + 1) * P], ccol[:, t:t + 1],
                                        start=(t == 0), stop=(t == LT - 1))
            last.then_inc(seq_pe, 1)
            pe.wait_ge(seq_dve, 3)
            pe.wait_ge(ld_wkv, 16)
            for ec in range(CC):
                for c in range(CC):
                    last = M.matmul(bank[4][:, ec * B:(ec + 1) * B], w_kv[:, 2, c, ec * P:(ec + 1) * P], zT[:, c, :],
                                    start=(c == 0), stop=(c == CC - 1))
            last.then_inc(seq_pe, 1)
            pe.wait_ge(seq_dve, 4)
            for b in range(B):
                for c in range(CC):
                    last = M.matmul(bank[6 + b // 2][:, (b % 2) * D:(b % 2 + 1) * D], mTb[:, c, b, :], w_kv[:, 3, c, :],
                                    start=(c == 0), stop=(c == CC - 1))
            last.then_inc(seq_pe, 1)
            pe.wait_ge(setup_done, 2)
            pe.wait_ge(code_ev, 3)
            SUBS = QT * 4
            pe.sem_inc(work_free[1], 1)
            with pe.Fori(0, B) as b:
                def freed(w, n):
                    pe.wait_ge(work_free[w], b * 6 + n + w)

                for nt in range(QT):
                    if nt:
                        freed(nt, 0)
                    for c in range(CC):
                        last = M.matmul(bank[6 + nt][:, 0:D], codesT[:, c, bass.ds(b * S + nt * P, P)], w_codesT[:, 0, c, :],
                                        start=(c == 0), stop=(c == CC - 1))
                    last.then_inc(work_full[nt], 1)
                pe.wait_ge(ld_ctx, b * 16 + 16)
                for oc in range(CC):
                    freed(oc, 1)
                    for c in range(CC):
                        last = M.matmul(bank[6 + oc][:], w_kv[:, 0, c, oc * P:(oc + 1) * P], ctxT[:, c, :],
                                        start=(c == 0), stop=(c == CC - 1))
                    last.then_inc(work_full[oc], 1)
                for nt in range(QT):
                    freed(nt, 2)
                    pe.wait_ge(dve_loop, b * 12 + 3 * (nt + 1))
                    for r in range(2):
                        for c in range(CC):
                            m = r * CC + c
                            last = M.transpose(bank[6 + nt][:, m * P:(m + 1) * P], q_split[:, nt, r, c * P:(c + 1) * P], ident[:])
                    last.then_inc(work_full[nt], 1)

                def scores(s):
                    nt, g = divmod(s, 4)
                    for j in range(4):
                        cc, par, _ = head(g, j)
                        if s:
                            pe.wait_ge(scored, b * SUBS * 4 + (s - 1) * 4 + j + 1)
                        M.matmul(bank[j][:], qT[32 * j:32 * j + 32, par, cc, nt * P:(nt + 1) * P], kT[32 * j:32 * j + 32, cc, :],
                                 start=True, stop=True).then_inc(score_full, 1)

                def probabilities(s):
                    for j in range(4):
                        pe.wait_ge(expd, b * SUBS * 4 + s * 4 + j + 1)
                        n = s * 2 + j // 2
                        if n:
                            pe.wait_ge(t_free[j % 2], b * SUBS * 2 + n)
                        for t in range(LT):
                            last = M.transpose(bank[4 + j % 2][:, t * P:(t + 1) * P], z_sb[:, s % 2, j, t * P:(t + 1) * P], ident[:])
                        last.then_inc(t_full, 1)

                def weigh(s):
                    nt, g = divmod(s, 4)
                    for k in range(2):
                        pe.wait_ge(t_free[k], b * SUBS * 2 + 2 * (s + 1))
                    if g == 0:
                        freed(0, 4 + nt)
                    for t in range(LT):
                        for j in range(4):
                            h = head(g, j)[2]
                            last = M.matmul(bank[6][32 * j:32 * j + 32, g * P:(g + 1) * P], v_sb[:, t, h, :], pT[:, s % 2, j, t, :],
                                            start=(t == 0), stop=(t == LT - 1))
                    last.then_inc(av_done, 1)

                def restore(nt):
                    freed(1, 4 + nt)
                    freed(0, 5 + nt)
                    for g in range(4):
                        last = M.transpose(bank[7][:, g * P:(g + 1) * P], oT[:, g, :], ident[:])
                    last.then_inc(work_full[1], 1)

                freed(0, 3)
                freed(1, 3)
                scores(0)
                for w in range(2):
                    for t in range(2):
                        for c in range(CC):
                            last = M.matmul(bank[6 + w][:, t * D:(t + 1) * D], ctxT[:, c, (2 * w + t) * P:(2 * w + t + 1) * P],
                                            w_kv[:, 1, c, :], start=(c == 0), stop=(c == CC - 1))
                    last.then_inc(work_full[w], 1)
                for s in range(SUBS):
                    if s + 1 < SUBS:
                        scores(s + 1)
                    probabilities(s)
                    if s:
                        weigh(s - 1)
                    if s == 5:
                        restore(0)
                weigh(SUBS - 1)
                restore(1)

            pe.wait_ge(coded, 3)
            transpose_codes(1)
            pe.wait_ge(code_ev, 5)
            for i in range(NT):
                if i >= 4:
                    pe.wait_ge(oproj_free, i - 3)
                for c in range(CC):
                    last = M.matmul(bank[2 + i % 4][:, 0:D], codesT[:, c, i * P:(i + 1) * P], w_codesT[:, 1, c, :],
                                    start=(c == 0), stop=(c == CC - 1))
                last.then_inc(oproj_full, 1)

            def ffn(y):
                f, E = fs[y.n], y.E
                pe.wait_ge(f["x_ready"], 1)
                for m in range(4):
                    for i in range(4):
                        t = (m % 2) * 4 + i
                        last = M.transpose(bank[m][:, i * P:(i + 1) * P], xn[:, t, (m // 2) * P:(m // 2 + 1) * P], ident[:])
                    last.then_inc(f["xT_full"], 1)
                pe.wait_ge(f["xT_ev"], 4)
                pe.wait_ge(f["ld_gate"], 16)
                ng = gate_w[y.n].shape[2]
                for i in range(NT):
                    for c in range(CC):
                        last = M.matmul(bank[6][:, i * 64:i * 64 + ng], xnT[:, c, i * P:(i + 1) * P], gate_w[y.n][:, c, :],
                                        start=(c == 0), stop=(c == CC - 1))
                last.then_inc(f["log_full"], 1)

                def positions():
                    pe.wait_ge(f["mem_ready"], 1)
                    for i in range(NT):
                        o = bank[7][:, i * 64:i * 64 + E]
                        M.matmul(o, onesb[:], earlier[:, i, 0:E], start=True, stop=False)
                        M.matmul(o, before[:], member[:, i, 0:E], start=False, stop=True)
                    M.matmul(bank[6][:, 0:E], onesb[:], earlier[:, NT, 0:E], start=True, stop=True).then_inc(f["pos_full"], 1)

                pe.wait_ge(f["ld_sh"], 16 * (1 + len(y.chunks)))
                nch = len(y.chunks)
                for half in range(2):
                    for c, (c0, n) in enumerate(y.chunks):
                        m = half * nch + c
                        if m >= 2:
                            pe.wait_ge(f["up_free"], m - 1)
                        for g in range(2):
                            for cc in range(CC):
                                last = M.matmul(bank[2 * (m % 2) + g][0:n, :], sh_in[:, cc, g * y.shared + c0:g * y.shared + c0 + n],
                                                xnT[:, cc, half * 512:half * 512 + 512], start=(cc == 0), stop=(cc == CC - 1))
                        last.then_inc(f["up_full"], 1)
                        if half == 0 and c == 1:
                            positions()
                    pe.wait_ge(f["up_free"], (half + 1) * nch)
                    for i in range(NT // 2):
                        t = half * (NT // 2) + i
                        if t >= 2:
                            pe.wait_ge(f["sh_free"], t - 1)
                        for c, (c0, n) in enumerate(y.chunks):
                            last = M.matmul(bank[4 + t % 2][:, 0:D], sh_h[0:n, c, i * P:(i + 1) * P], sh_out[0:n, c, :],
                                            start=(c == 0), stop=(c == nch - 1))
                        last.then_inc(f["sh_full"], 1)
                pe.wait_ge(f["sh_free"], NT)

                def turn(i, u, rnd, first):
                    if u % 2 == 0:
                        pe.wait_ge(f[f"ld_x{u // 2}"], 16 * rnd + 16)
                    if not first:
                        pe.wait_ge(f["xT2_ev"], i - 1)
                    for c in range(CC):
                        last = M.transpose(bank[u % 2][:, c * P:(c + 1) * P], xg[:, u, c * P:(c + 1) * P], ident[:])
                    last.then_inc(f["xT2_full"], 1)

                def up(i, u, rnd, first):
                    if u % 2 == 0:
                        pe.wait_ge(f[f"ld_w13_{u // 2}"], 32 * rnd + 32)
                    pe.wait_ge(f["xT2_ev"], i + 1)
                    if not first:
                        pe.wait_ge(f["e_mul"], i - 1)
                    for c in range(CC):
                        last = M.matmul(bank[2 + u % 2][:, 0:2 * I_EXP], xgT[:, u, c, :], w13[:, u, c, :], start=(c == 0), stop=(c == CC - 1))
                    last.then_inc(f["e_up_full"], 1)

                def turn_h(i, u, first):
                    pe.wait_ge(f["e_mul"], i + 1)
                    if not first:
                        pe.wait_ge(f["hT_ev"], i - 1)
                    for c in range(2):
                        last = M.transpose(bank[4 + u % 2][0:IC, c * P:(c + 1) * P], e_h[:, u % 2, c * IC:(c + 1) * IC], ident[:])
                    last.then_inc(f["hT_full"], 1)

                def down(i, u, rnd, first):
                    if u % 2 == 0:
                        pe.wait_ge(f[f"ld_w2_{u // 2}"], 32 * rnd + 32)
                    pe.wait_ge(f["hT_ev"], i + 1)
                    if not first:
                        pe.wait_ge(f["y_ev"], i - 1)
                    for c in range(2):
                        last = M.matmul(bank[6 + u % 2][:, 0:D], e_hT[:, u % 2, c, :], w2[:, u, c, :], start=(c == 0), stop=(c == 1))
                    last.then_inc(f["y_full"], 1)

                for i in range(3):
                    turn(i, i, 0, i < 2)
                up(0, 0, 0, True)
                turn_h(0, 0, True)
                last_t = y.main - 1

                def one(t, u, rnd, more, turns, first):
                    if more:
                        up(t + 1, (u + 1) % NB, rnd + (u + 1) // NB, first and t + 1 < 2)
                    down(t, u, rnd, first and t < 2)
                    if turns:
                        turn(t + 3, (u + 3) % NB, rnd + (u + 3) // NB, False)
                    if more:
                        turn_h(t + 1, (u + 1) % NB, first and t + 1 < 2)

                for t in range(NB):
                    one(t, t, 0, True, True, True)
                with pe.Fori(1, y.main // NB - 1) as it:
                    for u in range(NB):
                        one(it * NB + u, u, it, True, True, False)
                for t in range(y.main - NB, y.main):
                    one(t, t % NB, t // NB, t + 1 <= last_t, t + 3 <= last_t, False)
                if y.extra:
                    pe.wait_ge(f["plan_ready"], 1)
                    pe.wait_ge(f["y_ev"], y.main)
                    n = pe.value_load(nextra[0:1, 0:1], min_val=0, max_val=y.extra)
                    with pe.Fori(0, y.extra) as v:
                        with pe.If(n > v):
                            pe.wait_ge(f["ox_ld"], v * 48 + 48)
                            for c in range(CC):
                                last = M.transpose(bank[0][:, c * P:(c + 1) * P], xg[:, 0, c * P:(c + 1) * P], ident[:])
                            last.then_inc(f["o_tfull"], 1)
                            pe.wait_ge(f["o_tev"], v + 1)
                            for c in range(CC):
                                last = M.matmul(bank[2][:, 0:2 * I_EXP], xgT[:, 0, c, :], w13[:, 0, c, :], start=(c == 0), stop=(c == CC - 1))
                            last.then_inc(f["o_up"], 1)
                            pe.wait_ge(f["o_mul"], v + 1)
                            for c in range(2):
                                last = M.transpose(bank[4][0:IC, c * P:(c + 1) * P], e_h[:, 0, c * IC:(c + 1) * IC], ident[:])
                            last.then_inc(f["o_hfull"], 1)
                            pe.wait_ge(f["o_hev"], v + 1)
                            for c in range(2):
                                last = M.matmul(bank[6][:, 0:D], e_hT[:, 0, c, :], w2[:, 0, c, :], start=(c == 0), stop=(c == 1))
                            last.then_inc(f["o_y"], 1)

            ffn(L0)
            ffn(L1)


def layout(i):
    import numpy as np
    a = {k: np.asarray(v) for k, v in i.items()}
    c = np.ascontiguousarray

    def chunked(w, p=P):
        *lead, r, n = w.shape
        return c(np.moveaxis(w.reshape(*lead, r // p, p, n), -3, -2))

    t = {
        "x": a["x"].reshape(TOK, D),
        "ctx": a["ctx_2048"],
        "ctxT": chunked(a["ctx_2048"].transpose(0, 2, 1)),
        "mask": a["mask_BxSxS2_ff0"].reshape(NT, P, L),
        "w_qo": np.stack([a["L0_xattn_wq"], a["L0_xattn_wo"]]),
        "w_kv": np.stack([a["L0_xattn_wk"].T, a["L0_xattn_wv"].T, a["L1_xattn_W_in"].T, a["L1_xattn_W_out"].T]),
        "rows": np.stack([a["L0_xattn_bq"], a["L0_xattn_bv"], a["L0_xattn_bo"], a["L1_xattn_b_out"], a["L1_xattn_gamma"],
                          a["L1_xattn_beta"]]),
        "scalars": np.concatenate([a["g_xattn"], a["g_ffn"], a["L1_xattn_decay"].reshape(1), a["L1_ffn_router_bias"]]),
        "colb": np.stack([a["L0_xattn_bk"].reshape(CC, P).T, a["L1_xattn_b_in"].reshape(CC, P).T], axis=1),
        "gate0": chunked(np.concatenate([a["L0_ffn_gate_w"], a["L0_ffn_shared_gate_w"]]).T),
        "gate1": chunked(a["L1_ffn_gate_w"].T),
        "sh_in0": chunked(a["L0_ffn_se_gate_up_w"].T),
        "sh_out0": a["L0_ffn_se_down_w"].T,
        "sh_in1": chunked(np.concatenate([a["L1_ffn_sw1"], a["L1_ffn_sw3"]]).T),
        "sh_out1": a["L1_ffn_sw2"].T,
        "w13_0": chunked(a["L0_ffn_w13"].transpose(0, 2, 1)),
        "w2_0": chunked(a["L0_ffn_w2"].transpose(0, 2, 1), IC),
        "w13_1": chunked(np.concatenate([a["L1_ffn_W1"], a["L1_ffn_W3"]], axis=2)),
        "w2_1": chunked(a["L1_ffn_W2"], IC),
    }
    return {k: c(v) for k, v in t.items()}


def kernel(**inputs):
    import numpy as np
    import concourse.bacc as bacc
    from concourse.bass_utils import run_bass_kernel_spmd

    nc = bacc.Bacc("TRN2", target_bir_lowering=False, num_devices=1)
    arrays = {f"in_{k}": v for k, v in layout(inputs).items()}
    T = {k[3:]: nc.dram_tensor(k, v.shape, mybir.dt.from_np(v.dtype), kind="ExternalInput").ap() for k, v in arrays.items()}
    out = nc.dram_tensor("out", (TOK, D), F32, kind="ExternalOutput").ap()
    build(nc, T, out)
    r = run_bass_kernel_spmd(nc, [arrays], core_ids=[0])
    return np.asarray(r.results[0]["out"]).reshape(B, S, D)
```

```python
from contextlib import ExitStack

import concourse.bass as bass
from concourse import mybir

P = 128
F32 = mybir.dt.float32
BF16 = mybir.dt.bfloat16
I32 = mybir.dt.int32
U32 = mybir.dt.uint32
ALU = mybir.AluOpType
ACT = mybir.ActivationFunctionType
AX = mybir.AxisListType

B, S, D = 4, 256, 256
L = 512
H, DH = 16, 16
TOK = B * S
NT = TOK // P
CC = D // P
LT = L // P
QT = S // P
LN_EPS = 1e-5
Q_EPS = 1e-8
MAGIC = 12582912.0
BIG = 3.0e38
I_EXP = 176
IC = I_EXP // 2


NB = 6
PAIRS = NB // 2


class Layer:

    def __init__(self, n, experts, top, shared, own_tiles):
        self.n, self.E, self.K, self.shared = n, experts, top, shared
        self.own = own_tiles
        self.main = experts if own_tiles else -(-((TOK * top - experts) // P + experts) // NB) * NB
        self.extra = (TOK * top - experts) // P if own_tiles else 0
        self.tiles = -(-(self.main + self.extra) // B) * B
        self.chunks = [(c, min(P, shared - c)) for c in range(0, shared, P)]
        self.most = TOK // P


L0 = Layer(0, 60, 4, 704, 1)
L1 = Layer(1, 8, 2, 352, 0)
LAYERS = (L0, L1)
ROWS = ("bq", "bv", "bo", "b_out", "gamma", "beta")
NSC = 2 + 2 + 1 + L1.E


class Steps:

    def __init__(self, engine, sem, base=0):
        self.engine, self.sem, self.base, self.n = engine, sem, base, 0

    def add(self, instruction, by=1):
        instruction.then_inc(self.sem, by)
        self.n += by

    def wait(self):
        self.engine.wait_ge(self.sem, self.base + self.n)

    def done(self, instruction):
        self.add(instruction)
        self.wait()


def build(nc, T, out, dbg=None):
    with ExitStack() as ctx:
        def sb(name, shape, dt=F32):
            return ctx.enter_context(nc.sbuf_tensor(name, shape, dt))

        def sem(name):
            return ctx.enter_context(nc.semaphore(name))

        bank = [ctx.enter_context(nc.psum_tensor(f"bank{i}", [P, 512], F32)) for i in range(8)]

        xg_dram = [nc.dram_tensor(f"sorted_x{y.n}", [y.tiles * P, D], F32).ap() for y in LAYERS]
        y_dram = [nc.dram_tensor(f"expert_y{y.n}", [y.tiles * P, D], F32).ap() for y in LAYERS]

        stage = sb("stage", [P, 27424])
        at = [0]

        def part(shape):
            n = 1
            for m in shape:
                n *= m
            names = "abcd"[:len(shape)]
            v = stage[:, at[0]:at[0] + n].rearrange(f"p ({' '.join(names)}) -> p {' '.join(names)}", **dict(zip(names, shape)))
            at[0] += n
            assert at[0] <= stage.shape[1]
            return v

        x_sb = sb("x_sb", [P, NT, D])
        xn = sb("xn", [P, NT, D])
        tmp = sb("tmp", [P, NT, D])
        q_src = part([2 * QT, D])
        codes = sb("codes", [P, 2 * QT, D], BF16)
        codesT = sb("codesT", [P, CC, 2 * QT, P], BF16)
        st = sb("st", [P, NT, 6])
        mv = sb("mv", [P, NT, 2])
        rstd = sb("rstd", [P, NT])
        vare = sb("vare", [P, NT])
        mhalf = sb("mhalf", [P, NT])
        sx = sb("sx", [P, 2 * QT])
        sx4 = sb("sx4", [P, QT])
        rsx = sb("rsx", [P, 2 * QT])
        rows = sb("rows", [P, len(ROWS), D])
        scal = sb("scal", [P, NSC])
        tg = sb("tg", [P, 4])
        colb = sb("colb", [P, 2, CC])
        ident = sb("ident", [P, P])
        identb = sb("identb", [P, P], BF16)
        ones = sb("ones", [P, P])
        onesb = sb("onesb", [P, P], BF16)
        before = sb("before", [P, P], BF16)
        zeros = sb("zeros", [P, D])
        w_q = part([2, CC, D])
        w_codes = sb("w_codes", [P, 2, CC, D], BF16)
        w_codesT = sb("w_codesT", [P, 2, CC, D], BF16)
        sw = sb("sw", [P, 4])
        rsw = sb("rsw", [P, 4])
        diag = part([4, P])
        sw_rows = sb("sw_rows", [P, 2, D])
        w_kv = part([4, CC, D])
        ctxT = part([CC, L])
        mask = part([QT, L])
        q_split = part([QT, 2, D])
        q_tmp = sb("q_tmp", [P, QT, D])
        qT = part([2, CC, S])
        kT = part([CC, L])
        v_sb = part([LT, H, 32])
        z_sb = part([2, 4, L])
        pT = part([2, 4, LT, P])
        zmin = sb("zmin", [P, 2, 4])
        psum_row = sb("psum_row", [P, QT, 4, 4])
        rsum = sb("rsum", [P, QT, 4, 4])
        oT = sb("oT", [P, 4, P])
        krow = sb("krow", [P, 1])
        coef = part([L])
        csum = sb("csum", [P, 1])
        z_col = sb("z_col", [P, CC])
        zT = sb("zT", [P, CC, B])
        mT = sb("mT", [P, CC, B])
        bin_s = sb("bin_s", [P, CC])
        mTb = part([CC, B, P])
        summary = sb("summary", [P, B, D])
        at[0] = 0
        xnT = sb("xnT", [P, CC, TOK])
        gate_w = [sb(f"gate_w{y.n}", [P, CC, y.E + 1 - y.n]) for y in LAYERS]
        NSH = len(L0.chunks)
        sh_in = sb("sh_in", [P, CC, 2 * L0.shared])
        sh_out = sb("sh_out", [P, NSH, D])
        sh_act = part([2, 512])
        sh_h = part([NSH, 512])
        sh_y = part([NT, D])
        EM, KM = L0.E, L0.K
        logits = part([NT, 64])
        probs = sb("probs", [P, NT, EM])
        picks = part([NT, EM])
        rmax = sb("rmax", [P, NT])
        rsm = sb("rsm", [P, NT])
        sh_gate = sb("sh_gate", [P, NT])
        top8 = sb("top8", [P, NT, 8])
        idx8 = sb("idx8", [P, NT, 8], U32)
        idxf = sb("idxf", [P, NT, 8])
        hot = part([NT, KM, EM])
        hot2 = part([NT, KM, EM])
        member = sb("member", [P, NT, EM], BF16)
        earlier = sb("earlier", [P, NT + 1, EM], BF16)
        iota_e = sb("iota_e", [P, EM])
        iota_v = sb("iota_v", [P, 32])
        cnt = sb("cnt", [P, EM])
        ntile = sb("ntile", [P, EM])
        incl = sb("incl", [P, EM])
        base = sb("base", [P, EM])
        over = sb("over", [P, EM])
        pos = part([NT, EM])
        posb = part([NT, EM])
        slotf = sb("slotf", [P, NT, KM])
        slot = sb("slot", [P, NT, KM], U32)
        wts = sb("wts", [P, NT, KM])
        owner_c = hot2.rearrange("p t k e -> p (t k) e")[0:1]
        owner_f = sb("owner_f", [1, 32])
        owner = sb("owner", [1, 32], I32)
        nextra = sb("nextra", [1, 2], I32)
        xg = part([NB, D])
        xgT = part([NB, CC, P])
        w13 = part([NB, CC, 2 * I_EXP])
        w2 = part([NB, 2, D])[0:IC]
        e_act = sb("e_act", [P, 2, I_EXP])
        e_h = sb("e_h", [P, 2, I_EXP])
        e_hT = sb("e_hT", [IC, 2, 2, P])
        e_y = part([4, D])
        NG = 4
        yk = part([NG, D])
        acc = part([NT, D])

        FULL = (4, 6)
        ld_x0, ld_x, ld_small, ld_wqo, ld_wkv, ld_ctx = map(sem, ("ld_x0", "ld_x", "ld_small", "ld_wqo", "ld_wkv", "ld_ctx"))
        ld_mask = [sem("ld_mask0"), sem("ld_mask1")]
        zero_tile, zeroed = sem("zero_tile"), [sem("zeroed0"), sem("zeroed1")]
        pool_step, dve_step, act_step = sem("pool_step"), sem("dve_step"), sem("act_step")
        consts = sem("consts")
        var_ready, rstd_ready = sem("var_ready"), sem("rstd_ready")
        coded, code_t, code_ev = sem("coded"), sem("code_t"), sem("code_ev")
        q_ready, ctx_seen = sem("q_ready"), sem("ctx_seen")
        scales_ready, x_updated, pool_loop, pool_pass = sem("scales_ready"), sem("x_updated"), sem("pool_loop"), sem("pool_pass")
        diag_ready, sw_full, setup_done = sem("diag_ready"), sem("sw_full"), sem("setup_done")
        seq_pe, seq_dve = sem("seq_pe"), sem("seq_dve")
        gates_ready = sem("gates_ready")
        dve_loop = sem("dve_loop")
        work_full = [sem("work_full0"), sem("work_full1")]
        work_free = [sem("work_free0"), sem("work_free1")]
        score_full, scored, expd = sem("score_full"), sem("scored"), sem("expd")
        t_full, t_free = sem("t_full"), [sem("t_free0"), sem("t_free1")]
        av_done, dve_pass, sp_pass = sem("av_done"), sem("dve_pass"), sem("sp_pass")
        oproj_full, oproj_free = sem("oproj_full"), sem("oproj_free")
        fs = []
        for y in LAYERS:
            fs.append({k: sem(f"{k}{y.n}") for k in (
                "ld_sh", "ld_gate", "x_ready", "xT_full", "xT_ev", "log_full", "log_ev", "r_act", "mem_ready", "pos_full",
                "slots_ready", "plan_ready", "scattered", "up_full", "up_act", "up_free", "sh_full", "sh_free",
                "xT2_full", "xT2_ev", "e_up_full", "e_silu", "e_mul", "hT_full", "hT_ev", "y_full", "y_ev",
                "ox_ld", "o_tfull", "o_tev", "o_up", "o_silu", "o_mul", "o_hfull", "o_hev", "o_y", "o_yev", "o_st", "o_done", "extra_done",
                "gathered", "combined") if y.extra or k[0:2] not in ("o_", "ox")})
            for i in range(PAIRS):
                for k in ("ld_x", "ld_w13_", "ld_w2_"):
                    fs[-1][f"{k}{i}"] = sem(f"{k}{i}_{y.n}")
            for i in range(2):
                fs[-1][f"y_st{i}"] = sem(f"y_st{i}_{y.n}")
            for i in range(NG):
                fs[-1][f"gat{i}"] = sem(f"gat{i}_{y.n}")
        stored = sem("stored")
        dbg_sem = sem("dbg_sem")

        block = ctx.enter_context(nc.Block())
        R = {n: rows[:, i, :] for i, n in enumerate(ROWS)}

        def bc(ap, axis, n):
            v = ap.unsqueeze(axis)
            shape = list(v.shape)
            shape[axis] = n
            return v.to_broadcast(shape)

        def head(g, j):
            cc, par = divmod(g, 2)
            return cc, par, cc * 8 + 2 * j + par

        @block.sync
        def _(sp):
            def load_x_tiles(a, b, signal):
                sp.dma_start(x_sb[:, a:b, :], T["x"][a * P:b * P, :].rearrange("(t p) d -> p t d", p=P)).then_inc(signal, 16)

            def load_ctx(b):
                sp.dma_start(ctxT[:], T["ctxT"][bass.ds(b, 1)].rearrange("o p c l -> p (o c) l")).then_inc(ld_ctx, 16)

            def load_mask(b, nt):
                sp.dma_start(mask[:, nt, :], T["mask"][bass.ds(b * QT + nt, 1)].rearrange("o p l -> p (o l)")).then_inc(ld_mask[nt], 16)

            def shared_weights(y):
                f = fs[y.n]
                sp.dma_start(sh_in[:, :, 0:2 * y.shared], T[f"sh_in{y.n}"]).then_inc(f["ld_sh"], 16)
                for c, (c0, n) in enumerate(y.chunks):
                    sp.dma_start(sh_out[0:n, c, :], T[f"sh_out{y.n}"][c0:c0 + n, :]).then_inc(f["ld_sh"], 16)

            def zero_quarter(b):
                for y in LAYERS:
                    n = y.tiles // B
                    for d in (xg_dram[y.n], y_dram[y.n]):
                        sp.dma_start(d.rearrange("(p a) d -> p a d", p=P)[:, bass.ds(b * n, n), :],
                                     bc(zeros[:], 1, n)).then_inc(zeroed[y.n], 16)

            load_x_tiles(0, QT, ld_x0)
            sp.dma_start(w_q[:], T["w_qo"].rearrange("w (c p) d -> p w c d", p=P)).then_inc(ld_wqo, 16)
            sp.dma_start(rows[:], T["rows"].rearrange("(o r) d -> o r d", o=1).to_broadcast([P, len(ROWS), D])).then_inc(ld_small, 16)
            sp.dma_start(scal[:], T["scalars"].rearrange("(o r) -> o r", o=1).to_broadcast([P, NSC])).then_inc(ld_small, 16)
            sp.dma_start(colb[:], T["colb"]).then_inc(ld_small, 16)
            load_ctx(0)
            sp.dma_start(w_kv[:], T["w_kv"].rearrange("w (c p) d -> p w c d", p=P)).then_inc(ld_wkv, 16)
            load_mask(0, 0)
            load_x_tiles(QT, NT, ld_x)
            load_mask(0, 1)
            sp.wait_ge(zero_tile, 1)
            zero_quarter(0)
            with sp.Fori(0, B - 1) as b:
                sp.wait_ge(work_full[1], b * 6 + 4)
                sp.sem_inc(sp_pass, 1)
                sp.wait_ge(ctx_seen, b + 1)
                load_ctx(b + 1)
                for nt in range(QT):
                    sp.wait_ge(scored, b * (QT * 16) + (nt + 1) * 16)
                    load_mask(b + 1, nt)
                    if nt == 0:
                        zero_quarter(b + 1)
            for y in LAYERS:
                sp.dma_start(gate_w[y.n][:], T[f"gate{y.n}"]).then_inc(fs[y.n]["ld_gate"], 16)
            shared_weights(L0)
            if dbg is not None and "attn" in dbg:
                sp.wait_ge(fs[0]["x_ready"], 4)
                sp.dma_start(dbg["attn"].rearrange("(t p) d -> p t d", p=P), x_sb[:]).then_inc(dbg_sem, 16)
                sp.wait_ge(dbg_sem, 16)

            def experts(y):
                f = fs[y.n]
                wi, wo = T[f"w13_{y.n}"], T[f"w2_{y.n}"]

                def owners(p):
                    return [sp.value_load(owner[0:1, bass.ds(p * 2 + h, 1)], min_val=0, max_val=y.E - 1) for h in range(2)]

                def load_w(dst, src, p, s, key, own):
                    if y.own:
                        sp.dma_start(dst[:, 2 * s:2 * s + 2].rearrange("p e c n -> p e (c n)"),
                                     src[bass.ds(p * 2, 2)].rearrange("e p c n -> p e (c n)")).then_inc(f[f"{key}{s}"], 32)
                    else:
                        for h in range(2):
                            sp.dma_start(dst[:, 2 * s + h], src[bass.ds(own[h], 1)].rearrange("o p c n -> p (o c) n"))\
                              .then_inc(f[f"{key}{s}"], 16)

                def load_x(p, s):
                    sp.dma_start(xg[:, 2 * s:2 * s + 2, :],
                                 xg_dram[y.n][bass.ds(p * 2 * P, 2 * P), :].rearrange("(h p) d -> p h d", p=P)).then_inc(f[f"ld_x{s}"], 16)

                pairs = y.main // 2
                if y.own:
                    sp.wait_ge(f["xT_full"], B)
                else:
                    sp.wait_ge(f["plan_ready"], 1)
                for p in range(PAIRS):
                    own = None if y.own else owners(p)
                    load_w(w13, wi, p, p, "ld_w13_", own)
                    load_w(w2, wo, p, p, "ld_w2_", own)
                sp.wait_ge(f["scattered"], 16 * NT * y.K)
                for p in range(PAIRS):
                    load_x(p, p)
                sp.wait_ge(f["xT2_full"], 2)
                load_x(PAIRS, 0)

                def pair(p, s, whole, more_x):
                    own = None
                    if whole:
                        if not y.own:
                            own = owners(p + PAIRS)
                        sp.wait_ge(f["e_up_full"], p * 2 + 2)
                        load_w(w13, wi, p + PAIRS, s, "ld_w13_", own)
                    if more_x:
                        sp.wait_ge(f["xT2_full"], p * 2 + 4)
                        load_x(p + PAIRS + 1, (s + 1) % PAIRS)
                    if whole:
                        sp.wait_ge(f["y_full"], p * 2 + 2)
                        load_w(w2, wo, p + PAIRS, s, "ld_w2_", own)

                def store(p, q):
                    sp.wait_ge(f["y_ev"], p * 2 + 2)
                    sp.dma_start(y_dram[y.n][bass.ds(p * 2 * P, 2 * P), :].rearrange("(h p) d -> p h d", p=P),
                                 e_y[:, 2 * q:2 * q + 2, :]).then_inc(f[f"y_st{q}"], 16)

                turns = (pairs - PAIRS) // (2 * PAIRS)
                with sp.Fori(0, turns) as it:
                    for u in range(2 * PAIRS):
                        pair(it * (2 * PAIRS) + u, u % PAIRS, True, True)
                        store(it * (2 * PAIRS) + u, u % 2)
                for p in range(turns * 2 * PAIRS, pairs):
                    pair(p, p % PAIRS, p + PAIRS < pairs, p + PAIRS + 1 < pairs)
                    store(p, p % 2)
                if y.extra:
                    n = sp.value_load(nextra[0:1, 0:1], min_val=0, max_val=y.extra)
                    for q in range(2):
                        sp.wait_ge(f[f"y_st{q}"], 16 * (y.main // 4))
                    with sp.If(n > 0):
                        with sp.Fori(0, y.extra) as v:
                            with sp.If(n > v):
                                e = sp.value_load(owner[0:1, bass.ds(v, 1)], min_val=0, max_val=y.E - 1)
                                sp.dma_start(w13[:, 0], wi[bass.ds(e, 1)].rearrange("o p c n -> p (o c) n")).then_inc(f["ox_ld"], 16)
                                sp.dma_start(w2[:, 0], wo[bass.ds(e, 1)].rearrange("o p c n -> p (o c) n")).then_inc(f["ox_ld"], 16)
                                sp.dma_start(xg[:, 0, :], xg_dram[y.n][bass.ds((v + y.main) * P, P), :]).then_inc(f["ox_ld"], 16)
                                sp.wait_ge(f["o_yev"], v + 1)
                                sp.dma_start(y_dram[y.n][bass.ds((v + y.main) * P, P), :], e_y[:, 0, :]).then_inc(f["o_st"], 16)
                                sp.wait_ge(f["o_st"], v * 16 + 16)
                                sp.sem_inc(f["o_done"], 1)
                sp.sem_inc(f["extra_done"], 1)

            experts(L0)
            sp.wait_ge(fs[0]["sh_full"], NT)
            shared_weights(L1)
            if dbg is not None and "ffn0" in dbg:
                sp.wait_ge(fs[0]["combined"], 1)
                sp.dma_start(dbg["ffn0"].rearrange("(t p) d -> p t d", p=P), x_sb[:]).then_inc(dbg_sem, 16)
                sp.wait_ge(dbg_sem, 32)
            if dbg is not None and "seq" in dbg:
                sp.wait_ge(fs[1]["x_ready"], 1)
                sp.dma_start(dbg["seq"].rearrange("(t p) d -> p t d", p=P), x_sb[:]).then_inc(dbg_sem, 16)
                sp.wait_ge(dbg_sem, 48)
            experts(L1)
            sp.wait_ge(fs[1]["combined"], 1)
            sp.dma_start(out.rearrange("(t p) d -> p t d", p=P), x_sb[:]).then_inc(stored, 16)
            sp.wait_ge(stored, 16)

        @block.gpsimd
        def _(gp):
            step = Steps(gp, pool_step)
            step.done(gp.memset(zeros[:], 0.0))
            gp.sem_inc(zero_tile, 1)
            step.done(gp.memset(ident[:], 0.0))
            step.done(gp.affine_select(out=ident[:], in_=ident[:], compare_op=ALU.not_equal, fill=1.0, base=0,
                                       pattern=[[-1, P]], channel_multiplier=1))
            step.add(gp.tensor_copy(identb[:], ident[:]))
            step.done(gp.memset(ones[:], 1.0))
            step.add(gp.tensor_copy(onesb[:], ones[:]))
            step.add(gp.affine_select(out=before[:], in_=ones[:], compare_op=ALU.is_gt, fill=0.0, base=0,
                                      pattern=[[1, P]], channel_multiplier=-1))
            step.add(gp.iota(iota_e[:], pattern=[[1, EM]], base=0, channel_multiplier=0, allow_small_or_imprecise_dtypes=True))
            step.add(gp.iota(iota_v[:], pattern=[[1, 32]], base=0, channel_multiplier=0, allow_small_or_imprecise_dtypes=True))
            step.add(gp.memset(v_sb[:], 0.0))
            step.add(gp.memset(q_split[:], 0.0))
            step.done(gp.memset(mhalf[:], -0.5))
            gp.sem_inc(consts, 1)

            def power(n, tiles):
                gp.wait_ge(var_ready, n)
                gp.tensor_tensor(rstd[:, 0:tiles], vare[:, 0:tiles], mhalf[:, 0:tiles], ALU.pow).then_inc(rstd_ready, 1)

            def dispatch(y):
                f = fs[y.n]
                gp.wait_ge(f["slots_ready"], 1)
                gp.wait_ge(zeroed[y.n], 2 * B * 16)
                for i in range(NT):
                    for k in range(y.K):
                        gp.indirect_dma_start(out=xg_dram[y.n][:, :], out_offset=bass.IndirectOffsetOnAxis(slot[:, i, k:k + 1], 0),
                                              in_=xn[:, i, :], in_offset=None).then_inc(f["scattered"], 16)

            def collect(y):
                f = fs[y.n]
                for q in range(2):
                    gp.wait_ge(f[f"y_st{q}"], 16 * (y.main // 4))
                gp.wait_ge(f["extra_done"], 1)
                for i in range(NT):
                    for k in range(y.K):
                        n = i * y.K + k
                        if n >= NG:
                            gp.wait_ge(f["gathered"], n - NG + 1)
                        gp.indirect_dma_start(out=yk[:, n % NG, :], out_offset=None, in_=y_dram[y.n][:, :],
                                              in_offset=bass.IndirectOffsetOnAxis(slot[:, i, k:k + 1], 0)).then_inc(f[f"gat{n % NG}"], 16)

            FIRST_STEPS, MID_STEPS = 8, 18

            def batch(b, pre, post, base_steps):
                ls = Steps(gp, pool_loop, base_steps)
                lo, hi = (0 if pre else QT), (2 * QT if post else QT)

                def done(instruction):
                    ls.done(instruction)
                    gp.sem_inc(pool_pass, 1)

                def normalise(buf, count):
                    gp.wait_ge(var_ready, count)
                    gp.sem_inc(pool_pass, 1)
                    done(gp.tensor_tensor(rstd[:, 0:QT], vare[:, 0:QT], mhalf[:, 0:QT], ALU.pow))
                    for i in range(QT):
                        ls.add(gp.tensor_scalar(buf[:, i, :], buf[:, i, :], mv[:, i, 0:1], rstd[:, i:i + 1], ALU.subtract, ALU.mult))
                    ls.wait()
                    gp.sem_inc(pool_pass, 1)

                if pre:
                    done(gp.tensor_copy(q_src[:, 0:QT, :], x_sb[:, bass.ds((b + 1) * QT, QT), :]))
                    normalise(q_src[:, 0:QT, :], b * 2 + 1 if post else 2)
                    gp.sem_inc(rstd_ready, 1)
                gp.wait_ge(scales_ready, b + 1)
                gp.sem_inc(pool_pass, 1)
                for i in range(lo, hi):
                    ls.add(gp.tensor_scalar(tmp[:, i, :], q_src[:, i, :], rsx[:, i:i + 1], MAGIC, ALU.mult, ALU.add))
                ls.wait()
                gp.sem_inc(pool_pass, 1)
                done(gp.tensor_scalar(tmp[:, lo:hi, :], tmp[:, lo:hi, :], MAGIC, 127.0, ALU.subtract, ALU.min))
                done(gp.tensor_scalar(codes[:, lo:hi, :], tmp[:, lo:hi, :], -127.0, None, ALU.max))
                gp.sem_inc(coded, 1)
                if post:
                    y = tmp[:, 4:4 + QT, :]
                    xq, xnq = (v[:, bass.ds((b - 1) * QT, QT), :] for v in (x_sb, xn))
                    gp.wait_ge(oproj_free, b)
                    gp.sem_inc(pool_pass, 1)
                    done(gp.tensor_tensor(y, y, bc(R["bo"], 1, QT), ALU.add))
                    done(gp.tensor_scalar(y, y, tg[:, 0:1], None, ALU.mult))
                    done(gp.tensor_tensor(y, y, xq, ALU.add))
                    gp.sem_inc(x_updated, 1)
                    done(gp.tensor_copy(xq, y))
                    normalise(y, b * 2 + (2 if pre else 1))
                    done(gp.tensor_copy(xnq, y))
                    gp.sem_inc(rstd_ready, 1)
                    gp.sem_inc(fs[0]["x_ready"], 1)
                return ls.n

            power(1, QT)
            gp.wait_ge(coded, 1)
            gp.wait_ge(ld_x, 16)
            gp.wait_ge(gates_ready, 1)
            n = batch(0, True, False, 0)
            assert n == FIRST_STEPS, n
            with gp.Fori(1, B - 1) as b:
                n = batch(b, True, True, (b - 1) * MID_STEPS + FIRST_STEPS)
                assert n == MID_STEPS, n
            batch(B - 1, False, True, (B - 2) * MID_STEPS + FIRST_STEPS)
            power(2 * B, QT)
            dispatch(L0)
            collect(L0)
            for i in range(3):
                power(2 * B + 1 + i, NT)
            dispatch(L1)
            collect(L1)

        @block.vector
        def _(dve):
            step = Steps(dve, dve_step)
            V = nc.vector

            def moments(step, src, n):
                dve.sem_inc(dve_pass, 1)
                for i in range(n):
                    step.add(V.bn_stats(st[:, i, :], src(i)))
                step.wait()
                dve.sem_inc(dve_pass, 1)
                for i in range(n):
                    step.add(V.bn_aggr(mv[:, i, :], st[:, i, :]))
                step.wait()
                V.tensor_scalar(vare[:, 0:n], mv[:, 0:n, 1], LN_EPS, None, ALU.add).then_inc(var_ready, 1)

            def normalise(step, src, dst, n, count):
                dve.wait_ge(rstd_ready, count)
                for i in range(n):
                    step.add(V.tensor_scalar(dst(i), src(i), mv[:, i, 0:1], rstd[:, i:i + 1], ALU.subtract, ALU.mult))
                step.wait()

            def norm(src, dst, count):
                moments(step, lambda i: src[:, i, :], NT)
                normalise(step, lambda i: src[:, i, :], lambda i: dst[:, i, :], NT, count)

            def find_scales(step, src, scales, inverse):
                step.done(V.tensor_reduce(scales, src, AX.X, ALU.max, apply_absolute_value=True))
                step.done(V.tensor_scalar(scales, scales, 1.0 / 127.0, Q_EPS, ALU.mult, ALU.max))
                step.done(V.reciprocal(inverse, scales))

            def quantise(step, src, dst, scales, inverse, n, scratch):
                find_scales(step, src, scales, inverse)
                for i in range(n):
                    step.add(V.tensor_scalar(scratch[:, i, :], src[:, i, :], inverse[:, i:i + 1], MAGIC, ALU.mult, ALU.add))
                step.wait()
                step.done(V.tensor_scalar(scratch, scratch, MAGIC, 127.0, ALU.subtract, ALU.min))
                step.done(V.tensor_scalar(dst, scratch, -127.0, None, ALU.max))
                dve.sem_inc(coded, 1)

            def quantise_slots(step, lo, hi):
                quantise(step, q_src[:, lo:hi, :], codes[:, lo:hi, :], sx[:, lo:hi], rsx[:, lo:hi], hi - lo, tmp[:, lo:hi, :])
                if lo == 0:
                    step.done(V.tensor_scalar(sx4[:], sx[:, 0:QT], 0.25, None, ALU.mult))

            dve.wait_ge(ld_x0, 16)
            moments(step, lambda i: x_sb[:, i, :], QT)
            normalise(step, lambda i: x_sb[:, i, :], lambda i: q_src[:, i, :], QT, 1)
            quantise_slots(step, 0, QT)
            dve.wait_ge(ld_wqo, 16)
            wq3 = w_q[:].rearrange("p w c d -> p (w c) d")
            quantise(step, wq3, w_codes[:].rearrange("p w c d -> p (w c) d"), sw[:], rsw[:], 4, tmp[:, 0:4, :])
            dve.wait_ge(consts, 1)
            for i in range(4):
                step.add(V.tensor_scalar(diag[:, i, :], ident[:], sw[:, i:i + 1], None, ALU.mult))
            step.wait()
            dve.sem_inc(diag_ready, 1)
            dve.wait_ge(ld_small, 48)
            step.done(V.tensor_scalar(R["bq"], R["bq"], 0.25, None, ALU.mult))

            def take_codes(n, w, lo, hi):
                dve.wait_ge(code_t, n)
                src = bank[w][:].bitcast(BF16)[:, 0:CC * (hi - lo) * P].rearrange("p (c t n) -> p c t n", c=CC, t=hi - lo)
                V.tensor_copy(codesT[:, :, lo:hi, :], src).then_inc(code_ev, 1)

            take_codes(1, 0, 0, QT)
            dve.wait_ge(code_t, 2)
            V.tensor_copy(w_codesT[:].rearrange("p w c d -> p (w c d)"), bank[2][:].bitcast(BF16)).then_inc(code_ev, 1)
            dve.wait_ge(sw_full, 1)
            step.done(V.tensor_copy(sw_rows[:].rearrange("p w d -> p (w d)"), bank[3][:]))
            dve.sem_inc(setup_done, 1)

            SUBS = QT * 4
            FIRST_STEPS, MID_STEPS = 24, 25

            def batch(b, pre, post, base_steps):
                ls = Steps(dve, dve_loop, base_steps)
                lo, hi = (0 if pre else QT), (2 * QT if post else QT)
                x_next = lambda i: x_sb[:, bass.ds((b + 1) * QT + i, 1), :].rearrange("p o d -> p (o d)")

                for nt in range(QT):
                    dve.wait_ge(work_full[nt], b * FULL[nt] + 1)
                    q3 = V.scalar_tensor_tensor(out=q_tmp[:, nt, :], in0=bank[6 + nt][:, 0:D], scalar=sx4[:, nt:nt + 1],
                                                in1=sw_rows[:, 0, :], op0=ALU.mult, op1=ALU.mult)
                    ls.done(q3)
                    dve.sem_inc(work_free[nt], 1)
                    for par in range(2):
                        v = lambda ap: ap.rearrange("p (h two d) -> p h two d", two=2, d=DH)[:, :, par, :]
                        V.tensor_tensor(v(q_split[:, nt, par, :]), v(q_tmp[:, nt, :]), v(R["bq"]), ALU.add).then_inc(q_ready, 1)

                def score(s):
                    nt, g = divmod(s, 4)
                    if g == 0:
                        dve.wait_ge(ld_mask[nt], b * 16 + 16)
                    for j in range(4):
                        dve.wait_ge(score_full, b * SUBS * 4 + s * 4 + j + 1)
                        dve.sem_inc(dve_pass, 1)
                        V.tensor_tensor_reduce(out=z_sb[:, s % 2, j, :], in0=bank[j][:], in1=mask[:, nt, :], scale=-1.0,
                                               scalar=BIG, op0=ALU.add, op1=ALU.min,
                                               accum_out=zmin[:, s % 2, j:j + 1]).then_inc(scored, 1)
                        if j % 2 and s:
                            take(s - 1, j)
                    if s == 0:
                        values()

                def take(s, j):
                    dve.wait_ge(t_full, b * SUBS * 4 + s * 4 + j + 1)
                    V.tensor_copy(pT[:, s % 2, j].rearrange("p t n -> p (t n)"), bank[5][:]).then_inc(t_free[1], 1)

                def values():
                    for w in range(2):
                        dve.wait_ge(work_full[w], b * FULL[w] + 4)
                        V.tensor_tensor(v_sb[:, 2 * w:2 * w + 2, :, 0:DH],
                                        bank[6 + w][:].rearrange("p (t h d) -> p t h d", h=H, d=DH),
                                        bc(R["bv"].rearrange("p (h d) -> p h d", d=DH), 1, 2), ALU.add).then_inc(work_free[w], 1)

                def finish(nt):
                    dve.wait_ge(expd, b * SUBS * 4 + (nt + 1) * 16)
                    ls.done(V.reciprocal(rsum[:, nt], psum_row[:, nt]))
                    dve.wait_ge(work_full[1], b * 6 + 5 + nt)
                    for cc in range(CC):
                        src = bank[7][:].rearrange("p (g j d) -> p g j d", j=4, d=32)[:, 2 * cc:2 * cc + 2, :, 0:DH]
                        dst = q_src[:, QT + nt, :].rearrange("p (c j r d) -> p c r j d", c=CC, j=4, r=2)[:, cc]
                        ls.add(V.tensor_tensor(dst, src, bc(rsum[:, nt, 2 * cc:2 * cc + 2, :], 3, DH), ALU.mult))
                    ls.wait()
                    dve.sem_inc(work_free[1], 1)

                def decay_weights():
                    dve.wait_ge(gates_ready, 1)
                    ls.done(V.tensor_scalar(krow[:], krow[:], 1.0, None, ALU.add))
                    ls.done(V.reciprocal(krow[:], krow[:]))
                    ls.done(V.tensor_tensor_scan(coef[:, L - 1::-1], krow[:].to_broadcast([P, L]), ones[:, 0:1].to_broadcast([P, L]),
                                                 0.0, ALU.mult, ALU.add))
                    ls.done(V.tensor_reduce(csum[:], coef[:], AX.X, ALU.add))
                    ls.done(V.tensor_scalar(bin_s[:], colb[:, 1, :], csum[:], None, ALU.mult))

                def weigh_context():
                    scratch = tmp[:, 6:8, :].rearrange("p t d -> p (t d)")
                    for c in range(CC):
                        ls.done(V.tensor_tensor_reduce(out=scratch, in0=ctxT[:, c, :], in1=coef[:], scale=1.0, scalar=0.0,
                                                       op0=ALU.mult, op1=ALU.add, accum_out=z_col[:, c:c + 1]))
                    dve.sem_inc(ctx_seen, 1)
                    ls.done(V.tensor_copy(zT[:, :, bass.ds(b, 1)], z_col[:].unsqueeze(2)))

                def next_scales():
                    if pre:
                        dve.wait_ge(rstd_ready, b * 2 + 1 if post else 2)
                    find_scales(ls, q_src[:, lo:hi, :], sx[:, lo:hi], rsx[:, lo:hi])
                    if pre:
                        ls.done(V.tensor_scalar(sx4[:], sx[:, 0:QT], 0.25, None, ALU.mult))
                    dve.sem_inc(scales_ready, 1)

                for s in range(SUBS):
                    score(s)
                    if s == 0 and pre:
                        if post:
                            dve.wait_ge(rstd_ready, b * 2)
                        else:
                            dve.wait_ge(ld_x, 16)
                        moments(ls, x_next, QT)
                    if s == 1:
                        next_scales()
                    if s == 2:
                        if not post:
                            decay_weights()
                        weigh_context()
                    if s == 4:
                        take_codes(b + 3, 7, lo, hi)
                    if s == 5 and post:
                        take_output(ls, 4, b)
                    if s == 6:
                        finish(0)
                    if s == 7 and post:
                        dve.wait_ge(x_updated, b)
                        moments(ls, lambda i: tmp[:, 4 + i, :], QT)
                take(SUBS - 1, 1)
                take(SUBS - 1, 3)
                finish(1)
                return ls.n

            def take_output(step, at, count):
                dve.wait_ge(oproj_full, count)
                for i in range(QT):
                    step.add(V.scalar_tensor_tensor(out=tmp[:, at + i, :], in0=bank[7][:, i * D:(i + 1) * D], scalar=sx[:, QT + i:QT + i + 1],
                                                    in1=sw_rows[:, 1, :], op0=ALU.mult, op1=ALU.mult))
                step.wait()
                dve.sem_inc(oproj_free, 1)

            n = batch(0, True, False, 0)
            assert n == FIRST_STEPS, n
            with dve.Fori(1, B - 1) as b:
                n = batch(b, True, True, (b - 1) * MID_STEPS + FIRST_STEPS)
                assert n == MID_STEPS, n
            batch(B - 1, False, True, (B - 2) * MID_STEPS + FIRST_STEPS)

            quantise_slots(step, QT, 2 * QT)
            take_codes(B + 3, 7, QT, 2 * QT)
            dve.wait_ge(seq_pe, 1)
            step.done(V.tensor_tensor(mT[:], bank[4][:, 0:CC * B].rearrange("p (c b) -> p c b", c=CC), bc(bin_s[:], 2, B), ALU.add))
            step.done(V.tensor_scalar(mTb[:].rearrange("p c b n -> p (c b) n"), bc(mT[:].rearrange("p c b -> p (c b)"), 2, P),
                                      1.0 / L, None, ALU.mult))
            dve.sem_inc(seq_dve, 1)
            take_output(step, 0, B)
            step.done(V.tensor_tensor(tmp[:, 0:QT, :], tmp[:, 0:QT, :], bc(R["bo"], 1, QT), ALU.add))
            last_x = x_sb[:, NT - QT:NT, :]
            step.done(V.scalar_tensor_tensor(out=last_x, in0=tmp[:, 0:QT, :], scalar=tg[:, 0:1], in1=last_x, op0=ALU.mult, op1=ALU.add))
            dve.wait_ge(rstd_ready, 2 * B - 1)
            moments(step, lambda i: x_sb[:, NT - QT + i, :], QT)
            normalise(step, lambda i: x_sb[:, NT - QT + i, :], lambda i: xn[:, NT - QT + i, :], QT, 2 * B)
            dve.sem_inc(fs[0]["x_ready"], 1)
            dve.wait_ge(fs[0]["xT_full"], B)
            V.tensor_copy(xnT[:, :, (B - 1) * S:B * S], bank[7][:].rearrange("p (c n) -> p c n", c=CC)).then_inc(fs[0]["xT_ev"], 1)
            dve.wait_ge(seq_pe, 2)
            for h in range(2):
                step.add(V.tensor_tensor(summary[:, 2 * h:2 * h + 2, :], bank[4 + h][:].rearrange("p (b d) -> p b d", b=2),
                                         bc(R["b_out"], 1, 2), ALU.add))
            step.wait()
            dve.sem_inc(seq_dve, 1)

            def route(y):
                f, E, K = fs[y.n], y.E, y.K
                lg = logits[:, :, 0:E]
                pr, pk = probs[:, :, 0:E], picks[:, :, 0:E]
                dve.wait_ge(f["log_full"], 1)
                ng = gate_w[y.n].shape[2]
                step.done(V.tensor_copy(logits[:, :, 0:ng], bank[6][:].rearrange("p (t e) -> p t e", t=NT)[:, :, 0:ng]))
                if y.n == 0:
                    step.done(V.tensor_reduce(rmax[:], lg, AX.X, ALU.max))
                    V.tensor_tensor(pr, lg, bc(rmax[:], 2, E), ALU.subtract).then_inc(f["log_ev"], 1)
                    dve.wait_ge(f["r_act"], 2)
                    step.done(V.tensor_reduce(rsm[:], pr, AX.X, ALU.add))
                    step.done(V.reciprocal(rsm[:], rsm[:]))
                    step.done(V.tensor_tensor(pr, pr, bc(rsm[:], 2, E), ALU.mult))
                    step.done(V.tensor_scalar(sh_gate[:], sh_gate[:], 1.0, None, ALU.add))
                    step.done(V.reciprocal(sh_gate[:], sh_gate[:]))
                    keys = probs
                else:
                    dve.sem_inc(f["log_ev"], 1)
                    dve.wait_ge(f["r_act"], 1)
                    step.done(V.tensor_scalar(pr, pr, 1.0, None, ALU.add))
                    step.done(V.reciprocal(pr, pr))
                    step.done(V.tensor_tensor(pk, pr, bc(scal[:, 5:5 + E], 1, NT), ALU.add))
                    keys = picks
                for i in range(NT):
                    step.add(V.max(top8[:, i, :], keys[:, i, 0:E]))
                step.wait()
                for i in range(NT):
                    step.add(V.max_index(idx8[:, i, :], top8[:, i, :], keys[:, i, 0:E]))
                step.wait()
                step.done(V.tensor_copy(idxf[:], idx8[:]))
                h1, h2 = hot[:, :, 0:K, 0:E], hot2[:, :, 0:K, 0:E]
                for k in range(K):
                    step.add(V.tensor_tensor(hot[:, :, k, 0:E], bc(iota_e[:, 0:E], 1, NT), bc(idxf[:, :, k], 2, E), ALU.is_equal))
                step.wait()
                mem = member[:, :, 0:E]
                step.done(V.tensor_tensor(mem, hot[:, :, 0, 0:E], hot[:, :, 1, 0:E], ALU.add))
                for k in range(2, K):
                    step.done(V.tensor_tensor(mem, mem, hot[:, :, k, 0:E], ALU.add))
                step.done(V.memset(earlier[:, 0, 0:E], 0.0))
                for i in range(NT):
                    step.done(V.tensor_tensor(earlier[:, i + 1, 0:E], earlier[:, i, 0:E], member[:, i, 0:E], ALU.add))
                dve.sem_inc(f["mem_ready"], 1)
                if y.n == 0:
                    step.done(V.tensor_copy(wts[:], top8[:, :, 0:K]))
                else:
                    for k in range(K):
                        step.add(V.tensor_tensor(hot2[:, :, k, 0:E], hot[:, :, k, 0:E], pr, ALU.mult))
                    step.wait()
                    for k in range(K):
                        step.add(V.tensor_reduce(wts[:, :, k], hot2[:, :, k, 0:E], AX.X, ALU.add))
                    step.wait()
                    step.done(V.tensor_tensor(rsm[:], wts[:, :, 0], wts[:, :, 1], ALU.add))
                    step.done(V.tensor_scalar(rsm[:], rsm[:], 1e-12, None, ALU.max))
                    step.done(V.reciprocal(rsm[:], rsm[:]))
                    step.done(V.tensor_tensor(wts[:, :, 0:K], wts[:, :, 0:K], bc(rsm[:], 2, K), ALU.mult))
                dve.wait_ge(f["pos_full"], 1)
                c, n, inc, bs, ov = cnt[:, 0:E], ntile[:, 0:E], incl[:, 0:E], base[:, 0:E], over[:, 0:E]
                step.add(V.tensor_copy(c, bank[6][:, 0:E]))
                ps, pb = pos[:, :, 0:E], posb[:, :, 0:E]
                step.done(V.tensor_copy(ps, bank[7][:].rearrange("p (t e) -> p t e", t=NT)[:, :, 0:E]))
                first = P if y.own else 0
                step.done(V.tensor_scalar(n, c, float(first), None, ALU.is_gt))
                for m in range(first + P, TOK, P):
                    step.done(V.scalar_tensor_tensor(out=n, in0=c, scalar=float(m), in1=n, op0=ALU.is_gt, op1=ALU.add))
                step.done(V.tensor_tensor_scan(inc, ones[:, 0:E], n, 0.0, ALU.mult, ALU.add))
                step.done(V.tensor_tensor(bs, inc, n, ALU.subtract))
                step.done(V.tensor_scalar(bs, bs, float(P), None, ALU.mult))
                if y.own:
                    step.done(V.scalar_tensor_tensor(out=ov, in0=iota_e[:, 0:E], scalar=-float(P), in1=bs, op0=ALU.mult, op1=ALU.add))
                    step.done(V.tensor_scalar(ov, ov, float(P * (y.main - 1)), None, ALU.add))
                    step.done(V.tensor_scalar(pb, ps, float(P), None, ALU.is_ge))
                    step.done(V.tensor_tensor(pb, pb, bc(ov, 1, NT), ALU.mult))
                    step.done(V.tensor_tensor(pb, pb, ps, ALU.add))
                    step.done(V.tensor_scalar(ov, iota_e[:, 0:E], float(P), None, ALU.mult))
                    step.done(V.tensor_tensor(pb, pb, bc(ov, 1, NT), ALU.add))
                else:
                    step.done(V.tensor_tensor(pb, ps, bc(bs, 1, NT), ALU.add))
                for k in range(K):
                    step.add(V.tensor_tensor(hot[:, :, k, 0:E], hot[:, :, k, 0:E], pb, ALU.mult))
                step.wait()
                for k in range(K):
                    step.add(V.tensor_reduce(slotf[:, :, k], hot[:, :, k, 0:E], AX.X, ALU.add))
                step.wait()
                V.tensor_copy(slot[:, :, 0:K], slotf[:, :, 0:K]).then_inc(f["slots_ready"], 1)
                NV = y.extra if y.own else y.main
                step.done(V.tensor_tensor(owner_c[0:1, 0:NV, 0:E], bc(incl[0:1, 0:E], 1, NV), bc(iota_v[0:1, 0:NV], 2, E), ALU.is_le))
                step.done(V.tensor_reduce(owner_f[0:1, 0:NV], owner_c[0:1, 0:NV, 0:E], AX.X, ALU.add))
                step.done(V.tensor_scalar(owner_f[0:1, 0:NV], owner_f[0:1, 0:NV], float(E - 1), None, ALU.min))
                step.done(V.tensor_copy(owner[0:1, 0:NV], owner_f[0:1, 0:NV]))
                step.done(V.tensor_copy(nextra[0:1, 0:1], incl[0:1, E - 1:E]))
                dve.sem_inc(f["plan_ready"], 1)

            def shared(y):
                f = fs[y.n]
                nch = len(y.chunks)
                for half in range(2):
                    if half:
                        dve.wait_ge(f["sh_full"], NT // 2)
                    for c, (c0, n) in enumerate(y.chunks):
                        m = half * nch + c
                        dve.wait_ge(f["up_act"], m + 1)
                        V.tensor_tensor(sh_h[0:n, c, :], sh_act[0:n, m % 2, :], bank[2 * (m % 2) + 1][0:n, :],
                                        ALU.mult).then_inc(f["up_free"], 1)
                    for i in range(NT // 2):
                        t = half * (NT // 2) + i
                        dve.wait_ge(f["sh_full"], t + 1)
                        if y.n == 0:
                            V.tensor_scalar(sh_y[:, t, :], bank[4 + t % 2][:, 0:D], sh_gate[:, t:t + 1], None,
                                            ALU.mult).then_inc(f["sh_free"], 1)
                        else:
                            V.tensor_copy(sh_y[:, t, :], bank[4 + t % 2][:, 0:D]).then_inc(f["sh_free"], 1)

            def experts(y):
                f = fs[y.n]

                def take_x(i, u, first):
                    dve.wait_ge(f["xT2_full"], i + 1)
                    if not first:
                        dve.wait_ge(f["e_up_full"], i - NB + 1)
                    V.tensor_copy(xgT[:, u].rearrange("p c n -> p (c n)"), bank[u % 2][:, 0:2 * P]).then_inc(f["xT2_ev"], 1)

                def gated(i, q, first):
                    dve.wait_ge(f["e_silu"], i + 1)
                    if not first:
                        dve.wait_ge(f["hT_full"], i - 1)
                    V.tensor_tensor(e_h[:, q, :], e_act[:, q, :], bank[2 + q][:, I_EXP:2 * I_EXP], ALU.mult).then_inc(f["e_mul"], 1)

                def take_h(i, q, first):
                    dve.wait_ge(f["hT_full"], i + 1)
                    if not first:
                        dve.wait_ge(f["y_full"], i - 1)
                    V.tensor_copy(e_hT[:, q].rearrange("p c n -> p (c n)"), bank[4 + q][0:IC, 0:2 * P]).then_inc(f["hT_ev"], 1)

                def one(t, u, more, turn, first):
                    if more:
                        gated(t + 1, (u + 1) % 2, first)
                    if turn:
                        take_x(t + 3, (u + 3) % NB, first and t + 3 < NB)
                    if more:
                        take_h(t + 1, (u + 1) % 2, first)

                for i in range(3):
                    take_x(i, i, True)
                gated(0, 0, True)
                take_h(0, 0, True)
                last = y.main - 1
                for t in range(NB):
                    one(t, t, True, True, t < 1) if t < 1 or t + 3 >= NB else (gated(t + 1, (t + 1) % 2, False),
                                                                               take_x(t + 3, t + 3, True), take_h(t + 1, (t + 1) % 2, False))
                with dve.Fori(1, y.main // NB - 1) as it:
                    for u in range(NB):
                        one(it * NB + u, u, True, True, False)
                for t in range(y.main - NB, y.main):
                    one(t, t % NB, t + 1 <= last, t + 3 <= last, False)
                if y.extra:
                    n = dve.value_load(nextra[0:1, 0:1], min_val=0, max_val=y.extra)
                    with dve.If(n > 0):
                        with dve.Fori(0, y.extra) as v:
                            with dve.If(n > v):
                                dve.wait_ge(f["o_silu"], v + 1)
                                V.tensor_tensor(e_h[:, 0, :], e_act[:, 0, :], bank[2][:, I_EXP:2 * I_EXP], ALU.mult).then_inc(f["o_mul"], 1)
                                dve.wait_ge(f["o_hfull"], v + 1)
                                V.tensor_copy(e_hT[:, 0].rearrange("p c n -> p (c n)"), bank[4][0:IC, 0:2 * P]).then_inc(f["o_hev"], 1)

            def combine(y, gate):
                f = fs[y.n]
                for i in range(NT):
                    for k in range(y.K):
                        n = i * y.K + k
                        dve.wait_ge(f[f"gat{n % NG}"], 16 * (n // NG + 1))
                        src = sh_y[:, i, :] if k == 0 else acc[:, i, :]
                        ins = V.scalar_tensor_tensor(out=acc[:, i, :], in0=yk[:, n % NG, :], scalar=wts[:, i, k:k + 1], in1=src,
                                                     op0=ALU.mult, op1=ALU.add)
                        ins.then_inc(f["gathered"], 1)
                        dve.wait_ge(f["gathered"], n + 1)
                    step.add(V.scalar_tensor_tensor(out=x_sb[:, i, :], in0=acc[:, i, :], scalar=gate, in1=x_sb[:, i, :],
                                                    op0=ALU.mult, op1=ALU.add))
                step.wait()
                dve.sem_inc(f["combined"], 1)
                if dbg is not None and not y.n:
                    dve.wait_ge(dbg_sem, 32)

            for y in LAYERS:
                if y.n:
                    norm(x_sb, xn, 2 * B + 1)
                    step.done(V.tensor_tensor(tmp[:].rearrange("p (b q) d -> p b q d", q=QT), xn[:].rearrange("p (b q) d -> p b q d", q=QT),
                                              bc(summary[:], 2, QT), ALU.add))
                    norm(tmp, xn, 2 * B + 2)
                    step.done(V.tensor_tensor(xn[:], xn[:], bc(R["gamma"], 1, NT), ALU.mult))
                    step.done(V.tensor_tensor(xn[:], xn[:], bc(R["beta"], 1, NT), ALU.add))
                    step.done(V.scalar_tensor_tensor(out=x_sb[:], in0=xn[:], scalar=tg[:, 1:2], in1=x_sb[:], op0=ALU.mult, op1=ALU.add))
                    norm(x_sb, xn, 2 * B + 3)
                    dve.sem_inc(fs[y.n]["x_ready"], 1)
                    f = fs[y.n]
                    for m in range(4):
                        dve.wait_ge(f["xT_full"], m + 1)
                        V.tensor_copy(xnT[:, m // 2, (m % 2) * 512:(m % 2) * 512 + 512], bank[m][:]).then_inc(f["xT_ev"], 1)
                route(y)
                shared(y)
                experts(y)
                if dbg is not None:
                    dve.wait_ge(dbg_sem, 16 if y.n == 0 else 48)
                combine(y, tg[:, 2 + y.n:3 + y.n])

        @block.scalar
        def _(act):
            A = nc.scalar
            step = Steps(act, act_step)
            act.wait_ge(ld_small, 48)
            step.add(A.activation(tg[:], scal[:, 0:4], ACT.Tanh))
            step.done(A.activation(krow[:], scal[:, 4:5], ACT.Exp, scale=-1.0))
            act.sem_inc(gates_ready, 1)
            SUBS = QT * 4
            with act.Fori(0, B) as b:
                for oc in range(CC):
                    act.wait_ge(work_full[oc], b * FULL[oc] + 2)
                    A.activation(kT[:, oc, :], bank[6 + oc][:], ACT.Identity, bias=colb[:, 0, oc:oc + 1]).then_inc(work_free[oc], 1)
                for nt in range(QT):
                    act.wait_ge(work_full[nt], b * FULL[nt] + 3)
                    A.copy(qT[:, :, :, nt * P:(nt + 1) * P], bank[6 + nt][:].rearrange("p (r c n) -> p r c n", r=2, c=CC)).then_inc(work_free[nt], 1)

                def take(s, j):
                    act.wait_ge(t_full, b * SUBS * 4 + s * 4 + j + 1)
                    A.copy(pT[:, s % 2, j].rearrange("p t n -> p (t n)"), bank[4][:]).then_inc(t_free[0], 1)

                def back(nt):
                    act.wait_ge(av_done, b * SUBS + 4 * (nt + 1))
                    A.copy(oT[:].rearrange("p g n -> p (g n)"), bank[6][:]).then_inc(work_free[0], 1)

                for s in range(SUBS):
                    nt, g = divmod(s, 4)
                    for j in range(4):
                        act.wait_ge(scored, b * SUBS * 4 + s * 4 + j + 1)
                        A.activation(z_sb[:, s % 2, j, :], z_sb[:, s % 2, j, :], ACT.Exp, bias=zmin[:, s % 2, j:j + 1], scale=-1.0,
                                     accum_out=psum_row[:, nt, g, j:j + 1]).then_inc(expd, 1)
                        if j % 2 and s:
                            take(s - 1, j - 1)
                    if s == 5:
                        back(0)
                take(SUBS - 1, 0)
                take(SUBS - 1, 2)
                back(1)

            for q in range(B - 1):
                act.wait_ge(fs[0]["xT_full"], q + 1)
                A.copy(xnT[:, :, q * S:(q + 1) * S], bank[q][:].rearrange("p (c n) -> p c n", c=CC)).then_inc(fs[0]["xT_ev"], 1)

            def route(y):
                f, E = fs[y.n], y.E
                act.wait_ge(f["log_ev"], 1)
                if y.n == 0:
                    A.activation(probs[:], probs[:], ACT.Exp).then_inc(f["r_act"], 1)
                    A.activation(sh_gate[:], logits[:, :, E], ACT.Exp, scale=-1.0).then_inc(f["r_act"], 1)
                else:
                    A.activation(probs[:, :, 0:E], logits[:, :, 0:E], ACT.Exp, scale=-1.0).then_inc(f["r_act"], 1)

            def shared(y):
                f = fs[y.n]
                nch = len(y.chunks)
                for m in range(2 * nch):
                    n = y.chunks[m % nch][1]
                    act.wait_ge(f["up_full"], m + 1)
                    if m >= 2:
                        act.wait_ge(f["up_free"], m - 1)
                    A.activation(sh_act[0:n, m % 2, :], bank[2 * (m % 2)][0:n, :], ACT.Silu).then_inc(f["up_act"], 1)

            def experts(y):
                f = fs[y.n]

                def silu(i, q, first):
                    act.wait_ge(f["e_up_full"], i + 1)
                    if not first:
                        act.wait_ge(f["e_mul"], i - 1)
                    A.activation(e_act[:, q, :], bank[2 + q][:, 0:I_EXP], ACT.Silu).then_inc(f["e_silu"], 1)

                def take_y(t, u, rounds, first):
                    act.wait_ge(f["y_full"], t + 1)
                    if not first:
                        act.wait_ge(f[f"y_st{u // 2 % 2}"], rounds)
                    A.copy(e_y[:, u % 4, :], bank[6 + u % 2][:, 0:D]).then_inc(f["y_ev"], 1)

                silu(0, 0, True)
                last = y.main - 1

                def one(t, u, rounds, more, first_s, first_y):
                    if more:
                        silu(t + 1, (u + 1) % 2, first_s)
                    take_y(t, u, rounds, first_y)

                W = 2 * NB
                turns = y.main // W
                for t in range(NB):
                    one(t, t, 16 * (t // 4), True, t + 1 < 2, t < 4)
                with act.Fori(0, (y.main - 2 * NB) // W) as it:
                    for v in range(W):
                        t = it * W + NB + v
                        one(t, NB + v, it * (16 * W // 4) + 16 * ((NB + v) // 4), True, False, False)
                for t in range(NB + (y.main - 2 * NB) // W * W, y.main):
                    one(t, t, 16 * (t // 4), t + 1 <= last, False, False)
                if y.extra:
                    n = act.value_load(nextra[0:1, 0:1], min_val=0, max_val=y.extra)
                    with act.If(n > 0):
                        with act.Fori(0, y.extra) as v:
                            with act.If(n > v):
                                act.wait_ge(f["o_tfull"], v + 1)
                                A.copy(xgT[:, 0].rearrange("p c n -> p (c n)"), bank[0][:, 0:2 * P]).then_inc(f["o_tev"], 1)
                                act.wait_ge(f["o_up"], v + 1)
                                A.activation(e_act[:, 0, :], bank[2][:, 0:I_EXP], ACT.Silu).then_inc(f["o_silu"], 1)
                                act.wait_ge(f["o_y"], v + 1)
                                A.copy(e_y[:, 0, :], bank[6][:, 0:D]).then_inc(f["o_yev"], 1)

            for y in LAYERS:
                act.wait_ge(fs[y.n]["ld_gate"], 16)
                route(y)
                shared(y)
                act.wait_ge(fs[y.n]["plan_ready"], 1)
                experts(y)

        @block.tensor
        def _(pe):
            M = nc.tensor
            pe.wait_ge(consts, 1)

            def turn_codes(n, w, lo, hi):
                pe.wait_ge(coded, n)
                dst = bank[w][:].bitcast(BF16)[:, 0:CC * (hi - lo) * P].rearrange("p (c t n) -> p c t n", c=CC, t=hi - lo)
                for c in range(CC):
                    for i in range(hi - lo):
                        last = M.transpose(dst[:, c, i, :], codes[:, lo + i, c * P:(c + 1) * P], identb[:])
                last.then_inc(code_t, 1)

            turn_codes(1, 0, 0, QT)
            pe.wait_ge(coded, 2)
            tb = bank[2][:].bitcast(BF16).rearrange("p (w c d) -> p w c d", w=2, c=CC)
            for w in range(2):
                for oc in range(CC):
                    for c in range(CC):
                        last = M.transpose(tb[:, w, c, oc * P:(oc + 1) * P], w_codes[:, w, oc, c * P:(c + 1) * P], identb[:])
            last.then_inc(code_t, 1)
            pe.wait_ge(diag_ready, 1)
            M.matmul(bank[3][:], ones[:], diag[:].rearrange("p a b -> p (a b)"), start=True, stop=True).then_inc(sw_full, 1)
            pe.wait_ge(setup_done, 1)
            pe.wait_ge(code_ev, 2)
            pe.wait_ge(ld_wkv, 16)
            SUBS = QT * 4
            pe.sem_inc(work_free[1], 1)

            def output(q):
                pe.wait_ge(code_ev, q + 4)
                for i in range(QT):
                    for c in range(CC):
                        last = M.matmul(bank[7][:, i * D:(i + 1) * D], codesT[:, c, QT + i, :], w_codesT[:, 1, c, :],
                                        start=(c == 0), stop=(c == CC - 1))
                last.then_inc(oproj_full, 1)

            def turn_x(q, w):
                pe.wait_ge(fs[0]["x_ready"], q + 1)
                for c in range(CC):
                    for i in range(QT):
                        last = M.transpose(bank[w][:, (c * QT + i) * P:(c * QT + i + 1) * P],
                                           xn[:, q * QT + i, c * P:(c + 1) * P], ident[:])
                last.then_inc(fs[0]["xT_full"], 1)

            def batch(b, pre, post):
                lo, hi = (0 if pre else QT), (2 * QT if post else QT)

                def freed(w, n):
                    pe.wait_ge(work_free[w], b * 6 + n + w)

                for nt in range(QT):
                    if nt:
                        freed(nt, 0)
                    for c in range(CC):
                        last = M.matmul(bank[6 + nt][:, 0:D], codesT[:, c, nt, :], w_codesT[:, 0, c, :],
                                        start=(c == 0), stop=(c == CC - 1))
                    last.then_inc(work_full[nt], 1)
                pe.wait_ge(ld_ctx, b * 16 + 16)
                for oc in range(CC):
                    freed(oc, 1)
                    for c in range(CC):
                        last = M.matmul(bank[6 + oc][:], w_kv[:, 0, c, oc * P:(oc + 1) * P], ctxT[:, c, :],
                                        start=(c == 0), stop=(c == CC - 1))
                    last.then_inc(work_full[oc], 1)
                for nt in range(QT):
                    freed(nt, 2)
                    pe.wait_ge(q_ready, b * 4 + 2 * (nt + 1))
                    for r in range(2):
                        for c in range(CC):
                            m = r * CC + c
                            last = M.transpose(bank[6 + nt][:, m * P:(m + 1) * P], q_split[:, nt, r, c * P:(c + 1) * P], ident[:])
                    last.then_inc(work_full[nt], 1)

                def scores(s):
                    nt, g = divmod(s, 4)
                    for j in range(4):
                        cc, par, _ = head(g, j)
                        if s:
                            pe.wait_ge(scored, b * SUBS * 4 + (s - 1) * 4 + j + 1)
                        M.matmul(bank[j][:], qT[32 * j:32 * j + 32, par, cc, nt * P:(nt + 1) * P], kT[32 * j:32 * j + 32, cc, :],
                                 start=True, stop=True).then_inc(score_full, 1)

                def probabilities(s):
                    for j in range(4):
                        pe.wait_ge(expd, b * SUBS * 4 + s * 4 + j + 1)
                        n = s * 2 + j // 2
                        if n:
                            pe.wait_ge(t_free[j % 2], b * SUBS * 2 + n)
                        for t in range(LT):
                            last = M.transpose(bank[4 + j % 2][:, t * P:(t + 1) * P], z_sb[:, s % 2, j, t * P:(t + 1) * P], ident[:])
                        last.then_inc(t_full, 1)

                def weigh(s):
                    nt, g = divmod(s, 4)
                    for k in range(2):
                        pe.wait_ge(t_free[k], b * SUBS * 2 + 2 * (s + 1))
                    if g == 0:
                        freed(0, 4 + nt)
                    for t in range(LT):
                        for j in range(4):
                            h = head(g, j)[2]
                            last = M.matmul(bank[6][32 * j:32 * j + 32, g * P:(g + 1) * P], v_sb[:, t, h, :], pT[:, s % 2, j, t, :],
                                            start=(t == 0), stop=(t == LT - 1))
                    last.then_inc(av_done, 1)

                def restore(nt):
                    freed(1, 4 + nt)
                    freed(0, 5 + nt)
                    if nt == 0:
                        pe.wait_ge(code_ev, b + 3)
                        if post:
                            pe.wait_ge(oproj_free, b)
                    for g in range(4):
                        last = M.transpose(bank[7][:, g * P:(g + 1) * P], oT[:, g, :], ident[:])
                    last.then_inc(work_full[1], 1)

                freed(0, 3)
                freed(1, 3)
                scores(0)
                for w in range(2):
                    for t in range(2):
                        for c in range(CC):
                            last = M.matmul(bank[6 + w][:, t * D:(t + 1) * D], ctxT[:, c, (2 * w + t) * P:(2 * w + t + 1) * P],
                                            w_kv[:, 1, c, :], start=(c == 0), stop=(c == CC - 1))
                    last.then_inc(work_full[w], 1)
                for s in range(SUBS):
                    if s + 1 < SUBS:
                        scores(s + 1)
                    probabilities(s)
                    if s:
                        weigh(s - 1)
                    if s == 3:
                        freed(1, 4)
                        turn_codes(b + 3, 7, lo, hi)
                    if s == 4 and post:
                        output(b - 1)
                    if s == 5:
                        restore(0)
                weigh(SUBS - 1)
                restore(1)

            batch(0, True, False)
            with pe.Fori(1, B - 1) as b:
                batch(b, True, True)
            batch(B - 1, False, True)

            for q in range(B - 1):
                turn_x(q, q)
            turn_codes(B + 3, 7, QT, 2 * QT)
            for ec in range(CC):
                for c in range(CC):
                    last = M.matmul(bank[4][:, ec * B:(ec + 1) * B], w_kv[:, 2, c, ec * P:(ec + 1) * P], zT[:, c, :],
                                    start=(c == 0), stop=(c == CC - 1))
            last.then_inc(seq_pe, 1)
            output(B - 1)
            pe.wait_ge(seq_dve, 1)
            for b in range(B):
                for c in range(CC):
                    last = M.matmul(bank[4 + b // 2][:, (b % 2) * D:(b % 2 + 1) * D], mTb[:, c, b, :], w_kv[:, 3, c, :],
                                    start=(c == 0), stop=(c == CC - 1))
            last.then_inc(seq_pe, 1)
            turn_x(B - 1, 7)

            def ffn(y):
                f, E = fs[y.n], y.E
                if y.n:
                    pe.wait_ge(f["x_ready"], 1)
                    for m in range(4):
                        for i in range(4):
                            t = (m % 2) * 4 + i
                            last = M.transpose(bank[m][:, i * P:(i + 1) * P], xn[:, t, (m // 2) * P:(m // 2 + 1) * P], ident[:])
                        last.then_inc(f["xT_full"], 1)
                pe.wait_ge(f["xT_ev"], 4)
                pe.wait_ge(f["ld_gate"], 16)
                ng = gate_w[y.n].shape[2]
                for i in range(NT):
                    for c in range(CC):
                        last = M.matmul(bank[6][:, i * 64:i * 64 + ng], xnT[:, c, i * P:(i + 1) * P], gate_w[y.n][:, c, :],
                                        start=(c == 0), stop=(c == CC - 1))
                last.then_inc(f["log_full"], 1)

                def positions():
                    pe.wait_ge(f["mem_ready"], 1)
                    for i in range(NT):
                        o = bank[7][:, i * 64:i * 64 + E]
                        M.matmul(o, onesb[:], earlier[:, i, 0:E], start=True, stop=False)
                        M.matmul(o, before[:], member[:, i, 0:E], start=False, stop=True)
                    M.matmul(bank[6][:, 0:E], onesb[:], earlier[:, NT, 0:E], start=True, stop=True).then_inc(f["pos_full"], 1)

                pe.wait_ge(f["ld_sh"], 16 * (1 + len(y.chunks)))
                nch = len(y.chunks)
                for half in range(2):
                    for c, (c0, n) in enumerate(y.chunks):
                        m = half * nch + c
                        if m >= 2:
                            pe.wait_ge(f["up_free"], m - 1)
                        for g in range(2):
                            for cc in range(CC):
                                last = M.matmul(bank[2 * (m % 2) + g][0:n, :], sh_in[:, cc, g * y.shared + c0:g * y.shared + c0 + n],
                                                xnT[:, cc, half * 512:half * 512 + 512], start=(cc == 0), stop=(cc == CC - 1))
                        last.then_inc(f["up_full"], 1)
                        if half == 0 and c == 1:
                            positions()
                    pe.wait_ge(f["up_free"], (half + 1) * nch)
                    for i in range(NT // 2):
                        t = half * (NT // 2) + i
                        if t >= 2:
                            pe.wait_ge(f["sh_free"], t - 1)
                        for c, (c0, n) in enumerate(y.chunks):
                            last = M.matmul(bank[4 + t % 2][:, 0:D], sh_h[0:n, c, i * P:(i + 1) * P], sh_out[0:n, c, :],
                                            start=(c == 0), stop=(c == nch - 1))
                        last.then_inc(f["sh_full"], 1)
                pe.wait_ge(f["sh_free"], NT)

                def turn(i, u, rnd, first):
                    if u % 2 == 0:
                        pe.wait_ge(f[f"ld_x{u // 2}"], 16 * rnd + 16)
                    if not first:
                        pe.wait_ge(f["xT2_ev"], i - 1)
                    for c in range(CC):
                        last = M.transpose(bank[u % 2][:, c * P:(c + 1) * P], xg[:, u, c * P:(c + 1) * P], ident[:])
                    last.then_inc(f["xT2_full"], 1)

                def up(i, u, rnd, first):
                    if u % 2 == 0:
                        pe.wait_ge(f[f"ld_w13_{u // 2}"], 32 * rnd + 32)
                    pe.wait_ge(f["xT2_ev"], i + 1)
                    if not first:
                        pe.wait_ge(f["e_mul"], i - 1)
                    for c in range(CC):
                        last = M.matmul(bank[2 + u % 2][:, 0:2 * I_EXP], xgT[:, u, c, :], w13[:, u, c, :], start=(c == 0), stop=(c == CC - 1))
                    last.then_inc(f["e_up_full"], 1)

                def turn_h(i, u, first):
                    pe.wait_ge(f["e_mul"], i + 1)
                    if not first:
                        pe.wait_ge(f["hT_ev"], i - 1)
                    for c in range(2):
                        last = M.transpose(bank[4 + u % 2][0:IC, c * P:(c + 1) * P], e_h[:, u % 2, c * IC:(c + 1) * IC], ident[:])
                    last.then_inc(f["hT_full"], 1)

                def down(i, u, rnd, first):
                    if u % 2 == 0:
                        pe.wait_ge(f[f"ld_w2_{u // 2}"], 32 * rnd + 32)
                    pe.wait_ge(f["hT_ev"], i + 1)
                    if not first:
                        pe.wait_ge(f["y_ev"], i - 1)
                    for c in range(2):
                        last = M.matmul(bank[6 + u % 2][:, 0:D], e_hT[:, u % 2, c, :], w2[:, u, c, :], start=(c == 0), stop=(c == 1))
                    last.then_inc(f["y_full"], 1)

                for i in range(3):
                    turn(i, i, 0, i < 2)
                up(0, 0, 0, True)
                turn_h(0, 0, True)
                last_t = y.main - 1

                def one(t, u, rnd, more, turns, first):
                    if more:
                        up(t + 1, (u + 1) % NB, rnd + (u + 1) // NB, first and t + 1 < 2)
                    down(t, u, rnd, first and t < 2)
                    if turns:
                        turn(t + 3, (u + 3) % NB, rnd + (u + 3) // NB, False)
                    if more:
                        turn_h(t + 1, (u + 1) % NB, first and t + 1 < 2)

                for t in range(NB):
                    one(t, t, 0, True, True, True)
                with pe.Fori(1, y.main // NB - 1) as it:
                    for u in range(NB):
                        one(it * NB + u, u, it, True, True, False)
                for t in range(y.main - NB, y.main):
                    one(t, t % NB, t // NB, t + 1 <= last_t, t + 3 <= last_t, False)
                if y.extra:
                    pe.wait_ge(f["plan_ready"], 1)
                    pe.wait_ge(f["y_ev"], y.main)
                    n = pe.value_load(nextra[0:1, 0:1], min_val=0, max_val=y.extra)
                    with pe.If(n > 0):
                        with pe.Fori(0, y.extra) as v:
                            with pe.If(n > v):
                                pe.wait_ge(f["ox_ld"], v * 48 + 48)
                                for c in range(CC):
                                    last = M.transpose(bank[0][:, c * P:(c + 1) * P], xg[:, 0, c * P:(c + 1) * P], ident[:])
                                last.then_inc(f["o_tfull"], 1)
                                pe.wait_ge(f["o_tev"], v + 1)
                                for c in range(CC):
                                    last = M.matmul(bank[2][:, 0:2 * I_EXP], xgT[:, 0, c, :], w13[:, 0, c, :], start=(c == 0), stop=(c == CC - 1))
                                last.then_inc(f["o_up"], 1)
                                pe.wait_ge(f["o_mul"], v + 1)
                                for c in range(2):
                                    last = M.transpose(bank[4][0:IC, c * P:(c + 1) * P], e_h[:, 0, c * IC:(c + 1) * IC], ident[:])
                                last.then_inc(f["o_hfull"], 1)
                                pe.wait_ge(f["o_hev"], v + 1)
                                for c in range(2):
                                    last = M.matmul(bank[6][:, 0:D], e_hT[:, 0, c, :], w2[:, 0, c, :], start=(c == 0), stop=(c == 1))
                                last.then_inc(f["o_y"], 1)

            ffn(L0)
            ffn(L1)


def layout(i):
    import numpy as np
    a = {k: np.asarray(v) for k, v in i.items()}
    c = np.ascontiguousarray

    def chunked(w, p=P):
        *lead, r, n = w.shape
        return c(np.moveaxis(w.reshape(*lead, r // p, p, n), -3, -2))

    t = {
        "x": a["x"].reshape(TOK, D),
        "ctxT": chunked(a["ctx_2048"].transpose(0, 2, 1)),
        "mask": a["mask_BxSxS2_ff0"].reshape(NT, P, L),
        "w_qo": np.stack([a["L0_xattn_wq"], a["L0_xattn_wo"]]),
        "w_kv": np.stack([a["L0_xattn_wk"].T, a["L0_xattn_wv"].T, a["L1_xattn_W_in"].T, a["L1_xattn_W_out"].T]),
        "rows": np.stack([a["L0_xattn_bq"], a["L0_xattn_bv"], a["L0_xattn_bo"], a["L1_xattn_b_out"], a["L1_xattn_gamma"],
                          a["L1_xattn_beta"]]),
        "scalars": np.concatenate([a["g_xattn"], a["g_ffn"], a["L1_xattn_decay"].reshape(1), a["L1_ffn_router_bias"]]),
        "colb": np.stack([a["L0_xattn_bk"].reshape(CC, P).T, a["L1_xattn_b_in"].reshape(CC, P).T], axis=1),
        "gate0": chunked(np.concatenate([a["L0_ffn_gate_w"], a["L0_ffn_shared_gate_w"]]).T),
        "gate1": chunked(a["L1_ffn_gate_w"].T),
        "sh_in0": chunked(a["L0_ffn_se_gate_up_w"].T),
        "sh_out0": a["L0_ffn_se_down_w"].T,
        "sh_in1": chunked(np.concatenate([a["L1_ffn_sw1"], a["L1_ffn_sw3"]]).T),
        "sh_out1": a["L1_ffn_sw2"].T,
        "w13_0": chunked(a["L0_ffn_w13"].transpose(0, 2, 1)),
        "w2_0": chunked(a["L0_ffn_w2"].transpose(0, 2, 1), IC),
        "w13_1": chunked(np.concatenate([a["L1_ffn_W1"], a["L1_ffn_W3"]], axis=2)),
        "w2_1": chunked(a["L1_ffn_W2"], IC),
    }
    return {k: c(v) for k, v in t.items()}


def kernel(**inputs):
    import numpy as np
    import concourse.bacc as bacc
    from concourse.bass_utils import run_bass_kernel_spmd

    nc = bacc.Bacc("TRN2", target_bir_lowering=False, num_devices=1)
    arrays = {f"in_{k}": v for k, v in layout(inputs).items()}
    T = {k[3:]: nc.dram_tensor(k, v.shape, mybir.dt.from_np(v.dtype), kind="ExternalInput").ap() for k, v in arrays.items()}
    out = nc.dram_tensor("out", (TOK, D), F32, kind="ExternalOutput").ap()
    build(nc, T, out)
    r = run_bass_kernel_spmd(nc, [arrays], core_ids=[0])
    return np.asarray(r.results[0]["out"]).reshape(B, S, D)
```

```python
from contextlib import ExitStack

import concourse.bass as bass
from concourse import mybir

P = 128
F32 = mybir.dt.float32
BF16 = mybir.dt.bfloat16
I32 = mybir.dt.int32
U32 = mybir.dt.uint32
ALU = mybir.AluOpType
ACT = mybir.ActivationFunctionType
AX = mybir.AxisListType

B, S, D = 4, 256, 256
L = 512
H, DH = 16, 16
TOK = B * S
NT = TOK // P
CC = D // P
LT = L // P
QT = S // P
HT = NT // 2
MIX = ((0, QT), (QT, HT), (HT, NT))
LN_EPS = 1e-5
Q_EPS = 1e-8
MAGIC = 12582912.0
BIG = 3.0e38
I_EXP = 176
IC = I_EXP // 2


NB = 6
PAIRS = NB // 2


class Layer:

    def __init__(self, n, experts, top, shared, own_tiles):
        self.n, self.E, self.K, self.shared = n, experts, top, shared
        self.own = own_tiles
        rounds = -(-((TOK * top - experts) // P + experts) // NB)
        self.main = experts if own_tiles else (rounds - 1) * NB
        self.last_round = 0 if own_tiles else NB
        self.extra = (TOK * top - experts) // P if own_tiles else 0
        self.x_tiles = -(-(self.main + self.last_round + self.extra) // B) * B
        self.y_spare = -(-(self.last_round + self.extra) // B) * B
        self.w_inc = 16 if own_tiles else 32
        self.chunks = [(c, min(P, shared - c)) for c in range(0, shared, P)]
        self.late = {0: (4, 5), 2: (6,), 3: (7,)} if shared > 512 else {0: (4, 5, 6, 7)}
        self.late = [self.late.get(i, ()) for i in range(TOK // P)]


L0 = Layer(0, 60, 4, 704, 1)
L1 = Layer(1, 8, 2, 352, 0)
LAYERS = (L0, L1)
ROWS = ("bq", "bv", "bo", "b_out", "gamma", "beta")
NSC = 2 + 2 + 1 + L1.E


class Steps:

    def __init__(self, engine, sem, base=0):
        self.engine, self.sem, self.base, self.n = engine, sem, base, 0

    def add(self, instruction, by=1):
        instruction.then_inc(self.sem, by)
        self.n += by

    def wait(self):
        self.engine.wait_ge(self.sem, self.base + self.n)

    def done(self, instruction):
        self.add(instruction)
        self.wait()


def build(nc, T, out):
    with ExitStack() as ctx:
        def sb(name, shape, dt=F32):
            return ctx.enter_context(nc.sbuf_tensor(name, shape, dt))

        def sem(name):
            return ctx.enter_context(nc.semaphore(name))

        bank = [ctx.enter_context(nc.psum_tensor(f"bank{i}", [P, 512], F32)) for i in range(8)]

        xg_dram = [nc.dram_tensor(f"sorted_x{y.n}", [y.x_tiles * P, D], F32).ap() for y in LAYERS]
        y_dram = [nc.dram_tensor(f"expert_y{y.n}", [(y.main + y.y_spare) * P, D], F32).ap() for y in LAYERS]

        stage = sb("stage", [P, 27424])
        at = [0]

        def part(shape):
            n = 1
            for m in shape:
                n *= m
            names = "abcd"[:len(shape)]
            v = stage[:, at[0]:at[0] + n].rearrange(f"p ({' '.join(names)}) -> p {' '.join(names)}", **dict(zip(names, shape)))
            at[0] += n
            assert at[0] <= stage.shape[1]
            return v

        x_sb = sb("x_sb", [P, NT, D])
        xn = sb("xn", [P, NT, D])
        tmp = sb("tmp", [P, NT, D])
        q_src = part([2 * QT, D])
        codes = sb("codes", [P, 2 * QT, D], BF16)
        codesT = sb("codesT", [P, CC, 2 * QT, P], BF16)
        st = sb("st", [P, NT, 6])
        mv = sb("mv", [P, NT, 2])
        rstd = sb("rstd", [P, NT])
        vare = sb("vare", [P, NT])
        mhalf = sb("mhalf", [P, NT])
        sx = sb("sx", [P, 2 * QT])
        sx4 = sb("sx4", [P, QT])
        rsx = sb("rsx", [P, 2 * QT])
        rows = sb("rows", [P, len(ROWS), D])
        scal = sb("scal", [P, NSC])
        tg = sb("tg", [P, 4])
        colb = sb("colb", [P, 2, CC])
        ident = sb("ident", [P, P])
        identb = sb("identb", [P, P], BF16)
        ones = sb("ones", [P, P])
        onesb = sb("onesb", [P, P], BF16)
        before = sb("before", [P, P], BF16)
        zeros = sb("zeros", [P, D])
        w_q = part([2, CC, D])
        w_codes = sb("w_codes", [P, 2, CC, D], BF16)
        w_codesT = sb("w_codesT", [P, 2, CC, D], BF16)
        sw = sb("sw", [P, 4])
        rsw = sb("rsw", [P, 4])
        diag = part([4, P])
        sw_rows = sb("sw_rows", [P, 2, D])
        w_kv = part([4, CC, D])
        ctxT = part([CC, L])
        mask = part([QT, L])
        q_split = part([QT, 2, D])
        q_tmp = sb("q_tmp", [P, QT, D])
        qT = part([2, CC, S])
        kT = part([CC, L])
        v_sb = part([LT, H, 32])
        z_sb = part([2, 4, L])
        pT = part([2, 4, LT, P])
        zmin = sb("zmin", [P, 2, 4])
        psum_row = sb("psum_row", [P, QT, 4, 4])
        rsum = sb("rsum", [P, QT, 4, 4])
        oT = sb("oT", [P, 4, P])
        krow = sb("krow", [P, 1])
        coef = part([L])
        csum = sb("csum", [P, 1])
        z_col = sb("z_col", [P, CC])
        zT = sb("zT", [P, CC, B])
        mT = sb("mT", [P, CC, B])
        bin_s = sb("bin_s", [P, CC])
        mTb = part([CC, B, P])
        summary = sb("summary", [P, B, D])
        at[0] = 0
        xnT = sb("xnT", [P, CC, TOK])
        gate_w = [sb(f"gate_w{y.n}", [P, CC, y.E + 1 - y.n]) for y in LAYERS]
        NSH = len(L0.chunks)
        sh_in = sb("sh_in", [P, CC, 2 * L0.shared])
        sh_out = sb("sh_out", [P, NSH, D])
        sh_act = part([2, 512])
        sh_up = part([2, 512])
        sh_h = part([NSH, 512])
        sh_y = part([HT, D])
        EM, KM = L0.E, L0.K
        logits = part([NT, 64])
        probs = sb("probs", [P, NT, EM])
        picks = part([NT, EM])
        rmax = sb("rmax", [P, NT])
        rsm = sb("rsm", [P, NT])
        sh_gate = sb("sh_gate", [P, NT])
        sh_gate_x = sb("sh_gate_x", [P, NT])
        top8 = sb("top8", [P, NT, 8])
        idx8 = sb("idx8", [P, NT, 8], U32)
        idxf = sb("idxf", [P, NT, 8])
        hot = part([NT, KM, EM])
        hot2 = part([NT, KM, EM])
        member = sb("member", [P, NT, EM], BF16)
        iota_e = sb("iota_e", [P, EM])
        iota_v = sb("iota_v", [P, 32])
        cnt = sb("cnt", [P, EM])
        ntile = sb("ntile", [P, EM])
        incl = sb("incl", [P, EM])
        base = sb("base", [P, EM])
        over = sb("over", [P, EM])
        pos = part([NT, EM])
        posb = part([NT, EM])
        slotf = sb("slotf", [P, NT, KM])
        slot = sb("slot", [P, NT, KM], U32)
        wts = sb("wts", [P, NT, KM])
        owner_c = hot2.rearrange("p t k e -> p (t k) e")[0:1]
        owner_f = sb("owner_f", [1, 32])
        owner = sb("owner", [1, 32], I32)
        nextra = sb("nextra", [1, 2], I32)
        xg = part([NB, D])
        xgT = part([NB, CC, P])
        w13 = part([NB, CC, 2 * I_EXP])
        w2 = part([NB, 2, D])[0:IC]
        e_act = sb("e_act", [P, 2, I_EXP])
        e_h = sb("e_h", [P, 2, I_EXP])
        e_hT = sb("e_hT", [IC, 2, 2, P])
        e_y = part([4, D])
        NG = 4
        yk = part([NG, D])
        assert L0.K * NT * P <= NB * CC * 2 * I_EXP
        diag_w = w13.rearrange("p e c n -> p (e c n)")[:, 0:L0.K * NT * P].rearrange("p (i n) -> p i n", n=P)
        sdev = sb("sdev", [P, HT])
        newton = sb("newton", [P, HT])
        shift = sb("shift", [P, HT])

        FULL = (4, 6)
        ld_x0, ld_x, ld_small, ld_wqo, ld_wkv, ld_ctx = map(sem, ("ld_x0", "ld_x", "ld_small", "ld_wqo", "ld_wkv", "ld_ctx"))
        ld_mask = [sem("ld_mask0"), sem("ld_mask1")]
        zero_tile, zeroed = sem("zero_tile"), [sem("zeroed0"), sem("zeroed1")]
        pool_step, dve_step, act_step = sem("pool_step"), sem("dve_step"), sem("act_step")
        consts = sem("consts")
        var_ready, rstd_ready = sem("var_ready"), sem("rstd_ready")
        coded, code_t, code_ev = sem("coded"), sem("code_t"), sem("code_ev")
        q_ready, ctx_seen = sem("q_ready"), sem("ctx_seen")
        scales_ready, x_updated, pool_loop = sem("scales_ready"), sem("x_updated"), sem("pool_loop")
        diag_ready, sw_full, setup_done = sem("diag_ready"), sem("sw_full"), sem("setup_done")
        var_act, sdev_ready, shift_ready, applied = sem("var_act"), sem("sdev_ready"), sem("shift_ready"), sem("applied")
        seq_pe, seq_dve = sem("seq_pe"), sem("seq_dve")
        gates_ready = sem("gates_ready")
        dve_loop = sem("dve_loop")
        work_full = [sem("work_full0"), sem("work_full1")]
        work_free = [sem("work_free0"), sem("work_free1")]
        score_full, scored, expd = sem("score_full"), sem("scored"), sem("expd")
        t_full, t_free = sem("t_full"), [sem("t_free0"), sem("t_free1")]
        av_done = sem("av_done")
        passed = sem("passed")
        oproj_full, oproj_free = sem("oproj_full"), sem("oproj_free")
        fs = []
        for y in LAYERS:
            fs.append({k: sem(f"{k}{y.n}") for k in (
                "ld_sh", "ld_gate", "x_ready", "xT_full", "xT_ev", "log_full", "log_ev", "r_act", "mem_ready", "pos_full",
                "slots_ready", "plan_ready", "scattered", "up_full", "up_act", "up_free", "h_made", "sh_full", "sh_free",
                "xT2_full", "xT2_ev", "e_up_full", "e_silu", "e_mul", "hT_full", "hT_ev", "y_full", "y_ev",
                "ox_ld", "o_tfull", "o_tev", "o_up", "o_silu", "o_mul", "o_hfull", "o_hev", "o_y", "o_yev", "o_st", "extra_done",
                "shared_added", "diagonal", "gathered", "combined") if y.extra or k[0:2] not in ("o_", "ox")})
            for i in range(PAIRS):
                for k in ("ld_x", "ld_w13_", "ld_w2_"):
                    fs[-1][f"{k}{i}"] = sem(f"{k}{i}_{y.n}")
            for i in range(2):
                fs[-1][f"y_st{i}"] = sem(f"y_st{i}_{y.n}")
        got = [sem(f"got{i}") for i in range(NG)]
        stored = sem("stored")

        block = ctx.enter_context(nc.Block())
        R = {n: rows[:, i, :] for i, n in enumerate(ROWS)}

        def bc(ap, axis, n):
            v = ap.unsqueeze(axis)
            shape = list(v.shape)
            shape[axis] = n
            return v.to_broadcast(shape)

        def stores(pairs, q):
            return (pairs + 1 - q) // 2

        def head(g, j):
            cc, par = divmod(g, 2)
            return cc, par, cc * 8 + 2 * j + par

        @block.sync
        def _(sp):
            def load_x_tiles(a, b, signal):
                sp.dma_start(x_sb[:, a:b, :], T["x"][a * P:b * P, :].rearrange("(t p) d -> p t d", p=P)).then_inc(signal, 16)

            def load_ctx(b):
                sp.dma_start(ctxT[:], T["ctxT"][bass.ds(b, 1)].rearrange("o p c l -> p (o c) l")).then_inc(ld_ctx, 16)

            def load_mask(b, nt):
                sp.dma_start(mask[:, nt, :], T["mask"][bass.ds(b * QT + nt, 1)].rearrange("o p l -> p (o l)")).then_inc(ld_mask[nt], 16)

            def shared_weights(y):
                f = fs[y.n]
                sp.dma_start(sh_in[:, :, 0:2 * y.shared], T[f"sh_in{y.n}"]).then_inc(f["ld_sh"], 16)
                for c, (c0, n) in enumerate(y.chunks):
                    sp.dma_start(sh_out[0:n, c, :], T[f"sh_out{y.n}"][c0:c0 + n, :]).then_inc(f["ld_sh"], 16)

            def zero_quarter(b):
                for y in LAYERS:
                    for d, n in ((xg_dram[y.n], y.x_tiles // B), (y_dram[y.n][y.main * P:, :], y.y_spare // B)):
                        sp.dma_start(d.rearrange("(p a) d -> p a d", p=P)[:, bass.ds(b * n, n), :],
                                     bc(zeros[:], 1, n)).then_inc(zeroed[y.n], 16)

            load_x_tiles(0, QT, ld_x0)
            sp.dma_start(w_q[:], T["w_qo"].rearrange("w (c p) d -> p w c d", p=P)).then_inc(ld_wqo, 16)
            sp.dma_start(rows[:], T["rows"].rearrange("(o r) d -> o r d", o=1).to_broadcast([P, len(ROWS), D])).then_inc(ld_small, 16)
            sp.dma_start(scal[:], T["scalars"].rearrange("(o r) -> o r", o=1).to_broadcast([P, NSC])).then_inc(ld_small, 16)
            sp.dma_start(colb[:], T["colb"]).then_inc(ld_small, 16)
            load_ctx(0)
            sp.dma_start(w_kv[:], T["w_kv"].rearrange("w (c p) d -> p w c d", p=P)).then_inc(ld_wkv, 16)
            load_mask(0, 0)
            load_x_tiles(QT, NT, ld_x)
            load_mask(0, 1)
            sp.wait_ge(zero_tile, 1)
            zero_quarter(0)
            with sp.Fori(0, B - 1) as b:
                sp.wait_ge(work_full[1], b * 6 + 4)
                sp.sem_inc(passed, 1)
                sp.wait_ge(ctx_seen, b + 1)
                load_ctx(b + 1)
                for nt in range(QT):
                    sp.wait_ge(scored, b * (QT * 16) + (nt + 1) * 16)
                    load_mask(b + 1, nt)
                    if nt == 0:
                        zero_quarter(b + 1)
            for y in LAYERS:
                sp.dma_start(gate_w[y.n][:], T[f"gate{y.n}"]).then_inc(fs[y.n]["ld_gate"], 16)
            shared_weights(L0)
            def experts(y):
                f = fs[y.n]
                wi, wo = T[f"w13_{y.n}"], T[f"w2_{y.n}"]

                def owners(p):
                    return [sp.value_load(owner[0:1, bass.ds(p * 2 + h, 1)], min_val=0, max_val=y.E - 1) for h in range(2)]

                def load_w(dst, src, p, s, key, own):
                    if y.own:
                        sp.dma_start(dst[:, 2 * s:2 * s + 2].rearrange("p e c n -> p e (c n)"),
                                     src[bass.ds(p * 2, 2)].rearrange("e p c n -> p e (c n)")).then_inc(f[f"{key}{s}"], 16)
                    else:
                        for h in range(2):
                            sp.dma_start(dst[:, 2 * s + h], src[bass.ds(own[h], 1)].rearrange("o p c n -> p (o c) n"))\
                              .then_inc(f[f"{key}{s}"], 16)

                def load_x(p, s):
                    sp.dma_start(xg[:, 2 * s:2 * s + 2, :],
                                 xg_dram[y.n][bass.ds(p * 2 * P, 2 * P), :].rearrange("(h p) d -> p h d", p=P)).then_inc(f[f"ld_x{s}"], 16)

                pairs = y.main // 2
                if y.own:
                    sp.wait_ge(f["xT_full"], B)
                else:
                    sp.wait_ge(f["plan_ready"], 1)
                for p in range(PAIRS):
                    own = None if y.own else owners(p)
                    load_w(w13, wi, p, p, "ld_w13_", own)
                    load_w(w2, wo, p, p, "ld_w2_", own)
                sp.wait_ge(f["scattered"], 16 * NT * y.K)
                for p in range(PAIRS):
                    load_x(p, p)
                sp.wait_ge(f["xT2_full"], 2)
                load_x(PAIRS, 0)

                def pair(p, s, whole, more_x):
                    own = None
                    if whole:
                        if not y.own:
                            own = owners(p + PAIRS)
                        sp.wait_ge(f["e_up_full"], p * 2 + 2)
                        load_w(w13, wi, p + PAIRS, s, "ld_w13_", own)
                    if more_x:
                        sp.wait_ge(f["xT2_full"], p * 2 + 4)
                        load_x(p + PAIRS + 1, (s + 1) % PAIRS)
                    if whole:
                        sp.wait_ge(f["y_full"], p * 2 + 2)
                        load_w(w2, wo, p + PAIRS, s, "ld_w2_", own)

                def store(p, q):
                    sp.wait_ge(f["y_ev"], p * 2 + 2)
                    sp.dma_start(y_dram[y.n][bass.ds(p * 2 * P, 2 * P), :].rearrange("(h p) d -> p h d", p=P),
                                 e_y[:, 2 * q:2 * q + 2, :]).then_inc(f[f"y_st{q}"], 16)

                turns = (pairs - PAIRS - 1) // (2 * PAIRS)
                if turns:
                    with sp.Fori(0, turns) as it:
                        for u in range(2 * PAIRS):
                            pair(it * (2 * PAIRS) + u, u % PAIRS, True, True)
                            store(it * (2 * PAIRS) + u, u % 2)
                for p in range(turns * 2 * PAIRS, pairs):
                    pair(p, p % PAIRS, p + PAIRS < pairs, p + PAIRS + 1 < pairs)
                    store(p, p % 2)
                if y.last_round:
                    n = sp.value_load(nextra[0:1, 0:1], min_val=0, max_val=y.main + y.last_round)
                    with sp.If(n > y.main):
                        sp.wait_ge(f["y_full"], y.main)
                        for s in range(PAIRS):
                            own = owners(pairs + s)
                            load_x(pairs + s, s)
                            load_w(w13, wi, pairs + s, s, "ld_w13_", own)
                            load_w(w2, wo, pairs + s, s, "ld_w2_", own)
                        for p in range(pairs, pairs + PAIRS):
                            store(p, p % 2)
                        for q in range(2):
                            sp.wait_ge(f[f"y_st{q}"], 16 * stores(pairs + PAIRS, q))
                if y.extra:
                    n = sp.value_load(nextra[0:1, 0:1], min_val=0, max_val=y.extra)
                    for q in range(2):
                        sp.wait_ge(f[f"y_st{q}"], 16 * stores(pairs, q))
                    with sp.If(n > 0):
                        with sp.Fori(0, y.extra) as v:
                            with sp.If(n > v):
                                e = sp.value_load(owner[0:1, bass.ds(v, 1)], min_val=0, max_val=y.E - 1)
                                sp.dma_start(w13[:, 0], wi[bass.ds(e, 1)].rearrange("o p c n -> p (o c) n")).then_inc(f["ox_ld"], 16)
                                sp.dma_start(w2[:, 0], wo[bass.ds(e, 1)].rearrange("o p c n -> p (o c) n")).then_inc(f["ox_ld"], 16)
                                sp.dma_start(xg[:, 0, :], xg_dram[y.n][bass.ds((v + y.main) * P, P), :]).then_inc(f["ox_ld"], 16)
                                sp.wait_ge(f["o_yev"], v + 1)
                                sp.dma_start(y_dram[y.n][bass.ds((v + y.main) * P, P), :], e_y[:, 0, :]).then_inc(f["o_st"], 16)
                                sp.wait_ge(f["o_st"], v * 16 + 16)
                                sp.sem_inc(passed, 1)
                sp.sem_inc(f["extra_done"], 1)

            experts(L0)
            sp.wait_ge(fs[0]["sh_full"], NT)
            shared_weights(L1)
            experts(L1)
            for q in range(B):
                sp.wait_ge(fs[1]["combined"], (q + 1) * QT)
                sp.dma_start(out[q * S:(q + 1) * S, :].rearrange("(t p) d -> p t d", p=P), x_sb[:, q * QT:(q + 1) * QT, :]).then_inc(stored, 16)
            sp.wait_ge(stored, 16 * B)

        @block.gpsimd
        def _(gp):
            step = Steps(gp, pool_step)
            step.done(gp.memset(zeros[:], 0.0))
            gp.sem_inc(zero_tile, 1)
            step.done(gp.memset(ident[:], 0.0))
            step.done(gp.affine_select(out=ident[:], in_=ident[:], compare_op=ALU.not_equal, fill=1.0, base=0,
                                       pattern=[[-1, P]], channel_multiplier=1))
            step.add(gp.tensor_copy(identb[:], ident[:]))
            step.done(gp.memset(ones[:], 1.0))
            step.add(gp.tensor_copy(onesb[:], ones[:]))
            step.add(gp.affine_select(out=before[:], in_=ones[:], compare_op=ALU.is_gt, fill=0.0, base=0,
                                      pattern=[[1, P]], channel_multiplier=-1))
            step.add(gp.iota(iota_e[:], pattern=[[1, EM]], base=0, channel_multiplier=0, allow_small_or_imprecise_dtypes=True))
            step.add(gp.iota(iota_v[:], pattern=[[1, 32]], base=0, channel_multiplier=0, allow_small_or_imprecise_dtypes=True))
            step.done(gp.memset(mhalf[:], -0.5))
            gp.sem_inc(consts, 1)

            def power(n, tiles):
                gp.wait_ge(var_ready, n)
                gp.tensor_tensor(rstd[:, 0:tiles], vare[:, 0:tiles], mhalf[:, 0:tiles], ALU.pow).then_inc(rstd_ready, 1)

            def dispatch(y):
                f = fs[y.n]
                for c, (c0, n) in enumerate(y.chunks):
                    gp.wait_ge(f["up_act"], c + 1)
                    gp.wait_ge(f["up_free"], c + 1)
                    gp.tensor_tensor(sh_h[0:n, c, :], sh_act[0:n, c % 2, :], sh_up[0:n, c % 2, :], ALU.mult).then_inc(f["h_made"], 1)
                gp.wait_ge(f["slots_ready"], 1)
                gp.wait_ge(zeroed[y.n], 2 * B * 16)
                for i in range(NT):
                    for k in range(y.K):
                        gp.indirect_dma_start(out=xg_dram[y.n][:, :], out_offset=bass.IndirectOffsetOnAxis(slot[:, i, k:k + 1], 0),
                                              in_=xn[:, i, :], in_offset=None).then_inc(f["scattered"], 16)

            def collect(y):
                f = fs[y.n]
                gp.wait_ge(f["sh_free"], HT)
                step.done(gp.tensor_scalar(sh_y[:], sh_y[:], tg[:, 2 + y.n:3 + y.n], None, ALU.mult))
                gp.tensor_tensor(x_sb[:, 0:HT, :], x_sb[:, 0:HT, :], sh_y[:], ALU.add).then_inc(f["shared_added"], 1)
                for q in range(2):
                    gp.wait_ge(f[f"y_st{q}"], 16 * stores(y.main // 2, q))
                gp.wait_ge(f["extra_done"], 1)
                for i in range(NT):
                    for k in range(y.K):
                        n = i * y.K + k
                        if n >= NG:
                            gp.wait_ge(f["gathered"], n - NG + 1)
                        gp.indirect_dma_start(out=yk[:, n % NG, :], out_offset=None, in_=y_dram[y.n][:, :],
                                              in_offset=bass.IndirectOffsetOnAxis(slot[:, i, k:k + 1], 0)).then_inc(got[n % NG], 16)

            FIRST_STEPS, MID_STEPS = 8, 18

            def batch(b, pre, post, base_steps):
                ls = Steps(gp, pool_loop, base_steps)
                lo, hi = (0 if pre else QT), (2 * QT if post else QT)

                def done(instruction):
                    ls.done(instruction)
                    gp.sem_inc(passed, 1)

                def normalise(buf, count):
                    gp.wait_ge(var_ready, count)
                    gp.sem_inc(passed, 1)
                    done(gp.tensor_tensor(rstd[:, 0:QT], vare[:, 0:QT], mhalf[:, 0:QT], ALU.pow))
                    for i in range(QT):
                        ls.add(gp.tensor_scalar(buf[:, i, :], buf[:, i, :], mv[:, i, 0:1], rstd[:, i:i + 1], ALU.subtract, ALU.mult))
                    ls.wait()
                    gp.sem_inc(passed, 1)

                if pre:
                    done(gp.tensor_copy(q_src[:, 0:QT, :], x_sb[:, bass.ds((b + 1) * QT, QT), :]))
                    normalise(q_src[:, 0:QT, :], b * 2 + 1 if post else 2)
                    gp.sem_inc(rstd_ready, 1)
                gp.wait_ge(scales_ready, b + 1)
                gp.sem_inc(passed, 1)
                for i in range(lo, hi):
                    ls.add(gp.tensor_scalar(tmp[:, i, :], q_src[:, i, :], rsx[:, i:i + 1], MAGIC, ALU.mult, ALU.add))
                ls.wait()
                gp.sem_inc(passed, 1)
                done(gp.tensor_scalar(tmp[:, lo:hi, :], tmp[:, lo:hi, :], MAGIC, 127.0, ALU.subtract, ALU.min))
                done(gp.tensor_scalar(codes[:, lo:hi, :], tmp[:, lo:hi, :], -127.0, None, ALU.max))
                gp.sem_inc(coded, 1)
                if post:
                    y = tmp[:, 4:4 + QT, :]
                    xq, xnq = (v[:, bass.ds((b - 1) * QT, QT), :] for v in (x_sb, xn))
                    gp.wait_ge(oproj_free, b)
                    gp.sem_inc(passed, 1)
                    done(gp.tensor_tensor(y, y, bc(R["bo"], 1, QT), ALU.add))
                    done(gp.tensor_scalar(y, y, tg[:, 0:1], None, ALU.mult))
                    done(gp.tensor_tensor(y, y, xq, ALU.add))
                    gp.sem_inc(x_updated, 1)
                    done(gp.tensor_copy(xq, y))
                    normalise(y, b * 2 + (2 if pre else 1))
                    done(gp.tensor_copy(xnq, y))
                    gp.sem_inc(rstd_ready, 1)
                    gp.sem_inc(fs[0]["x_ready"], 1)
                return ls.n

            power(1, QT)
            step.add(gp.memset(q_split[:], 0.0))
            step.done(gp.memset(v_sb[:], 0.0))
            gp.sem_inc(consts, 1)
            gp.wait_ge(coded, 1)
            gp.wait_ge(ld_x, 16)
            gp.wait_ge(gates_ready, 1)
            n = batch(0, True, False, 0)
            assert n == FIRST_STEPS, n
            with gp.Fori(1, B - 1) as b:
                n = batch(b, True, True, (b - 1) * MID_STEPS + FIRST_STEPS)
                assert n == MID_STEPS, n
            batch(B - 1, False, True, (B - 2) * MID_STEPS + FIRST_STEPS)
            power(2 * B, QT)
            dispatch(L0)
            collect(L0)
            dispatch(L1)
            collect(L1)

        @block.vector
        def _(dve):
            step = Steps(dve, dve_step)
            V = nc.vector

            def moments(step, src, n):
                dve.sem_inc(passed, 1)
                for i in range(n):
                    step.add(V.bn_stats(st[:, i, :], src(i)))
                step.wait()
                dve.sem_inc(passed, 1)
                for i in range(n):
                    step.add(V.bn_aggr(mv[:, i, :], st[:, i, :]))
                step.wait()
                V.tensor_scalar(vare[:, 0:n], mv[:, 0:n, 1], LN_EPS, None, ALU.add).then_inc(var_ready, 1)

            def normalise(step, src, dst, n, count):
                dve.wait_ge(rstd_ready, count)
                for i in range(n):
                    step.add(V.tensor_scalar(dst(i), src(i), mv[:, i, 0:1], rstd[:, i:i + 1], ALU.subtract, ALU.mult))
                step.wait()

            def find_scales(step, src, scales, inverse):
                step.done(V.tensor_reduce(scales, src, AX.X, ALU.max, apply_absolute_value=True))
                step.done(V.tensor_scalar(scales, scales, 1.0 / 127.0, Q_EPS, ALU.mult, ALU.max))
                step.done(V.reciprocal(inverse, scales))

            def quantise(step, src, dst, inverse, n, scratch):
                for i in range(n):
                    step.add(V.tensor_scalar(scratch[:, i, :], src[:, i, :], inverse[:, i:i + 1], MAGIC, ALU.mult, ALU.add))
                step.wait()
                step.done(V.tensor_scalar(scratch, scratch, MAGIC, 127.0, ALU.subtract, ALU.min))
                step.done(V.tensor_scalar(dst, scratch, -127.0, None, ALU.max))
                dve.sem_inc(coded, 1)

            def quantise_slots(step, lo, hi):
                find_scales(step, q_src[:, lo:hi, :], sx[:, lo:hi], rsx[:, lo:hi])
                quantise(step, q_src[:, lo:hi, :], codes[:, lo:hi, :], rsx[:, lo:hi], hi - lo, tmp[:, lo:hi, :])
                if lo == 0:
                    step.done(V.tensor_scalar(sx4[:], sx[:, 0:QT], 0.25, None, ALU.mult))

            dve.wait_ge(ld_x0, 16)
            moments(step, lambda i: x_sb[:, i, :], QT)
            dve.wait_ge(ld_wqo, 16)
            wq3 = w_q[:].rearrange("p w c d -> p (w c) d")
            find_scales(step, wq3, sw[:], rsw[:])
            normalise(step, lambda i: x_sb[:, i, :], lambda i: q_src[:, i, :], QT, 1)
            quantise_slots(step, 0, QT)
            quantise(step, wq3, w_codes[:].rearrange("p w c d -> p (w c) d"), rsw[:], 4, tmp[:, 0:4, :])
            dve.wait_ge(consts, 1)
            for i in range(4):
                step.add(V.tensor_scalar(diag[:, i, :], ident[:], sw[:, i:i + 1], None, ALU.mult))
            step.wait()
            dve.sem_inc(diag_ready, 1)
            dve.wait_ge(ld_small, 48)
            step.done(V.tensor_scalar(R["bq"], R["bq"], 0.25, None, ALU.mult))

            def take_codes(n, w, lo, hi):
                dve.wait_ge(code_t, n)
                src = bank[w][:].bitcast(BF16)[:, 0:CC * (hi - lo) * P].rearrange("p (c t n) -> p c t n", c=CC, t=hi - lo)
                V.tensor_copy(codesT[:, :, lo:hi, :], src).then_inc(code_ev, 1)

            take_codes(1, 0, 0, QT)
            dve.wait_ge(code_t, 2)
            V.tensor_copy(w_codesT[:].rearrange("p w c d -> p (w c d)"), bank[2][:].bitcast(BF16)).then_inc(code_ev, 1)
            dve.wait_ge(sw_full, 1)
            step.done(V.tensor_copy(sw_rows[:].rearrange("p w d -> p (w d)"), bank[3][:]))
            dve.sem_inc(setup_done, 1)
            dve.wait_ge(consts, 2)

            SUBS = QT * 4
            FIRST_STEPS, MID_STEPS = 24, 25

            def batch(b, pre, post, base_steps):
                ls = Steps(dve, dve_loop, base_steps)
                lo, hi = (0 if pre else QT), (2 * QT if post else QT)
                x_next = lambda i: x_sb[:, bass.ds((b + 1) * QT + i, 1), :].rearrange("p o d -> p (o d)")

                for nt in range(QT):
                    dve.wait_ge(work_full[nt], b * FULL[nt] + 1)
                    q3 = V.scalar_tensor_tensor(out=q_tmp[:, nt, :], in0=bank[nt][:, 0:D], scalar=sx4[:, nt:nt + 1],
                                                in1=sw_rows[:, 0, :], op0=ALU.mult, op1=ALU.mult)
                    ls.done(q3)
                    dve.sem_inc(work_free[nt], 1)
                    for par in range(2):
                        v = lambda ap: ap.rearrange("p (h two d) -> p h two d", two=2, d=DH)[:, :, par, :]
                        V.tensor_tensor(v(q_split[:, nt, par, :]), v(q_tmp[:, nt, :]), v(R["bq"]), ALU.add).then_inc(q_ready, 1)

                def score(s):
                    nt, g = divmod(s, 4)
                    if g == 0:
                        dve.wait_ge(ld_mask[nt], b * 16 + 16)
                    for j in range(4):
                        dve.wait_ge(score_full, b * SUBS * 4 + s * 4 + j + 1)
                        dve.sem_inc(passed, 1)
                        V.tensor_tensor_reduce(out=z_sb[:, s % 2, j, :], in0=bank[j][:], in1=mask[:, nt, :], scale=-1.0,
                                               scalar=BIG, op0=ALU.add, op1=ALU.min,
                                               accum_out=zmin[:, s % 2, j:j + 1]).then_inc(scored, 1)
                        if j % 2 and s:
                            take(s - 1, j)
                    if s == 0:
                        values()

                def take(s, j):
                    dve.wait_ge(t_full, b * SUBS * 4 + s * 4 + j + 1)
                    V.tensor_copy(pT[:, s % 2, j].rearrange("p t n -> p (t n)"), bank[5][:]).then_inc(t_free[1], 1)

                def values():
                    for w in range(2):
                        dve.wait_ge(work_full[w], b * FULL[w] + 4)
                        V.tensor_tensor(v_sb[:, 2 * w:2 * w + 2, :, 0:DH],
                                        bank[6 + w][:].rearrange("p (t h d) -> p t h d", h=H, d=DH),
                                        bc(R["bv"].rearrange("p (h d) -> p h d", d=DH), 1, 2), ALU.add).then_inc(work_free[w], 1)

                def finish(nt):
                    dve.wait_ge(expd, b * SUBS * 4 + (nt + 1) * 16)
                    ls.done(V.reciprocal(rsum[:, nt], psum_row[:, nt]))
                    dve.wait_ge(work_full[1], b * 6 + 5 + nt)
                    for cc in range(CC):
                        src = bank[7][:].rearrange("p (g j d) -> p g j d", j=4, d=32)[:, 2 * cc:2 * cc + 2, :, 0:DH]
                        dst = q_src[:, QT + nt, :].rearrange("p (c j r d) -> p c r j d", c=CC, j=4, r=2)[:, cc]
                        ls.add(V.tensor_tensor(dst, src, bc(rsum[:, nt, 2 * cc:2 * cc + 2, :], 3, DH), ALU.mult))
                    ls.wait()
                    dve.sem_inc(work_free[1], 1)

                def decay_weights():
                    dve.wait_ge(gates_ready, 1)
                    ls.done(V.tensor_scalar(krow[:], krow[:], 1.0, None, ALU.add))
                    ls.done(V.reciprocal(krow[:], krow[:]))
                    ls.done(V.tensor_tensor_scan(coef[:, L - 1::-1], krow[:].to_broadcast([P, L]), ones[:, 0:1].to_broadcast([P, L]),
                                                 0.0, ALU.mult, ALU.add))
                    ls.done(V.tensor_reduce(csum[:], coef[:], AX.X, ALU.add))
                    ls.done(V.tensor_scalar(bin_s[:], colb[:, 1, :], csum[:], None, ALU.mult))

                def weigh_context():
                    scratch = tmp[:, 6:8, :].rearrange("p t d -> p (t d)")
                    for c in range(CC):
                        ls.done(V.tensor_tensor_reduce(out=scratch, in0=ctxT[:, c, :], in1=coef[:], scale=1.0, scalar=0.0,
                                                       op0=ALU.mult, op1=ALU.add, accum_out=z_col[:, c:c + 1]))
                    dve.sem_inc(ctx_seen, 1)
                    ls.done(V.tensor_copy(zT[:, :, bass.ds(b, 1)], z_col[:].unsqueeze(2)))

                def next_scales():
                    if pre:
                        dve.wait_ge(rstd_ready, b * 2 + 1 if post else 2)
                    find_scales(ls, q_src[:, lo:hi, :], sx[:, lo:hi], rsx[:, lo:hi])
                    if pre:
                        ls.done(V.tensor_scalar(sx4[:], sx[:, 0:QT], 0.25, None, ALU.mult))
                    dve.sem_inc(scales_ready, 1)

                for s in range(SUBS):
                    score(s)
                    if s == 0 and pre:
                        if post:
                            dve.wait_ge(rstd_ready, b * 2)
                        else:
                            dve.wait_ge(ld_x, 16)
                        moments(ls, x_next, QT)
                    if s == 1:
                        next_scales()
                    if s == 2:
                        if not post:
                            decay_weights()
                        weigh_context()
                    if s == 4:
                        take_codes(b + 3, 7, lo, hi)
                    if s == 5 and post:
                        take_output(ls, 4, b)
                    if s == 6:
                        finish(0)
                    if s == 7 and post:
                        dve.wait_ge(x_updated, b)
                        moments(ls, lambda i: tmp[:, 4 + i, :], QT)
                take(SUBS - 1, 1)
                take(SUBS - 1, 3)
                finish(1)
                return ls.n

            def take_output(step, at, count):
                dve.wait_ge(oproj_full, count)
                for i in range(QT):
                    step.add(V.scalar_tensor_tensor(out=tmp[:, at + i, :], in0=bank[7][:, i * D:(i + 1) * D], scalar=sx[:, QT + i:QT + i + 1],
                                                    in1=sw_rows[:, 1, :], op0=ALU.mult, op1=ALU.mult))
                step.wait()
                dve.sem_inc(oproj_free, 1)

            n = batch(0, True, False, 0)
            assert n == FIRST_STEPS, n
            with dve.Fori(1, B - 1) as b:
                n = batch(b, True, True, (b - 1) * MID_STEPS + FIRST_STEPS)
                assert n == MID_STEPS, n
            batch(B - 1, False, True, (B - 2) * MID_STEPS + FIRST_STEPS)

            quantise_slots(step, QT, 2 * QT)
            take_codes(B + 3, 7, QT, 2 * QT)
            dve.wait_ge(seq_pe, 1)
            step.done(V.tensor_tensor(mT[:], bank[4][:, 0:CC * B].rearrange("p (c b) -> p c b", c=CC), bc(bin_s[:], 2, B), ALU.add))
            step.done(V.tensor_scalar(mTb[:].rearrange("p c b n -> p (c b) n"), bc(mT[:].rearrange("p c b -> p (c b)"), 2, P),
                                      1.0 / L, None, ALU.mult))
            dve.sem_inc(seq_dve, 1)
            take_output(step, 0, B)
            step.done(V.tensor_tensor(tmp[:, 0:QT, :], tmp[:, 0:QT, :], bc(R["bo"], 1, QT), ALU.add))
            last_x = x_sb[:, NT - QT:NT, :]
            step.done(V.scalar_tensor_tensor(out=last_x, in0=tmp[:, 0:QT, :], scalar=tg[:, 0:1], in1=last_x, op0=ALU.mult, op1=ALU.add))
            dve.wait_ge(rstd_ready, 2 * B - 1)
            moments(step, lambda i: x_sb[:, NT - QT + i, :], QT)
            normalise(step, lambda i: x_sb[:, NT - QT + i, :], lambda i: xn[:, NT - QT + i, :], QT, 2 * B)
            dve.sem_inc(fs[0]["x_ready"], 1)
            dve.wait_ge(fs[0]["xT_full"], B)
            V.tensor_copy(xnT[:, :, (B - 1) * S:B * S], bank[7][:].rearrange("p (c n) -> p c n", c=CC)).then_inc(fs[0]["xT_ev"], 1)
            dve.wait_ge(seq_pe, 2)
            for h in range(2):
                step.add(V.tensor_tensor(summary[:, 2 * h:2 * h + 2, :], bank[4 + h][:].rearrange("p (b d) -> p b d", b=2),
                                         bc(R["b_out"], 1, 2), ALU.add))
            step.wait()
            dve.sem_inc(seq_dve, 1)

            def route(y):
                f, E, K = fs[y.n], y.E, y.K
                lg = logits[:, :, 0:E]
                pr, pk = probs[:, :, 0:E], picks[:, :, 0:E]
                dve.wait_ge(f["log_full"], 2 if y.n else 1)
                ng = gate_w[y.n].shape[2]
                step.done(V.tensor_copy(logits[:, :, 0:ng], bank[6][:].rearrange("p (t e) -> p t e", t=NT)[:, :, 0:ng]))
                if y.n == 0:
                    step.done(V.tensor_reduce(rmax[:], lg, AX.X, ALU.max))
                    V.tensor_tensor(pr, lg, bc(rmax[:], 2, E), ALU.subtract).then_inc(f["log_ev"], 1)
                    dve.wait_ge(f["r_act"], 2)
                    step.done(V.tensor_reduce(rsm[:], pr, AX.X, ALU.add))
                    step.done(V.reciprocal(rsm[:], rsm[:]))
                    step.done(V.tensor_tensor(pr, pr, bc(rsm[:], 2, E), ALU.mult))
                    step.done(V.tensor_scalar(sh_gate[:], sh_gate[:], 1.0, None, ALU.add))
                    step.done(V.reciprocal(sh_gate[:], sh_gate[:]))
                    step.add(V.tensor_scalar(sh_gate_x[:], sh_gate[:], tg[:, 2:3], None, ALU.mult))
                    keys = probs
                else:
                    dve.sem_inc(f["log_ev"], 1)
                    dve.wait_ge(f["r_act"], 1)
                    step.done(V.tensor_scalar(pr, pr, 1.0, None, ALU.add))
                    step.done(V.reciprocal(pr, pr))
                    step.done(V.tensor_tensor(pk, pr, bc(scal[:, 5:5 + E], 1, NT), ALU.add))
                    keys = picks
                for i in range(NT):
                    step.add(V.max(top8[:, i, :], keys[:, i, 0:E]))
                step.wait()
                for i in range(NT):
                    step.add(V.max_index(idx8[:, i, :], top8[:, i, :], keys[:, i, 0:E]))
                step.wait()
                step.done(V.tensor_copy(idxf[:], idx8[:]))
                h1, h2 = hot[:, :, 0:K, 0:E], hot2[:, :, 0:K, 0:E]
                for k in range(K):
                    step.add(V.tensor_tensor(hot[:, :, k, 0:E], bc(iota_e[:, 0:E], 1, NT), bc(idxf[:, :, k], 2, E), ALU.is_equal))
                step.wait()
                mem = member[:, :, 0:E]
                step.done(V.tensor_tensor(mem, hot[:, :, 0, 0:E], hot[:, :, 1, 0:E], ALU.add))
                for k in range(2, K):
                    step.done(V.tensor_tensor(mem, mem, hot[:, :, k, 0:E], ALU.add))
                dve.sem_inc(f["mem_ready"], 1)
                if y.n == 0:
                    step.done(V.tensor_copy(wts[:], top8[:, :, 0:K]))
                else:
                    for k in range(K):
                        step.add(V.tensor_tensor(hot2[:, :, k, 0:E], hot[:, :, k, 0:E], pr, ALU.mult))
                    step.wait()
                    for k in range(K):
                        step.add(V.tensor_reduce(wts[:, :, k], hot2[:, :, k, 0:E], AX.X, ALU.add))
                    step.wait()
                    step.done(V.tensor_tensor(rsm[:], wts[:, :, 0], wts[:, :, 1], ALU.add))
                    step.done(V.tensor_scalar(rsm[:], rsm[:], 1e-12, None, ALU.max))
                    step.done(V.reciprocal(rsm[:], rsm[:]))
                    step.done(V.tensor_tensor(wts[:, :, 0:K], wts[:, :, 0:K], bc(rsm[:], 2, K), ALU.mult))
                dve.wait_ge(f["pos_full"], 1)
                c, n, inc, bs, ov = cnt[:, 0:E], ntile[:, 0:E], incl[:, 0:E], base[:, 0:E], over[:, 0:E]
                step.add(V.tensor_copy(c, bank[6][:, 0:E]))
                ps, pb = pos[:, :, 0:E], posb[:, :, 0:E]
                step.done(V.tensor_copy(ps, bank[7][:].rearrange("p (t e) -> p t e", t=NT)[:, :, 0:E]))
                step.done(V.tensor_scalar(n, c, P / 2 - 0.5, 1.0 / P, ALU.add, ALU.mult))
                step.done(V.tensor_scalar(n, n, MAGIC, None, ALU.add))
                step.done(V.tensor_scalar(n, n, MAGIC + y.own, 0.0, ALU.subtract, ALU.max))
                step.done(V.tensor_tensor_scan(inc, ones[:, 0:E], n, 0.0, ALU.mult, ALU.add))
                step.done(V.tensor_tensor(bs, inc, n, ALU.subtract))
                step.done(V.tensor_scalar(bs, bs, float(P), None, ALU.mult))
                if y.own:
                    step.done(V.scalar_tensor_tensor(out=ov, in0=iota_e[:, 0:E], scalar=-float(P), in1=bs, op0=ALU.mult, op1=ALU.add))
                    step.done(V.tensor_scalar(ov, ov, float(P * (y.main - 1)), None, ALU.add))
                    step.done(V.tensor_scalar(pb, ps, float(P), None, ALU.is_ge))
                    step.done(V.tensor_tensor(pb, pb, bc(ov, 1, NT), ALU.mult))
                    step.done(V.tensor_tensor(pb, pb, ps, ALU.add))
                    step.done(V.tensor_scalar(ov, iota_e[:, 0:E], float(P), None, ALU.mult))
                    step.done(V.tensor_tensor(pb, pb, bc(ov, 1, NT), ALU.add))
                else:
                    step.done(V.tensor_tensor(pb, ps, bc(bs, 1, NT), ALU.add))
                for k in range(K):
                    step.add(V.tensor_tensor(hot[:, :, k, 0:E], hot[:, :, k, 0:E], pb, ALU.mult))
                step.wait()
                for k in range(K):
                    step.add(V.tensor_reduce(slotf[:, :, k], hot[:, :, k, 0:E], AX.X, ALU.add))
                step.wait()
                V.tensor_copy(slot[:, :, 0:K], slotf[:, :, 0:K]).then_inc(f["slots_ready"], 1)
                NV = y.extra if y.own else y.main + y.last_round
                step.done(V.tensor_tensor(owner_c[0:1, 0:NV, 0:E], bc(incl[0:1, 0:E], 1, NV), bc(iota_v[0:1, 0:NV], 2, E), ALU.is_le))
                step.done(V.tensor_reduce(owner_f[0:1, 0:NV], owner_c[0:1, 0:NV, 0:E], AX.X, ALU.add))
                step.done(V.tensor_scalar(owner_f[0:1, 0:NV], owner_f[0:1, 0:NV], float(E - 1), None, ALU.min))
                step.done(V.tensor_copy(owner[0:1, 0:NV], owner_f[0:1, 0:NV]))
                step.done(V.tensor_copy(nextra[0:1, 0:1], incl[0:1, E - 1:E]))
                dve.sem_inc(f["plan_ready"], 1)

            def shared(y):
                f = fs[y.n]
                nch = len(y.chunks)
                dve.wait_ge(f["sh_full"], HT)
                for c, (c0, n) in enumerate(y.chunks):
                    m = nch + c
                    dve.wait_ge(f["up_act"], m + 1)
                    V.tensor_tensor(sh_h[0:n, c, :], sh_act[0:n, m % 2, :], bank[2 * (m % 2) + 1][0:n, :],
                                    ALU.mult).then_inc(f["up_free"], 1)

            def shared_out(y, tiles):
                f = fs[y.n]
                for t in tiles:
                    dve.wait_ge(f["sh_full"], t + 1)
                    gate = tg[:, 3:4] if y.n else sh_gate_x[:, t:t + 1]
                    V.scalar_tensor_tensor(out=x_sb[:, t, :], in0=bank[4 + t % 2][:, 0:D], scalar=gate, in1=x_sb[:, t, :],
                                           op0=ALU.mult, op1=ALU.add).then_inc(f["sh_free"], 1)

            def experts(y):
                f = fs[y.n]

                def take_x(i, u, first):
                    dve.wait_ge(f["xT2_full"], i + 1)
                    if not first:
                        dve.wait_ge(f["e_up_full"], i - NB + 1)
                    V.tensor_copy(xgT[:, u].rearrange("p c n -> p (c n)"), bank[u % 2][:, 0:2 * P]).then_inc(f["xT2_ev"], 1)

                def gated(i, q, first):
                    dve.wait_ge(f["e_silu"], i + 1)
                    if not first:
                        dve.wait_ge(f["hT_full"], i - 1)
                    V.tensor_tensor(e_h[:, q, :], e_act[:, q, :], bank[2 + q][:, I_EXP:2 * I_EXP], ALU.mult).then_inc(f["e_mul"], 1)

                def take_h(i, q, first):
                    dve.wait_ge(f["hT_full"], i + 1)
                    if not first:
                        dve.wait_ge(f["y_full"], i - 1)
                    V.tensor_copy(e_hT[:, q].rearrange("p c n -> p (c n)"), bank[4 + q][0:IC, 0:2 * P]).then_inc(f["hT_ev"], 1)

                def one(t, u, more, turn, first, first_x=False):
                    if more:
                        gated(t + 1, (u + 1) % 2, first)
                    if turn:
                        take_x(t + 3, (u + 3) % NB, first_x)
                    if more:
                        take_h(t + 1, (u + 1) % 2, first)

                for i in range(3):
                    take_x(i, i, True)
                gated(0, 0, True)
                take_h(0, 0, True)
                last = y.main - 1
                for t in range(NB):
                    one(t, t, True, True, t < 1, t + 3 < NB)
                with dve.Fori(1, y.main // NB - 1) as it:
                    for u in range(NB):
                        one(it * NB + u, u, True, True, False)
                for t in range(y.main - NB, y.main):
                    one(t, t % NB, t + 1 <= last, t + 3 <= last, False)
                if y.last_round:
                    n = dve.value_load(nextra[0:1, 0:1], min_val=0, max_val=y.main + y.last_round)
                    with dve.If(n > y.main):
                        for i in range(3):
                            take_x(y.main + i, i, False)
                        gated(y.main, 0, False)
                        take_h(y.main, 0, False)
                        last = y.main + y.last_round - 1
                        for t in range(y.main, last + 1):
                            one(t, t % NB, t + 1 <= last, t + 3 <= last, False)
                if y.extra:
                    n = dve.value_load(nextra[0:1, 0:1], min_val=0, max_val=y.extra)
                    with dve.If(n > 0):
                        with dve.Fori(0, y.extra) as v:
                            with dve.If(n > v):
                                dve.wait_ge(f["o_silu"], v + 1)
                                V.tensor_tensor(e_h[:, 0, :], e_act[:, 0, :], bank[2][:, I_EXP:2 * I_EXP], ALU.mult).then_inc(f["o_mul"], 1)
                                dve.wait_ge(f["o_hfull"], v + 1)
                                V.tensor_copy(e_hT[:, 0].rearrange("p c n -> p (c n)"), bank[4][0:IC, 0:2 * P]).then_inc(f["o_hev"], 1)

            def combine(y, lo, hi):
                f = fs[y.n]
                for i in range(lo, hi):
                    shared_out(y, y.late[i])
                    if i == 0:
                        dve.wait_ge(f["shared_added"], 1)
                    if i == HT:
                        dve.wait_ge(f["sh_free"], NT)
                    dve.wait_ge(f["gathered"], (i + 1) * y.K)
                    V.scalar_tensor_tensor(out=x_sb[:, i, :], in0=bank[i % 4][:, 0:D], scalar=tg[:, 2 + y.n:3 + y.n], in1=x_sb[:, i, :],
                                           op0=ALU.mult, op1=ALU.add).then_inc(f["combined"], 1)

            roots = [0]

            def deviation(src, n):
                for i in range(n):
                    step.add(V.bn_stats(st[:, i, :], src(i)))
                step.wait()
                for i in range(n):
                    step.add(V.bn_aggr(mv[:, i, :], st[:, i, :]))
                step.wait()
                V.tensor_scalar(vare[:, 0:n], mv[:, 0:n, 1], LN_EPS, None, ALU.add).then_inc(var_act, 1)
                roots[0] += 1
                dve.wait_ge(sdev_ready, roots[0])
                r = rstd[:, 0:n]
                step.done(V.reciprocal(r, sdev[:, 0:n]))
                step.done(V.scalar_tensor_tensor(out=newton[:, 0:n], in0=r, scalar=-0.5, in1=r, op0=ALU.mult, op1=ALU.mult))
                step.done(V.tensor_tensor(newton[:, 0:n], newton[:, 0:n], vare[:, 0:n], ALU.mult))
                step.done(V.scalar_tensor_tensor(out=r, in0=newton[:, 0:n], scalar=1.5, in1=r, op0=ALU.add, op1=ALU.mult))

            def for_act(n):
                V.scalar_tensor_tensor(out=shift[:, 0:n], in0=mv[:, 0:n, 0], scalar=-1.0, in1=rstd[:, 0:n],
                                       op0=ALU.mult, op1=ALU.mult).then_inc(shift_ready, 1)

            def mix(q, lo, hi):
                tiles, n = range(lo, hi), hi - lo
                y = tmp[:, lo:hi, :]
                xq = x_sb[:, lo:hi, :]
                dve.wait_ge(fs[0]["combined"], hi)
                deviation(lambda i: x_sb[:, lo + i, :], n)
                for_act(n)
                dve.wait_ge(applied, q + 1)
                yb = y.rearrange("p (b t) d -> p b t d", t=QT)
                step.done(V.tensor_tensor(yb, yb, bc(summary[:, lo // QT:hi // QT, :], 2, QT), ALU.add))
                deviation(lambda i: tmp[:, lo + i, :], n)
                for i, t in enumerate(tiles):
                    step.add(V.scalar_tensor_tensor(out=tmp[:, t, :], in0=tmp[:, t, :], scalar=mv[:, i, 0:1], in1=R["gamma"],
                                                    op0=ALU.subtract, op1=ALU.mult))
                step.wait()
                for i, t in enumerate(tiles):
                    step.add(V.scalar_tensor_tensor(out=tmp[:, t, :], in0=tmp[:, t, :], scalar=rstd[:, i:i + 1], in1=R["beta"],
                                                    op0=ALU.mult, op1=ALU.add))
                step.wait()
                step.done(V.scalar_tensor_tensor(out=xq, in0=y, scalar=tg[:, 1:2], in1=xq, op0=ALU.mult, op1=ALU.add))
                deviation(lambda i: x_sb[:, lo + i, :], n)
                for_act(n)

            for y in LAYERS:
                route(y)
                shared(y)
                experts(y)
                for q, (lo, hi) in enumerate(MIX):
                    combine(y, lo, hi)
                    if not y.n:
                        mix(q, lo, hi)

        @block.scalar
        def _(act):
            A = nc.scalar
            step = Steps(act, act_step)
            act.wait_ge(ld_small, 48)
            step.add(A.activation(tg[:], scal[:, 0:4], ACT.Tanh))
            step.done(A.activation(krow[:], scal[:, 4:5], ACT.Exp, scale=-1.0))
            act.sem_inc(gates_ready, 1)
            SUBS = QT * 4
            with act.Fori(0, B) as b:
                for oc in range(CC):
                    act.wait_ge(work_full[oc], b * FULL[oc] + 2)
                    A.activation(kT[:, oc, :], bank[6 + oc][:], ACT.Identity, bias=colb[:, 0, oc:oc + 1]).then_inc(work_free[oc], 1)
                for nt in range(QT):
                    act.wait_ge(work_full[nt], b * FULL[nt] + 3)
                    A.copy(qT[:, :, :, nt * P:(nt + 1) * P], bank[4 + nt][:].rearrange("p (r c n) -> p r c n", r=2, c=CC)).then_inc(work_free[nt], 1)

                def take(s, j):
                    act.wait_ge(t_full, b * SUBS * 4 + s * 4 + j + 1)
                    A.copy(pT[:, s % 2, j].rearrange("p t n -> p (t n)"), bank[4][:]).then_inc(t_free[0], 1)

                def back(nt):
                    act.wait_ge(av_done, b * SUBS + 4 * (nt + 1))
                    A.copy(oT[:].rearrange("p g n -> p (g n)"), bank[6][:]).then_inc(work_free[0], 1)

                for s in range(SUBS):
                    nt, g = divmod(s, 4)
                    for j in range(4):
                        act.wait_ge(scored, b * SUBS * 4 + s * 4 + j + 1)
                        A.activation(z_sb[:, s % 2, j, :], z_sb[:, s % 2, j, :], ACT.Exp, bias=zmin[:, s % 2, j:j + 1], scale=-1.0,
                                     accum_out=psum_row[:, nt, g, j:j + 1]).then_inc(expd, 1)
                        if j % 2 and s:
                            take(s - 1, j - 1)
                    if s == 5:
                        back(0)
                take(SUBS - 1, 0)
                take(SUBS - 1, 2)
                back(1)

            for q in range(B - 1):
                act.wait_ge(fs[0]["xT_full"], q + 1)
                A.copy(xnT[:, :, q * S:(q + 1) * S], bank[q][:].rearrange("p (c n) -> p c n", c=CC)).then_inc(fs[0]["xT_ev"], 1)

            def route(y):
                f, E = fs[y.n], y.E
                act.wait_ge(f["log_ev"], 1)
                if y.n == 0:
                    A.activation(probs[:], probs[:], ACT.Exp).then_inc(f["r_act"], 1)
                    A.activation(sh_gate[:], logits[:, :, E], ACT.Exp, scale=-1.0).then_inc(f["r_act"], 1)
                else:
                    A.activation(probs[:, :, 0:E], logits[:, :, 0:E], ACT.Exp, scale=-1.0).then_inc(f["r_act"], 1)

            def shared(y):
                f = fs[y.n]
                nch = len(y.chunks)
                for m in range(2 * nch):
                    n = y.chunks[m % nch][1]
                    act.wait_ge(f["up_full"], m + 1)
                    if m >= nch + 2:
                        act.wait_ge(f["up_free"], m - 1)
                    elif m >= 2:
                        act.wait_ge(f["h_made"], m - 1)
                    A.activation(sh_act[0:n, m % 2, :], bank[2 * (m % 2)][0:n, :], ACT.Silu).then_inc(f["up_act"], 1)
                    if m < nch:
                        A.copy(sh_up[0:n, m % 2, :], bank[2 * (m % 2) + 1][0:n, :]).then_inc(f["up_free"], 1)
                    if m == nch - 1:
                        act.wait_ge(f["mem_ready"], 1)
                        for t in range(NT // 2):
                            act.wait_ge(f["sh_full"], t + 1)
                            if y.n == 0:
                                A.activation(sh_y[:, t, :], bank[4 + t % 2][:, 0:D], ACT.Copy, scale=sh_gate[:, t:t + 1]).then_inc(f["sh_free"], 1)
                            else:
                                A.copy(sh_y[:, t, :], bank[4 + t % 2][:, 0:D]).then_inc(f["sh_free"], 1)

            def experts(y):
                f = fs[y.n]

                def silu(i, q, first):
                    act.wait_ge(f["e_up_full"], i + 1)
                    if not first:
                        act.wait_ge(f["e_mul"], i - 1)
                    A.activation(e_act[:, q, :], bank[2 + q][:, 0:I_EXP], ACT.Silu).then_inc(f["e_silu"], 1)

                def take_y(t, u, rounds, first):
                    act.wait_ge(f["y_full"], t + 1)
                    if not first:
                        act.wait_ge(f[f"y_st{u // 2 % 2}"], rounds)
                    A.copy(e_y[:, u % 4, :], bank[6 + u % 2][:, 0:D]).then_inc(f["y_ev"], 1)

                silu(0, 0, True)
                last = y.main - 1

                def one(t, u, rounds, more, first_s, first_y):
                    if more:
                        silu(t + 1, (u + 1) % 2, first_s)
                    take_y(t, u, rounds, first_y)

                W = 2 * NB
                for t in range(NB):
                    one(t, t, 16 * (t // 4), True, t + 1 < 2, t < 4)
                if y.main >= 2 * NB + W:
                    with act.Fori(0, (y.main - 2 * NB) // W) as it:
                        for v in range(W):
                            t = it * W + NB + v
                            one(t, NB + v, it * (16 * W // 4) + 16 * ((NB + v) // 4), True, False, False)
                for t in range(NB + (y.main - 2 * NB) // W * W, y.main):
                    one(t, t, 16 * (t // 4), t + 1 <= last, False, False)
                if y.last_round:
                    n = act.value_load(nextra[0:1, 0:1], min_val=0, max_val=y.main + y.last_round)
                    with act.If(n > y.main):
                        silu(y.main, 0, False)
                        last = y.main + y.last_round - 1
                        for t in range(y.main, last + 1):
                            one(t, t, 16 * (t // 4), t + 1 <= last, False, False)
                if y.extra:
                    n = act.value_load(nextra[0:1, 0:1], min_val=0, max_val=y.extra)
                    with act.If(n > 0):
                        with act.Fori(0, y.extra) as v:
                            with act.If(n > v):
                                act.wait_ge(f["o_tfull"], v + 1)
                                A.copy(xgT[:, 0].rearrange("p c n -> p (c n)"), bank[0][:, 0:2 * P]).then_inc(f["o_tev"], 1)
                                act.wait_ge(f["o_up"], v + 1)
                                A.activation(e_act[:, 0, :], bank[2][:, 0:I_EXP], ACT.Silu).then_inc(f["o_silu"], 1)
                                act.wait_ge(f["o_y"], v + 1)
                                A.copy(e_y[:, 0, :], bank[6][:, 0:D]).then_inc(f["o_yev"], 1)

            def diagonals(y):
                f = fs[y.n]
                for n in range(NT * y.K):
                    i, k = divmod(n, y.K)
                    A.activation(diag_w[:, n, :], ident[:], ACT.Copy, scale=wts[:, i, k:k + 1]).then_inc(f["diagonal"], 1)

            roots = [0]

            def root(n):
                roots[0] += 1
                act.wait_ge(var_act, roots[0])
                A.activation(sdev[:, 0:n], vare[:, 0:n], ACT.Sqrt).then_inc(sdev_ready, 1)

            def apply(lo, hi, count, dst, signal):
                act.wait_ge(shift_ready, count)
                for i, t in enumerate(range(lo, hi)):
                    step.add(A.activation(dst[:, t, :], x_sb[:, t, :], ACT.Identity, bias=shift[:, i:i + 1], scale=rstd[:, i:i + 1]))
                step.wait()
                act.sem_inc(signal, 1)

            def take_x(q):
                for c in range(CC):
                    act.wait_ge(fs[1]["xT_full"], q * CC + c + 1)
                    A.copy(xnT[:, c, q * HT * P:(q + 1) * HT * P], bank[4 + c][:]).then_inc(fs[1]["xT_ev"], 1)

            def mix(q, lo, hi):
                root(hi - lo)
                apply(lo, hi, 2 * q + 1, tmp, applied)
                root(hi - lo)
                root(hi - lo)
                if hi == NT:
                    step.done(A.activation(krow[:], krow[:], ACT.Exp))
                apply(lo, hi, 2 * q + 2, xn, fs[1]["x_ready"])
                if hi % HT == 0:
                    take_x(hi // HT - 1)

            for y in LAYERS:
                if y.n:
                    for q, (lo, hi) in enumerate(MIX):
                        mix(q, lo, hi)
                act.wait_ge(fs[y.n]["ld_gate"], 16)
                route(y)
                shared(y)
                act.wait_ge(fs[y.n]["plan_ready"], 1)
                experts(y)
                diagonals(y)

        @block.tensor
        def _(pe):
            M = nc.tensor
            pe.wait_ge(consts, 1)

            def turn_codes(n, w, lo, hi):
                pe.wait_ge(coded, n)
                dst = bank[w][:].bitcast(BF16)[:, 0:CC * (hi - lo) * P].rearrange("p (c t n) -> p c t n", c=CC, t=hi - lo)
                for c in range(CC):
                    for i in range(hi - lo):
                        last = M.transpose(dst[:, c, i, :], codes[:, lo + i, c * P:(c + 1) * P], identb[:])
                last.then_inc(code_t, 1)

            turn_codes(1, 0, 0, QT)
            pe.wait_ge(coded, 2)
            tb = bank[2][:].bitcast(BF16).rearrange("p (w c d) -> p w c d", w=2, c=CC)
            for w in range(2):
                for oc in range(CC):
                    for c in range(CC):
                        last = M.transpose(tb[:, w, c, oc * P:(oc + 1) * P], w_codes[:, w, oc, c * P:(c + 1) * P], identb[:])
            last.then_inc(code_t, 1)
            pe.wait_ge(diag_ready, 1)
            M.matmul(bank[3][:], ones[:], diag[:].rearrange("p a b -> p (a b)"), start=True, stop=True).then_inc(sw_full, 1)
            pe.wait_ge(setup_done, 1)
            pe.wait_ge(code_ev, 2)
            pe.wait_ge(ld_wkv, 16)
            SUBS = QT * 4
            pe.sem_inc(work_free[1], 1)

            def output(q):
                pe.wait_ge(code_ev, q + 4)
                for i in range(QT):
                    for c in range(CC):
                        last = M.matmul(bank[7][:, i * D:(i + 1) * D], codesT[:, c, QT + i, :], w_codesT[:, 1, c, :],
                                        start=(c == 0), stop=(c == CC - 1))
                last.then_inc(oproj_full, 1)

            def turn_x(q, w):
                pe.wait_ge(fs[0]["x_ready"], q + 1)
                for c in range(CC):
                    for i in range(QT):
                        last = M.transpose(bank[w][:, (c * QT + i) * P:(c * QT + i + 1) * P],
                                           xn[:, q * QT + i, c * P:(c + 1) * P], ident[:])
                last.then_inc(fs[0]["xT_full"], 1)

            def batch(b, pre, post):
                lo, hi = (0 if pre else QT), (2 * QT if post else QT)

                def freed(w, n):
                    pe.wait_ge(work_free[w], b * 6 + n + w)

                for nt in range(QT):
                    for c in range(CC):
                        last = M.matmul(bank[nt][:, 0:D], codesT[:, c, nt, :], w_codesT[:, 0, c, :],
                                        start=(c == 0), stop=(c == CC - 1))
                    last.then_inc(work_full[nt], 1)
                pe.wait_ge(ld_ctx, b * 16 + 16)
                for oc in range(CC):
                    if oc:
                        freed(1, 0)
                    for c in range(CC):
                        last = M.matmul(bank[6 + oc][:], w_kv[:, 0, c, oc * P:(oc + 1) * P], ctxT[:, c, :],
                                        start=(c == 0), stop=(c == CC - 1))
                    last.then_inc(work_full[oc], 1)
                for nt in range(QT):
                    pe.wait_ge(q_ready, b * 4 + 2 * (nt + 1))
                    for r in range(2):
                        for c in range(CC):
                            m = r * CC + c
                            last = M.transpose(bank[4 + nt][:, m * P:(m + 1) * P], q_split[:, nt, r, c * P:(c + 1) * P], ident[:])
                    last.then_inc(work_full[nt], 1)

                def scores(s):
                    nt, g = divmod(s, 4)
                    for j in range(4):
                        cc, par, _ = head(g, j)
                        if s:
                            pe.wait_ge(scored, b * SUBS * 4 + (s - 1) * 4 + j + 1)
                        M.matmul(bank[j][:], qT[32 * j:32 * j + 32, par, cc, nt * P:(nt + 1) * P], kT[32 * j:32 * j + 32, cc, :],
                                 start=True, stop=True).then_inc(score_full, 1)

                def probabilities(s):
                    for j in range(4):
                        pe.wait_ge(expd, b * SUBS * 4 + s * 4 + j + 1)
                        n = s * 2 + j // 2
                        if n:
                            pe.wait_ge(t_free[j % 2], b * SUBS * 2 + n)
                        for t in range(LT):
                            last = M.transpose(bank[4 + j % 2][:, t * P:(t + 1) * P], z_sb[:, s % 2, j, t * P:(t + 1) * P], ident[:])
                        last.then_inc(t_full, 1)

                def weigh(s):
                    nt, g = divmod(s, 4)
                    for k in range(2):
                        pe.wait_ge(t_free[k], b * SUBS * 2 + 2 * (s + 1))
                    if g == 0:
                        freed(0, 4 + nt)
                    for t in range(LT):
                        for j in range(4):
                            h = head(g, j)[2]
                            last = M.matmul(bank[6][32 * j:32 * j + 32, g * P:(g + 1) * P], v_sb[:, t, h, :], pT[:, s % 2, j, t, :],
                                            start=(t == 0), stop=(t == LT - 1))
                    last.then_inc(av_done, 1)

                def restore(nt):
                    freed(1, 4 + nt)
                    freed(0, 5 + nt)
                    if nt == 0:
                        pe.wait_ge(code_ev, b + 3)
                        if post:
                            pe.wait_ge(oproj_free, b)
                    for g in range(4):
                        last = M.transpose(bank[7][:, g * P:(g + 1) * P], oT[:, g, :], ident[:])
                    last.then_inc(work_full[1], 1)

                freed(0, 3)
                freed(1, 2)
                scores(0)
                freed(1, 3)
                for w in range(2):
                    for t in range(2):
                        for c in range(CC):
                            last = M.matmul(bank[6 + w][:, t * D:(t + 1) * D], ctxT[:, c, (2 * w + t) * P:(2 * w + t + 1) * P],
                                            w_kv[:, 1, c, :], start=(c == 0), stop=(c == CC - 1))
                    last.then_inc(work_full[w], 1)
                for s in range(SUBS):
                    if s + 1 < SUBS:
                        scores(s + 1)
                    probabilities(s)
                    if s:
                        weigh(s - 1)
                    if s == 3:
                        freed(1, 4)
                        turn_codes(b + 3, 7, lo, hi)
                    if s == 4 and post:
                        output(b - 1)
                    if s == 5:
                        restore(0)
                weigh(SUBS - 1)
                restore(1)

            batch(0, True, False)
            with pe.Fori(1, B - 1) as b:
                batch(b, True, True)
            batch(B - 1, False, True)

            for q in range(B - 1):
                turn_x(q, q)
            turn_codes(B + 3, 7, QT, 2 * QT)
            for ec in range(CC):
                for c in range(CC):
                    last = M.matmul(bank[4][:, ec * B:(ec + 1) * B], w_kv[:, 2, c, ec * P:(ec + 1) * P], zT[:, c, :],
                                    start=(c == 0), stop=(c == CC - 1))
            last.then_inc(seq_pe, 1)
            output(B - 1)
            pe.wait_ge(seq_dve, 1)
            for b in range(B):
                for c in range(CC):
                    last = M.matmul(bank[4 + b // 2][:, (b % 2) * D:(b % 2 + 1) * D], mTb[:, c, b, :], w_kv[:, 3, c, :],
                                    start=(c == 0), stop=(c == CC - 1))
            last.then_inc(seq_pe, 1)
            turn_x(B - 1, 7)

            def logits_of(y, tiles):
                f = fs[y.n]
                pe.wait_ge(f["ld_gate"], 16)
                ng = gate_w[y.n].shape[2]
                for i in tiles:
                    for c in range(CC):
                        last = M.matmul(bank[6][:, i * 64:i * 64 + ng], xnT[:, c, i * P:(i + 1) * P], gate_w[y.n][:, c, :],
                                        start=(c == 0), stop=(c == CC - 1))
                last.then_inc(f["log_full"], 1)

            def down_shared(y, tiles):
                f = fs[y.n]
                for t in tiles:
                    if t >= 2:
                        pe.wait_ge(f["sh_free"], t - 1)
                    for c, (c0, n) in enumerate(y.chunks):
                        last = M.matmul(bank[4 + t % 2][:, 0:D], sh_h[0:n, c, t % HT * P:(t % HT + 1) * P], sh_out[0:n, c, :],
                                        start=(c == 0), stop=(c == len(y.chunks) - 1))
                    last.then_inc(f["sh_full"], 1)

            def ffn(y):
                f, E = fs[y.n], y.E
                pe.wait_ge(f["xT_ev"], 4)
                if not y.n:
                    logits_of(y, range(NT))

                def positions():
                    pe.wait_ge(f["mem_ready"], 1)
                    o = bank[7][:].rearrange("p (t e) -> p t e", t=NT)[:, :, 0:E]
                    M.matmul(o, before[:], member[:, :, 0:E], start=True, stop=False)
                    for j in range(NT - 2, -1, -1):
                        M.matmul(o[:, j + 1:NT, :], onesb[:], bc(member[:, j, 0:E], 1, NT - 1 - j), start=False, stop=(j == 0))
                    for i in range(NT):
                        last = M.matmul(bank[6][:, 0:E], onesb[:], member[:, i, 0:E], start=(i == 0), stop=(i == NT - 1))
                    last.then_inc(f["pos_full"], 1)

                pe.wait_ge(f["ld_sh"], 16 * (1 + len(y.chunks)))
                nch = len(y.chunks)

                for half in range(2):
                    for c, (c0, n) in enumerate(y.chunks):
                        m = half * nch + c
                        if m >= 2:
                            pe.wait_ge(f["up_act"], m - 1)
                            pe.wait_ge(f["up_free"], m - 1)
                        for g in range(2):
                            for cc in range(CC):
                                last = M.matmul(bank[2 * (m % 2) + g][0:n, :], sh_in[:, cc, g * y.shared + c0:g * y.shared + c0 + n],
                                                xnT[:, cc, half * 512:half * 512 + 512], start=(cc == 0), stop=(cc == CC - 1))
                        last.then_inc(f["up_full"], 1)
                        if half == 0 and c == nch // 2:
                            positions()
                    if half == 0:
                        pe.wait_ge(f["h_made"], nch)
                        down_shared(y, range(HT))
                pe.wait_ge(f["sh_free"], HT)
                pe.wait_ge(f["up_free"], 2 * nch)

                def turn(i, u, rnd, first):
                    if u % 2 == 0:
                        pe.wait_ge(f[f"ld_x{u // 2}"], 16 * rnd + 16)
                    if not first:
                        pe.wait_ge(f["xT2_ev"], i - 1)
                    for c in range(CC):
                        last = M.transpose(bank[u % 2][:, c * P:(c + 1) * P], xg[:, u, c * P:(c + 1) * P], ident[:])
                    last.then_inc(f["xT2_full"], 1)

                def up(i, u, rnd, first):
                    if u % 2 == 0:
                        pe.wait_ge(f[f"ld_w13_{u // 2}"], y.w_inc * rnd + y.w_inc)
                    pe.wait_ge(f["xT2_ev"], i + 1)
                    if not first:
                        pe.wait_ge(f["e_mul"], i - 1)
                    for c in range(CC):
                        last = M.matmul(bank[2 + u % 2][:, 0:2 * I_EXP], xgT[:, u, c, :], w13[:, u, c, :], start=(c == 0), stop=(c == CC - 1))
                    last.then_inc(f["e_up_full"], 1)

                def turn_h(i, u, first):
                    pe.wait_ge(f["e_mul"], i + 1)
                    if not first:
                        pe.wait_ge(f["hT_ev"], i - 1)
                    for c in range(2):
                        last = M.transpose(bank[4 + u % 2][0:IC, c * P:(c + 1) * P], e_h[:, u % 2, c * IC:(c + 1) * IC], ident[:])
                    last.then_inc(f["hT_full"], 1)

                def down(i, u, rnd, first):
                    if u % 2 == 0:
                        pe.wait_ge(f[f"ld_w2_{u // 2}"], y.w_inc * rnd + y.w_inc)
                    pe.wait_ge(f["hT_ev"], i + 1)
                    if not first:
                        pe.wait_ge(f["y_ev"], i - 1)
                    for c in range(2):
                        last = M.matmul(bank[6 + u % 2][:, 0:D], e_hT[:, u % 2, c, :], w2[:, u, c, :], start=(c == 0), stop=(c == 1))
                    last.then_inc(f["y_full"], 1)

                for i in range(3):
                    turn(i, i, 0, i < 2)
                up(0, 0, 0, True)
                turn_h(0, 0, True)
                last_t = y.main - 1

                def one(t, u, rnd, more, turns, first):
                    if more:
                        up(t + 1, (u + 1) % NB, rnd + (u + 1) // NB, first and t + 1 < 2)
                    down(t, u, rnd, first and t < 2)
                    if turns:
                        turn(t + 3, (u + 3) % NB, rnd + (u + 3) // NB, False)
                    if more:
                        turn_h(t + 1, (u + 1) % NB, first and t + 1 < 2)

                for t in range(NB):
                    one(t, t, 0, True, True, True)
                with pe.Fori(1, y.main // NB - 1) as it:
                    for u in range(NB):
                        one(it * NB + u, u, it, True, True, False)
                for t in range(y.main - NB, y.main):
                    one(t, t % NB, t // NB, t + 1 <= last_t, t + 3 <= last_t, False)
                if y.last_round:
                    pe.wait_ge(f["plan_ready"], 1)
                    n = pe.value_load(nextra[0:1, 0:1], min_val=0, max_val=y.main + y.last_round)
                    with pe.If(n > y.main):
                        rnd, last_t = y.main // NB, y.main + y.last_round - 1
                        for i in range(3):
                            turn(y.main + i, i, rnd, False)
                        up(y.main, 0, rnd, False)
                        turn_h(y.main, 0, False)
                        for t in range(y.main, last_t + 1):
                            one(t, t % NB, t // NB, t + 1 <= last_t, t + 3 <= last_t, False)
                if y.extra:
                    pe.wait_ge(f["plan_ready"], 1)
                    pe.wait_ge(f["y_ev"], y.main)
                    n = pe.value_load(nextra[0:1, 0:1], min_val=0, max_val=y.extra)
                    with pe.If(n > 0):
                        with pe.Fori(0, y.extra) as v:
                            with pe.If(n > v):
                                pe.wait_ge(f["ox_ld"], v * 48 + 48)
                                for c in range(CC):
                                    last = M.transpose(bank[0][:, c * P:(c + 1) * P], xg[:, 0, c * P:(c + 1) * P], ident[:])
                                last.then_inc(f["o_tfull"], 1)
                                pe.wait_ge(f["o_tev"], v + 1)
                                for c in range(CC):
                                    last = M.matmul(bank[2][:, 0:2 * I_EXP], xgT[:, 0, c, :], w13[:, 0, c, :], start=(c == 0), stop=(c == CC - 1))
                                last.then_inc(f["o_up"], 1)
                                pe.wait_ge(f["o_mul"], v + 1)
                                for c in range(2):
                                    last = M.transpose(bank[4][0:IC, c * P:(c + 1) * P], e_h[:, 0, c * IC:(c + 1) * IC], ident[:])
                                last.then_inc(f["o_hfull"], 1)
                                pe.wait_ge(f["o_hev"], v + 1)
                                for c in range(2):
                                    last = M.matmul(bank[6][:, 0:D], e_hT[:, 0, c, :], w2[:, 0, c, :], start=(c == 0), stop=(c == 1))
                                last.then_inc(f["o_y"], 1)
            def combine(y, q):
                f = fs[y.n]
                for i in range(q * HT, (q + 1) * HT):
                    down_shared(y, y.late[i])
                    if i >= 4:
                        pe.wait_ge(f["combined"], i - 3)
                    for k in range(y.K):
                        n = i * y.K + k
                        pe.wait_ge(f["diagonal"], n + 1)
                        pe.wait_ge(got[n % NG], 16 * ((n + y.n * NT * L0.K) // NG + 1))
                        M.matmul(bank[i % 4][:, 0:D], diag_w[:, n, :], yk[:, n % NG, :], start=(k == 0), stop=(k == y.K - 1))\
                         .then_inc(f["gathered"], 1)

            def turn_mixed(q):
                pe.wait_ge(fs[1]["x_ready"], q + 2)
                for c in range(CC):
                    if q:
                        pe.wait_ge(fs[1]["xT_ev"], c + 1)
                    for i in range(HT):
                        last = M.transpose(bank[4 + c][:, i * P:(i + 1) * P], xn[:, q * HT + i, c * P:(c + 1) * P], ident[:])
                    last.then_inc(fs[1]["xT_full"], 1)
                pe.wait_ge(fs[1]["xT_ev"], (q + 1) * CC)
                logits_of(L1, range(q * HT, (q + 1) * HT))

            ffn(L0)
            combine(L0, 0)
            combine(L0, 1)
            turn_mixed(0)
            turn_mixed(1)
            ffn(L1)
            for q in range(2):
                combine(L1, q)


def layout(i):
    import numpy as np
    a = {k: np.asarray(v) for k, v in i.items()}
    c = np.ascontiguousarray

    def chunked(w, p=P):
        *lead, r, n = w.shape
        return c(np.moveaxis(w.reshape(*lead, r // p, p, n), -3, -2))

    t = {
        "x": a["x"].reshape(TOK, D),
        "ctxT": chunked(a["ctx_2048"].transpose(0, 2, 1)),
        "mask": a["mask_BxSxS2_ff0"].reshape(NT, P, L),
        "w_qo": np.stack([a["L0_xattn_wq"], a["L0_xattn_wo"]]),
        "w_kv": np.stack([a["L0_xattn_wk"].T, a["L0_xattn_wv"].T, a["L1_xattn_W_in"].T, a["L1_xattn_W_out"].T]),
        "rows": np.stack([a["L0_xattn_bq"], a["L0_xattn_bv"], a["L0_xattn_bo"], a["L1_xattn_b_out"], a["L1_xattn_gamma"],
                          a["L1_xattn_beta"]]),
        "scalars": np.concatenate([a["g_xattn"], a["g_ffn"], a["L1_xattn_decay"].reshape(1), a["L1_ffn_router_bias"]]),
        "colb": np.stack([a["L0_xattn_bk"].reshape(CC, P).T, a["L1_xattn_b_in"].reshape(CC, P).T], axis=1),
        "gate0": chunked(np.concatenate([a["L0_ffn_gate_w"], a["L0_ffn_shared_gate_w"]]).T),
        "gate1": chunked(a["L1_ffn_gate_w"].T),
        "sh_in0": chunked(a["L0_ffn_se_gate_up_w"].T),
        "sh_out0": a["L0_ffn_se_down_w"].T,
        "sh_in1": chunked(np.concatenate([a["L1_ffn_sw1"], a["L1_ffn_sw3"]]).T),
        "sh_out1": a["L1_ffn_sw2"].T,
        "w13_0": chunked(a["L0_ffn_w13"].transpose(0, 2, 1)),
        "w2_0": chunked(a["L0_ffn_w2"].transpose(0, 2, 1), IC),
        "w13_1": chunked(np.concatenate([a["L1_ffn_W1"], a["L1_ffn_W3"]], axis=2)),
        "w2_1": chunked(a["L1_ffn_W2"], IC),
    }
    return {k: c(v) for k, v in t.items()}


def kernel(**inputs):
    import numpy as np
    import concourse.bacc as bacc
    from concourse.bass_utils import run_bass_kernel_spmd

    nc = bacc.Bacc("TRN2", target_bir_lowering=False, num_devices=1)
    arrays = {f"in_{k}": v for k, v in layout(inputs).items()}
    T = {k[3:]: nc.dram_tensor(k, v.shape, mybir.dt.from_np(v.dtype), kind="ExternalInput").ap() for k, v in arrays.items()}
    out = nc.dram_tensor("out", (TOK, D), F32, kind="ExternalOutput").ap()
    build(nc, T, out)
    r = run_bass_kernel_spmd(nc, [arrays], core_ids=[0])
    return np.asarray(r.results[0]["out"]).reshape(B, S, D)
```
